# Optimizing a Trainium2 kernel written in Bass

```python
import numpy as np
import jax
import jax.numpy as jnp

def _softmax(x, axis=-1):
    return jax.nn.softmax(x, axis=axis)

def _gelu(x):
    return jax.nn.gelu(x, approximate=True)

def _silu(x):
    return jax.nn.silu(x)

def _sigmoid(x):
    return jax.nn.sigmoid(x)

def _layernorm(x, axis=-1, eps=1e-05):
    m = jnp.mean(x, axis=axis, keepdims=True)
    v = jnp.var(x, axis=axis, keepdims=True)
    return (x - m) / jnp.sqrt(v + eps)

def _scatter_add(tgt, idx, src, axis=0):
    return tgt.at[idx].add(src)

def _segment_sum(src, seg, n):
    return jax.ops.segment_sum(src, seg, n)
kernel_name = 'mk_conv_seq_d4_conv_nchw192_r2_d48526'

def setup_inputs(seed: int=0):
    np.random.seed(seed)
    _w = jnp.asarray

    def _rec_inputs():
        import jax
        import jax.numpy as jnp
        _gk = jax.random.key(seed)
        x = -0.0004039 + 1 * jax.random.normal(jax.random.fold_in(_gk, 1), (4, 96, 64, 64), jnp.float32)
        return x
    x = _rec_inputs()

    def _L0_conv_setup():
        import jax, jax.numpy as jnp
        import numpy as np
        B, C, H, W = (4, 96, 64, 64)
        K = 4
        DSTATE = 8
        DTRANK = max(8, C // 16)
        EPS = 1e-05

        def _ln(x, w, b):
            mu = jnp.mean(x, axis=-1, keepdims=True)
            var = jnp.var(x, axis=-1, keepdims=True)
            return (x - mu) * jax.lax.rsqrt(var + EPS) * w + b
        key = jax.random.key(seed)
        ks = jax.random.split(key, 16)
        s_in = 1.0 / np.sqrt(C)
        inp = {'x': jax.random.normal(ks[0], (B, C, H, W), jnp.float32), 'norm_w': 1.0 + 0.02 * jax.random.normal(ks[1], (C,), jnp.float32), 'norm_b': 0.02 * jax.random.normal(ks[2], (C,), jnp.float32), 'w_in': s_in * jax.random.normal(ks[3], (2 * C, C), jnp.float32), 'ssm_in_w': s_in * jax.random.normal(ks[4], (2 * C, C), jnp.float32), 'x_proj_w': s_in * jax.random.normal(ks[5], (K, DTRANK + 2 * DSTATE, C), jnp.float32), 'dt_w': 1.0 / np.sqrt(DTRANK) * jax.random.normal(ks[6], (K, C, DTRANK), jnp.float32), 'dt_b': 0.1 * jax.random.normal(ks[7], (K, C), jnp.float32), 'A_logs': jnp.log(jnp.broadcast_to(jnp.arange(1, DSTATE + 1, dtype=jnp.float32), (K * C, DSTATE))), 'Ds': jnp.ones((K * C,), jnp.float32), 'out_norm_w': 1.0 + 0.02 * jax.random.normal(ks[8], (C,), jnp.float32), 'out_norm_b': 0.02 * jax.random.normal(ks[9], (C,), jnp.float32), 'ssm_out_w': s_in * jax.random.normal(ks[10], (C, C), jnp.float32), 'w_out': s_in * jax.random.normal(ks[11], (C, C), jnp.float32)}
        return inp
    _L0_conv_all = _L0_conv_setup()
    _L0_conv_in = {k: v for k, v in _L0_conv_all.items() if k in ('norm_w', 'norm_b', 'w_in', 'ssm_in_w', 'x_proj_w', 'dt_w', 'dt_b', 'A_logs', 'Ds', 'out_norm_w', 'out_norm_b', 'ssm_out_w', 'w_out')}
    del _L0_conv_all

    def _L1_conv_setup():
        import jax, jax.numpy as jnp
        import numpy as np
        B, DIM, H, W = (2, 96, 128, 128)
        WIN = 4
        EPS = 1e-05

        def _cd_conj(x):
            if len(x) == 1:
                return x
            h = len(x) // 2
            return np.concatenate([_cd_conj(x[:h]), -x[h:]])

        def _cd_mult(a, b):
            n = len(a)
            if n == 1:
                return a * b
            h = n // 2
            a1, a2, b1, b2 = (a[:h], a[h:], b[:h], b[h:])
            c1 = _cd_mult(a1, b1) - _cd_mult(_cd_conj(b2), a2)
            c2 = _cd_mult(b2, a1) + _cd_mult(a2, _cd_conj(b1))
            return np.concatenate([c1, c2])

        def _sedenion_table(n=16):
            eye = np.eye(n, dtype=np.float32)
            M = np.zeros((n, n, n), dtype=np.float32)
            for i in range(n):
                for j in range(n):
                    M[i, j] = _cd_mult(eye[i], eye[j])
            return M
        SED_TABLE = jnp.asarray(_sedenion_table(16))

        def layer_norm(x, g, b):
            m = x.mean(-1, keepdims=True)
            v = ((x - m) ** 2).mean(-1, keepdims=True)
            return (x - m) * jax.lax.rsqrt(v + EPS) * g + b

        def get_window(x):
            b, c, h, w = x.shape
            x = x.reshape(b, c, h // WIN, WIN, w // WIN, WIN)
            x = x.transpose(0, 2, 4, 3, 5, 1)
            return x.reshape(b, h // WIN, w // WIN, WIN * WIN * c)

        def reverse_window(x, c):
            b, hh, ww, _ = x.shape
            x = x.reshape(b, hh, ww, WIN, WIN, c)
            x = x.transpose(0, 5, 1, 3, 2, 4)
            return x.reshape(b, c, hh * WIN, ww * WIN)

        def sedenion_full_weight(w_sed):
            d = w_sed.shape[1]
            wf = jnp.einsum('ijk,jde->idke', SED_TABLE, w_sed)
            return wf.reshape(16 * d, 16 * w_sed.shape[2])
        key = jax.random.key(seed)
        ks = jax.random.split(key, 8)
        d, dh = (DIM, 4 * DIM)
        s = 0.02
        return {'x': jax.random.normal(ks[0], (B, DIM, H, W), jnp.float32), 'norm1_g': jnp.ones((d,), jnp.float32), 'norm1_b': jnp.zeros((d,), jnp.float32), 'w_sed': jax.random.normal(ks[1], (16, d, d), jnp.float32) * s, 'proj_w': jax.random.normal(ks[2], (d, d), jnp.float32) * s, 'proj_b': jnp.zeros((d,), jnp.float32), 'norm2_g': jnp.ones((d,), jnp.float32), 'norm2_b': jnp.zeros((d,), jnp.float32), 'fc1_w': jax.random.normal(ks[3], (d, dh), jnp.float32) * s, 'fc1_b': jnp.zeros((dh,), jnp.float32), 'fc2_w': jax.random.normal(ks[4], (dh, d), jnp.float32) * s, 'fc2_b': jnp.zeros((d,), jnp.float32)}
    _L1_conv_all = _L1_conv_setup()
    _L1_conv_in = {k: v for k, v in _L1_conv_all.items() if k in ('norm1_g', 'norm1_b', 'w_sed', 'proj_w', 'proj_b', 'norm2_g', 'norm2_b', 'fc1_w', 'fc1_b', 'fc2_w', 'fc2_b')}
    del _L1_conv_all

    def _L2_conv_setup():
        import jax, jax.numpy as jnp
        import numpy as np
        DIM = 96
        HEADS = 6
        HD = DIM // HEADS
        WIN = 7
        K = WIN * WIN
        B, H, W = (4, 56, 56)
        EPS = 1e-05
        PAD = WIN // 2

        def _conv1x1(x, w, b):
            return jnp.einsum('bchw,oc->bohw', x, w) + b[None, :, None, None]
        key = jax.random.key(seed)
        ks = jax.random.split(key, 8)

        def n(k, shape, scale=0.02):
            return jax.random.normal(k, shape, dtype=jnp.float32) * scale
        return {'x': jax.random.normal(ks[0], (B, DIM, H, W), dtype=jnp.float32), 'bn_gamma': jnp.ones((DIM,), jnp.float32), 'bn_beta': jnp.zeros((DIM,), jnp.float32), 'qkv_w': n(ks[1], (3 * DIM, DIM)), 'qkv_b': jnp.zeros((3 * DIM,), jnp.float32), 'dm_w': n(ks[2], (K, 2 * HD, WIN, WIN)), 'dm_b': jnp.zeros((K,), jnp.float32), 'rel_bias': n(ks[3], (K, HEADS)), 'proj_w': n(ks[4], (DIM, DIM)), 'proj_b': jnp.zeros((DIM,), jnp.float32), 'c1_w': n(ks[5], (4 * DIM, DIM)), 'c1_b': jnp.zeros((4 * DIM,), jnp.float32), 'c2_w': n(ks[6], (DIM, 4 * DIM)), 'c2_b': jnp.zeros((DIM,), jnp.float32)}
    _L2_conv_all = _L2_conv_setup()
    _L2_conv_in = {k: v for k, v in _L2_conv_all.items() if k in ('bn_gamma', 'bn_beta', 'qkv_w', 'qkv_b', 'dm_w', 'dm_b', 'rel_bias', 'proj_w', 'proj_b', 'c1_w', 'c1_b', 'c2_w', 'c2_b')}
    del _L2_conv_all

    def _L3_conv_setup():
        import jax, jax.numpy as jnp
        import numpy as np
        B_SZ, D_IN, H_SZ, W_SZ = (8, 96, 32, 32)
        N_ST, R_DT, K_GRP = (16, 6, 4)
        LN_EPS = 1e-05

        def _ss2d(x, x_proj_weight, dt_projs_weight, dt_projs_bias, A_logs, Ds, ln_g, ln_b):
            B, D, H, W = x.shape
            L = H * W
            K = x_proj_weight.shape[0]
            N = A_logs.shape[1]
            R = dt_projs_weight.shape[2]
            x0 = x.reshape(B, D, L)
            x1 = x.transpose(0, 1, 3, 2).reshape(B, D, L)
            xs = jnp.stack([x0, x1, x0[..., ::-1], x1[..., ::-1]], axis=1)
            x_dbl = jnp.einsum('bkdl,kcd->bkcl', xs, x_proj_weight)
            dts, Bs, Cs = jnp.split(x_dbl, [R, R + N], axis=2)
            dts = jnp.einsum('bkrl,kdr->bkdl', dts, dt_projs_weight)
            A = -jnp.exp(A_logs.astype(jnp.float32)).reshape(K, D, N)
            delta = jax.nn.softplus(dts + dt_projs_bias[None, :, :, None])

            def step(h, inp):
                u_t, d_t, B_t, C_t = inp
                h = jnp.exp(d_t[..., None] * A) * h + (d_t * u_t)[..., None] * B_t[:, :, None, :]
                y = jnp.einsum('bkdn,bkn->bkd', h, C_t)
                return (h, y)
            h0 = jnp.zeros((B, K, D, N), dtype=jnp.float32)
            seq = (xs.transpose(3, 0, 1, 2), delta.transpose(3, 0, 1, 2), Bs.transpose(3, 0, 1, 2), Cs.transpose(3, 0, 1, 2))
            _, ys = jax.lax.scan(step, h0, seq)
            ys = ys.transpose(1, 2, 3, 0) + Ds.reshape(K, D)[None, :, :, None] * xs
            ym = ys[:, 0:2] + ys[:, 2:4][..., ::-1]
            y = ym[:, 0] + ym[:, 1].reshape(B, D, W, H).transpose(0, 1, 3, 2).reshape(B, D, L)
            y = y.reshape(B, D, H, W)
            mean = jnp.mean(y, axis=1, keepdims=True)
            var = jnp.var(y, axis=1, keepdims=True)
            return (y - mean) / jnp.sqrt(var + LN_EPS) * ln_g + ln_b
        key = jax.random.key(seed)
        ks = jax.random.split(key, 6)
        x = jax.random.normal(ks[0], (B_SZ, D_IN, H_SZ, W_SZ), dtype=jnp.float32)
        x_proj_weight = jax.random.normal(ks[1], (K_GRP, R_DT + 2 * N_ST, D_IN), dtype=jnp.float32) * 0.02
        dt_projs_weight = jax.random.normal(ks[2], (K_GRP, D_IN, R_DT), dtype=jnp.float32) * R_DT ** (-0.5)
        dt_projs_bias = jax.random.normal(ks[3], (K_GRP, D_IN), dtype=jnp.float32) * 0.1
        A_logs = jnp.log(jnp.tile(jnp.arange(1, N_ST + 1, dtype=jnp.float32), (K_GRP * D_IN, 1)))
        Ds = jnp.ones((K_GRP * D_IN,), dtype=jnp.float32)
        ln_g = jnp.ones((1, D_IN, 1, 1), dtype=jnp.float32)
        ln_b = jnp.zeros((1, D_IN, 1, 1), dtype=jnp.float32)
        return dict(x=x, x_proj_weight=x_proj_weight, dt_projs_weight=dt_projs_weight, dt_projs_bias=dt_projs_bias, A_logs=A_logs, Ds=Ds, ln_g=ln_g, ln_b=ln_b)
    _L3_conv_all = _L3_conv_setup()
    _L3_conv_in = {k: v for k, v in _L3_conv_all.items() if k in ('x_proj_weight', 'dt_projs_weight', 'dt_projs_bias', 'A_logs', 'Ds', 'ln_g', 'ln_b')}
    del _L3_conv_all
    return {'x': x, 'L0_conv_norm_w': _L0_conv_in['norm_w'], 'L0_conv_norm_b': _L0_conv_in['norm_b'], 'L0_conv_w_in': _L0_conv_in['w_in'], 'L0_conv_ssm_in_w': _L0_conv_in['ssm_in_w'], 'L0_conv_x_proj_w': _L0_conv_in['x_proj_w'], 'L0_conv_dt_w': _L0_conv_in['dt_w'], 'L0_conv_dt_b': _L0_conv_in['dt_b'], 'L0_conv_A_logs': _L0_conv_in['A_logs'], 'L0_conv_Ds': _L0_conv_in['Ds'], 'L0_conv_out_norm_w': _L0_conv_in['out_norm_w'], 'L0_conv_out_norm_b': _L0_conv_in['out_norm_b'], 'L0_conv_ssm_out_w': _L0_conv_in['ssm_out_w'], 'L0_conv_w_out': _L0_conv_in['w_out'], 'L1_conv_norm1_g': _L1_conv_in['norm1_g'], 'L1_conv_norm1_b': _L1_conv_in['norm1_b'], 'L1_conv_w_sed': _L1_conv_in['w_sed'], 'L1_conv_proj_w': _L1_conv_in['proj_w'], 'L1_conv_proj_b': _L1_conv_in['proj_b'], 'L1_conv_norm2_g': _L1_conv_in['norm2_g'], 'L1_conv_norm2_b': _L1_conv_in['norm2_b'], 'L1_conv_fc1_w': _L1_conv_in['fc1_w'], 'L1_conv_fc1_b': _L1_conv_in['fc1_b'], 'L1_conv_fc2_w': _L1_conv_in['fc2_w'], 'L1_conv_fc2_b': _L1_conv_in['fc2_b'], 'L2_conv_bn_gamma': _L2_conv_in['bn_gamma'], 'L2_conv_bn_beta': _L2_conv_in['bn_beta'], 'L2_conv_qkv_w': _L2_conv_in['qkv_w'], 'L2_conv_qkv_b': _L2_conv_in['qkv_b'], 'L2_conv_dm_w': _L2_conv_in['dm_w'], 'L2_conv_dm_b': _L2_conv_in['dm_b'], 'L2_conv_rel_bias': _L2_conv_in['rel_bias'], 'L2_conv_proj_w': _L2_conv_in['proj_w'], 'L2_conv_proj_b': _L2_conv_in['proj_b'], 'L2_conv_c1_w': _L2_conv_in['c1_w'], 'L2_conv_c1_b': _L2_conv_in['c1_b'], 'L2_conv_c2_w': _L2_conv_in['c2_w'], 'L2_conv_c2_b': _L2_conv_in['c2_b'], 'L3_conv_x_proj_weight': _L3_conv_in['x_proj_weight'], 'L3_conv_dt_projs_weight': _L3_conv_in['dt_projs_weight'], 'L3_conv_dt_projs_bias': _L3_conv_in['dt_projs_bias'], 'L3_conv_A_logs': _L3_conv_in['A_logs'], 'L3_conv_Ds': _L3_conv_in['Ds'], 'L3_conv_ln_g': _L3_conv_in['ln_g'], 'L3_conv_ln_b': _L3_conv_in['ln_b']}

def reference(x, L0_conv_norm_w, L0_conv_norm_b, L0_conv_w_in, L0_conv_ssm_in_w, L0_conv_x_proj_w, L0_conv_dt_w, L0_conv_dt_b, L0_conv_A_logs, L0_conv_Ds, L0_conv_out_norm_w, L0_conv_out_norm_b, L0_conv_ssm_out_w, L0_conv_w_out, L1_conv_norm1_g, L1_conv_norm1_b, L1_conv_w_sed, L1_conv_proj_w, L1_conv_proj_b, L1_conv_norm2_g, L1_conv_norm2_b, L1_conv_fc1_w, L1_conv_fc1_b, L1_conv_fc2_w, L1_conv_fc2_b, L2_conv_bn_gamma, L2_conv_bn_beta, L2_conv_qkv_w, L2_conv_qkv_b, L2_conv_dm_w, L2_conv_dm_b, L2_conv_rel_bias, L2_conv_proj_w, L2_conv_proj_b, L2_conv_c1_w, L2_conv_c1_b, L2_conv_c2_w, L2_conv_c2_b, L3_conv_x_proj_weight, L3_conv_dt_projs_weight, L3_conv_dt_projs_bias, L3_conv_A_logs, L3_conv_Ds, L3_conv_ln_g, L3_conv_ln_b):
    import jax
    import jax.numpy as jnp

    def _L0_conv_ref(x, norm_w, norm_b, w_in, ssm_in_w, x_proj_w, dt_w, dt_b, A_logs, Ds, out_norm_w, out_norm_b, ssm_out_w, w_out):
        import jax, jax.numpy as jnp
        import numpy as np
        B, C, H, W = (4, 96, 64, 64)
        K = 4
        DSTATE = 8
        DTRANK = max(8, C // 16)
        EPS = 1e-05

        def _ln(x, w, b):
            mu = jnp.mean(x, axis=-1, keepdims=True)
            var = jnp.var(x, axis=-1, keepdims=True)
            return (x - mu) * jax.lax.rsqrt(var + EPS) * w + b
        xh = jnp.transpose(x, (0, 2, 3, 1))
        xn = _ln(xh, norm_w, norm_b)
        p = xn @ w_in.T
        x1, x2 = (p[..., :C], p[..., C:])
        u = x1 @ ssm_in_w.T
        xss, z = (u[..., :C], u[..., C:])
        z = jax.nn.silu(z)
        xss = jax.nn.silu(xss)
        xd = jnp.einsum('bhwd,kcd->bhwkc', xss, x_proj_w)
        dtr = xd[..., :DTRANK]
        Bv = xd[..., DTRANK:DTRANK + DSTATE]
        Cv = xd[..., DTRANK + DSTATE:]
        dt = jax.nn.softplus(jnp.einsum('bhwkr,kdr->bhwkd', dtr, dt_w) + dt_b)
        bc = jnp.sum(Bv * Cv, axis=-1)
        gain = jnp.sum(bc[..., None] * dt + Ds.reshape(K, C), axis=-2)
        y = xss * gain
        y = _ln(y, out_norm_w, out_norm_b)
        y = y * z
        s = y @ ssm_out_w.T
        o = s * jax.nn.silu(x2) @ w_out.T
        return x + jnp.transpose(o, (0, 3, 1, 2))

    def _L1_conv_ref(x, norm1_g, norm1_b, w_sed, proj_w, proj_b, norm2_g, norm2_b, fc1_w, fc1_b, fc2_w, fc2_b):
        import jax, jax.numpy as jnp
        import numpy as np
        B, DIM, H, W = (2, 96, 128, 128)
        WIN = 4
        EPS = 1e-05

        def _cd_conj(x):
            if len(x) == 1:
                return x
            h = len(x) // 2
            return np.concatenate([_cd_conj(x[:h]), -x[h:]])

        def _cd_mult(a, b):
            n = len(a)
            if n == 1:
                return a * b
            h = n // 2
            a1, a2, b1, b2 = (a[:h], a[h:], b[:h], b[h:])
            c1 = _cd_mult(a1, b1) - _cd_mult(_cd_conj(b2), a2)
            c2 = _cd_mult(b2, a1) + _cd_mult(a2, _cd_conj(b1))
            return np.concatenate([c1, c2])

        def _sedenion_table(n=16):
            eye = np.eye(n, dtype=np.float32)
            M = np.zeros((n, n, n), dtype=np.float32)
            for i in range(n):
                for j in range(n):
                    M[i, j] = _cd_mult(eye[i], eye[j])
            return M
        SED_TABLE = jnp.asarray(_sedenion_table(16))

        def layer_norm(x, g, b):
            m = x.mean(-1, keepdims=True)
            v = ((x - m) ** 2).mean(-1, keepdims=True)
            return (x - m) * jax.lax.rsqrt(v + EPS) * g + b

        def get_window(x):
            b, c, h, w = x.shape
            x = x.reshape(b, c, h // WIN, WIN, w // WIN, WIN)
            x = x.transpose(0, 2, 4, 3, 5, 1)
            return x.reshape(b, h // WIN, w // WIN, WIN * WIN * c)

        def reverse_window(x, c):
            b, hh, ww, _ = x.shape
            x = x.reshape(b, hh, ww, WIN, WIN, c)
            x = x.transpose(0, 5, 1, 3, 2, 4)
            return x.reshape(b, c, hh * WIN, ww * WIN)

        def sedenion_full_weight(w_sed):
            d = w_sed.shape[1]
            wf = jnp.einsum('ijk,jde->idke', SED_TABLE, w_sed)
            return wf.reshape(16 * d, 16 * w_sed.shape[2])
        b, c, h, w = x.shape
        xn = layer_norm(x.transpose(0, 2, 3, 1), norm1_g, norm1_b).transpose(0, 3, 1, 2)
        xw = get_window(xn)
        wf = sedenion_full_weight(w_sed)
        xw = xw @ wf
        x1 = reverse_window(xw, c)
        y = x1.transpose(0, 2, 3, 1)
        y = jax.nn.gelu(y, approximate=False)
        y = y @ proj_w + proj_b
        x = x + y.transpose(0, 3, 1, 2)
        hbr = layer_norm(x.transpose(0, 2, 3, 1), norm2_g, norm2_b)
        hbr = jax.nn.gelu(hbr @ fc1_w + fc1_b, approximate=False)
        hbr = hbr @ fc2_w + fc2_b
        x = x + hbr.transpose(0, 3, 1, 2)
        return x

    def _L2_conv_ref(x, bn_gamma, bn_beta, qkv_w, qkv_b, dm_w, dm_b, rel_bias, proj_w, proj_b, c1_w, c1_b, c2_w, c2_b):
        import jax, jax.numpy as jnp
        import numpy as np
        DIM = 96
        HEADS = 6
        HD = DIM // HEADS
        WIN = 7
        K = WIN * WIN
        B, H, W = (4, 56, 56)
        EPS = 1e-05
        PAD = WIN // 2

        def _conv1x1(x, w, b):
            return jnp.einsum('bchw,oc->bohw', x, w) + b[None, :, None, None]
        Bx, C, Hx, Wx = x.shape
        shortcut = x
        mean = jnp.mean(x, axis=(0, 2, 3), keepdims=True)
        var = jnp.var(x, axis=(0, 2, 3), keepdims=True)
        xn = (x - mean) * jax.lax.rsqrt(var + EPS)
        xn = xn * bn_gamma[None, :, None, None] + bn_beta[None, :, None, None]
        qkv = _conv1x1(xn, qkv_w, qkv_b).reshape(Bx, 3, HEADS, HD, Hx, Wx)
        q, k, v = (qkv[:, 0], qkv[:, 1], qkv[:, 2])
        scale = HD ** (-0.5)
        qk = jnp.concatenate([(q * scale).reshape(Bx * HEADS, HD, Hx, Wx), k.reshape(Bx * HEADS, HD, Hx, Wx)], axis=1)
        attn = jax.lax.conv_general_dilated(qk, dm_w, (1, 1), [(PAD, PAD), (PAD, PAD)], dimension_numbers=('NCHW', 'OIHW', 'NCHW')) + dm_b[None, :, None, None]
        attn = attn.reshape(Bx, HEADS, K, Hx, Wx)
        attn = attn + rel_bias.T[None, :, :, None, None]
        attn = jax.nn.softmax(attn, axis=2)
        patches = jax.lax.conv_general_dilated_patches(v.reshape(Bx * HEADS, HD, Hx, Wx), (WIN, WIN), (1, 1), [(PAD, PAD), (PAD, PAD)], dimension_numbers=('NCHW', 'OIHW', 'NCHW'))
        patches = patches.reshape(Bx, HEADS, HD, K, Hx, Wx)
        out = jnp.einsum('bnckhw,bnkhw->bnchw', patches, attn).reshape(Bx, C, Hx, Wx)
        out = _conv1x1(out, proj_w, proj_b)
        x1 = shortcut + out
        h = _conv1x1(x1, c1_w, c1_b)
        h = jax.nn.gelu(h, approximate=False)
        h = _conv1x1(h, c2_w, c2_b)
        return x1 + h

    def _L3_conv_ref(x, x_proj_weight, dt_projs_weight, dt_projs_bias, A_logs, Ds, ln_g, ln_b):
        import jax, jax.numpy as jnp
        import numpy as np
        B_SZ, D_IN, H_SZ, W_SZ = (8, 96, 32, 32)
        N_ST, R_DT, K_GRP = (16, 6, 4)
        LN_EPS = 1e-05

        def _ss2d(x, x_proj_weight, dt_projs_weight, dt_projs_bias, A_logs, Ds, ln_g, ln_b):
            B, D, H, W = x.shape
            L = H * W
            K = x_proj_weight.shape[0]
            N = A_logs.shape[1]
            R = dt_projs_weight.shape[2]
            x0 = x.reshape(B, D, L)
            x1 = x.transpose(0, 1, 3, 2).reshape(B, D, L)
            xs = jnp.stack([x0, x1, x0[..., ::-1], x1[..., ::-1]], axis=1)
            x_dbl = jnp.einsum('bkdl,kcd->bkcl', xs, x_proj_weight)
            dts, Bs, Cs = jnp.split(x_dbl, [R, R + N], axis=2)
            dts = jnp.einsum('bkrl,kdr->bkdl', dts, dt_projs_weight)
            A = -jnp.exp(A_logs.astype(jnp.float32)).reshape(K, D, N)
            delta = jax.nn.softplus(dts + dt_projs_bias[None, :, :, None])

            def step(h, inp):
                u_t, d_t, B_t, C_t = inp
                h = jnp.exp(d_t[..., None] * A) * h + (d_t * u_t)[..., None] * B_t[:, :, None, :]
                y = jnp.einsum('bkdn,bkn->bkd', h, C_t)
                return (h, y)
            h0 = jnp.zeros((B, K, D, N), dtype=jnp.float32)
            seq = (xs.transpose(3, 0, 1, 2), delta.transpose(3, 0, 1, 2), Bs.transpose(3, 0, 1, 2), Cs.transpose(3, 0, 1, 2))
            _, ys = jax.lax.scan(step, h0, seq)
            ys = ys.transpose(1, 2, 3, 0) + Ds.reshape(K, D)[None, :, :, None] * xs
            ym = ys[:, 0:2] + ys[:, 2:4][..., ::-1]
            y = ym[:, 0] + ym[:, 1].reshape(B, D, W, H).transpose(0, 1, 3, 2).reshape(B, D, L)
            y = y.reshape(B, D, H, W)
            mean = jnp.mean(y, axis=1, keepdims=True)
            var = jnp.var(y, axis=1, keepdims=True)
            return (y - mean) / jnp.sqrt(var + LN_EPS) * ln_g + ln_b
        return _ss2d(x, x_proj_weight, dt_projs_weight, dt_projs_bias, A_logs, Ds, ln_g, ln_b)

    def _gn(v, G=32, eps=1e-05):
        B_, C_, H_, W_ = v.shape
        g = v.reshape(B_, G, C_ // G, H_, W_)
        m = jnp.mean(g, axis=(2, 3, 4), keepdims=True)
        s = jnp.var(g, axis=(2, 3, 4), keepdims=True)
        return ((g - m) / jnp.sqrt(s + eps)).reshape(v.shape)

    def _ln_c(v, eps=1e-06):
        m = jnp.mean(v, axis=1, keepdims=True)
        s = jnp.var(v, axis=1, keepdims=True)
        return (v - m) / jnp.sqrt(s + eps)

    def _ln_t(v, eps=1e-05):
        m = jnp.mean(v, axis=-1, keepdims=True)
        s = jnp.var(v, axis=-1, keepdims=True)
        return (v - m) / jnp.sqrt(s + eps)

    def _to_tokens(v):
        B_, C_, H_, W_ = v.shape
        return v.reshape(B_, C_, H_ * W_).transpose(0, 2, 1)

    def _from_tokens(t, like):
        B_, C_, H_, W_ = like.shape
        return t.transpose(0, 2, 1).reshape(B_, C_, H_, W_)
    x = _L0_conv_ref(x, L0_conv_norm_w, L0_conv_norm_b, L0_conv_w_in, L0_conv_ssm_in_w, L0_conv_x_proj_w, L0_conv_dt_w, L0_conv_dt_b, L0_conv_A_logs, L0_conv_Ds, L0_conv_out_norm_w, L0_conv_out_norm_b, L0_conv_ssm_out_w, L0_conv_w_out)
    x = _L1_conv_ref(x, L1_conv_norm1_g, L1_conv_norm1_b, L1_conv_w_sed, L1_conv_proj_w, L1_conv_proj_b, L1_conv_norm2_g, L1_conv_norm2_b, L1_conv_fc1_w, L1_conv_fc1_b, L1_conv_fc2_w, L1_conv_fc2_b)
    x = _L2_conv_ref(x, L2_conv_bn_gamma, L2_conv_bn_beta, L2_conv_qkv_w, L2_conv_qkv_b, L2_conv_dm_w, L2_conv_dm_b, L2_conv_rel_bias, L2_conv_proj_w, L2_conv_proj_b, L2_conv_c1_w, L2_conv_c1_b, L2_conv_c2_w, L2_conv_c2_b)
    x = _L3_conv_ref(x, L3_conv_x_proj_weight, L3_conv_dt_projs_weight, L3_conv_dt_projs_bias, L3_conv_A_logs, L3_conv_Ds, L3_conv_ln_g, L3_conv_ln_b)
    return x

_drawn_inputs = setup_inputs


def setup_inputs(seed=0):
    import zlib

    import numpy as np

    out = dict(_drawn_inputs(seed))
    spreads = {'L0_conv_Ds': (1.0, 0.2),
     'L1_conv_norm1_g': (1.0, 0.6),
     'L1_conv_norm1_b': (0.0, 2.0),
     'L1_conv_proj_b': (0.0, 0.426),
     'L1_conv_norm2_g': (1.0, 0.6),
     'L1_conv_norm2_b': (0.0, 2.0),
     'L1_conv_fc1_b': (0.0, 1.603),
     'L1_conv_fc2_b': (0.0, 0.431),
     'L2_conv_bn_gamma': (1.0, 0.6),
     'L2_conv_bn_beta': (0.0, 0.8),
     'L2_conv_qkv_b': (0.0, 0.414),
     'L2_conv_dm_b': (0.0, 0.8),
     'L2_conv_proj_b': (0.0, 0.495),
     'L2_conv_c1_b': (0.0, 1.259),
     'L2_conv_c2_b': (0.0, 0.371),
     'L3_conv_Ds': (1.0, 0.6),
     'L3_conv_ln_g': (1.0, 0.2),
     'L3_conv_ln_b': (0.0, 0.1)}
    factors = {'L0_conv_norm_w': 4.318,
     'L0_conv_norm_b': 3.988,
     'L0_conv_dt_b': 5.657,
     'L0_conv_out_norm_w': 7.93,
     'L0_conv_out_norm_b': 8.0,
     'L2_conv_qkv_w': 8.0,
     'L2_conv_dm_w': 8.0,
     'L2_conv_rel_bias': 47.3,
     'L2_conv_proj_w': 2.74,
     'L3_conv_x_proj_weight': 3.371,
     'L3_conv_dt_projs_weight': 5.491,
     'L3_conv_dt_projs_bias': 8.0,
     'L3_conv_A_logs': 6.8,
     'L1_conv_fc1_w': 3.248}
    for name, (base, spread) in spreads.items():
        noise = np.random.default_rng([zlib.crc32(name.encode()), seed]).standard_normal(out[name].shape)
        drawn = base * np.exp(spread * noise) if base else spread * noise
        out[name] = jnp.asarray(drawn.astype(out[name].dtype))
    for name, factor in factors.items():
        out[name] = (out[name] * factor).astype(out[name].dtype)
    return out
```

```python
from contextlib import ExitStack

import numpy as np

import concourse.bass as bass
from concourse import mybir

ALU = mybir.AluOpType
ACT = mybir.ActivationFunctionType
AX_X = mybir.AxisListType.X
F32 = mybir.dt.float32
BF16 = mybir.dt.bfloat16
LN_EXP = "natural_log_exp_and_others"

B, C, H, W = 4, 96, 64, 64
HW = H * W
T = B * HW
N = 512
TILES = T // N
EPS = 1e-5
VAR_SCALE = 2.0 ** -12
WIDE_VAR_SCALE = 2.0 ** -46


def gated_ssm_block(nc, x, w, X):
    K, S, R = 4, 8, 8
    with ExitStack() as ctx:
        sb = lambda name, shape, dt=F32: ctx.enter_context(nc.sbuf_tensor(name, shape, dt))
        ps = lambda name, shape: ctx.enter_context(nc.psum_tensor(name, shape, F32))
        sem = lambda name: ctx.enter_context(nc.semaphore(name))

        center = sb("l0_center", [C, C])
        mean_w = sb("l0_mean_w", [C, C])
        w_in1 = sb("l0_w_in1", [C, C])
        ssm_in = sb("l0_ssm_in", [C, 2 * C])
        w_u = sb("l0_w_u", [C, 2 * C])
        w_g = sb("l0_w_g", [C, C])
        w_bc = sb("l0_w_bc", [C, 2, K * S])
        xp_dt = sb("l0_xp_dt", [R, K, C])
        dt_w = sb("l0_dt_w", [R, K, C])
        w_dt = sb("l0_w_dt", [C, K, C])
        pick = sb("l0_pick", [K * S, K, C])
        w_so = sb("l0_w_so", [C, C])
        w_o = sb("l0_w_o", [C, C])
        cols = sb("l0_cols", [C, 12])
        d_sum = sb("l0_d_sum", [C, 1])
        eps = sb("l0_eps", [C, 2])

        xsq = sb("l0_xsq", [C, N])
        rstd = sb("l0_rstd", [C, N])
        xn = sb("l0_xn", [C, N])
        xss = sb("l0_xss", [C, 2, N])
        z = sb("l0_z", [C, 2, N])
        sg = sb("l0_sg", [C, 2, N])
        bs = sb("l0_bs", [K * S, N])
        bcp = sb("l0_bcp", [K * S, N])
        dx = sb("l0_dx", [C, K, N])
        sp = sb("l0_sp", [C, K, N])
        dt = sb("l0_dt", [C, K, N])
        gain = sb("l0_gain", [C, K, N])
        y = sb("l0_y", [C, N])
        ysq = sb("l0_ysq", [C, N])
        yrstd = sb("l0_yrstd", [C, N])
        yn = sb("l0_yn", [C, N])
        sgated = sb("l0_sgated", [C, N])

        p_xc, p_var, p_u = ps("l0_p0", [C, N]), ps("l0_p1", [C, N]), ps("l0_p2", [C, N])
        p_z, p_g = p_xc, p_var
        p_b, p_c = ps("l0_p3", [C, N]), ps("l0_p4", [C, N])
        p_dt = [ps("l0_p5", [C, N]), ps("l0_p6", [C, N])]
        p_bc = [ps("l0_p7", [C, N]), p_b]
        p_yc, p_yvar, p_s, p_o = p_c, p_dt[0], p_dt[1], p_bc[0]

        s_w, s_x = sem("l0_weights"), sem("l0_x_loaded")
        s_setup, s_setup_cp, s_const = sem("l0_setup_mm"), sem("l0_setup_copied"), sem("l0_constants")
        s_xc, s_xsq, s_var, s_lnv, s_rstd, s_xn0, s_xn = (sem("l0_" + n) for n in (
            "xc", "xsq", "var", "lnvar", "rstd", "xn_plain", "xn"))
        s_zg, s_silu = sem("l0_projections"), sem("l0_silu")
        s_bcm, s_bs, s_bcp, s_dtm, s_dx, s_abs, s_exp, s_sp, s_dt, s_bc, s_gain = (sem("l0_" + n) for n in (
            "b_and_c", "b_copied", "bc_product", "dt_mm", "dx", "dt_abs", "dt_exp", "softplus_log", "dt",
            "bc_mm", "gain"))
        s_dsum = sem("l0_gain_sums")
        s_y, s_yc, s_ysq, s_yvar, s_ylnv, s_yrstd, s_yn, s_s, s_sgated, s_o, s_out = (sem("l0_" + n) for n in (
            "y", "yc", "ysq", "yvar", "ylnvar", "yrstd", "yn", "s", "s_gated", "o", "x_written"))
        block = ctx.enter_context(nc.Block())

        weights = [(center[:], w["center"]), (mean_w[:], w["mean_w"]), (w_in1[:], w["w_in1"]),
                   (ssm_in[:], w["ssm_in_T"]), (w_g[:], w["w_g_T"]), (w_bc[:], w["w_bc_T"]),
                   (xp_dt[:], w["xp_dt"]), (dt_w[:], w["dt_w_T"]), (pick[:], w["pick"]),
                   (w_so[:], w["ssm_out_T"]), (w_o[:], w["w_out_T"]), (cols[:], w["cols"])]

        @block.sync
        def _(sp_):
            for dst, src in weights:
                sp_.dma_start(dst, src).then_inc(s_w, 16)
            for b in range(B):
                sp_.dma_start(X[:, b * HW:(b + 1) * HW], x[b]).then_inc(s_x, 16)

        @block.tensor
        def _(pe):
            pe.wait_ge(s_w, 16 * len(weights))
            pe.matmul(p_xc[:, 0:2 * C], w_in1[:], ssm_in[:], start=True, stop=True).then_inc(s_setup, 1)
            for k in range(K):
                pe.matmul(p_var[:, k * C:(k + 1) * C], xp_dt[:, k, :], dt_w[:, k, :],
                          start=True, stop=True).then_inc(s_setup, 1)
            pe.wait_ge(s_setup_cp, 2)

            def ln_a(t):
                if not (isinstance(t, int) and t == 0):
                    pe.wait_ge(s_silu, 3 * t)
                pe.nop(nofuse=True)
                pe.matmul(p_xc[:], center[:], X[:, bass.ds(t * N, N)], start=True, stop=True).then_inc(s_xc, 1)

            def var_a(t):
                pe.wait_ge(s_xsq, t + 1)
                pe.matmul(p_var[:], mean_w[:], xsq[:], start=True, stop=True).then_inc(s_var, 1)

            def proj_a(t):
                pe.wait_ge(s_xn, t + 1)
                pe.matmul(p_u[:], w_u[:, 0:C], xn[:], start=True, stop=True)
                pe.matmul(p_z[:], w_u[:, C:2 * C], xn[:], start=True, stop=True)
                pe.matmul(p_g[:], w_g[:], xn[:], start=True, stop=True).then_inc(s_zg, 1)

            def bc_b(t, par):
                pe.wait_ge(s_silu, 3 * t + 1)
                pe.matmul(p_b[0:K * S, :], w_bc[:, 0, :], xss[:, par, :], start=True, stop=True)
                pe.matmul(p_c[0:K * S, :], w_bc[:, 1, :], xss[:, par, :], start=True, stop=True).then_inc(s_bcm, 1)

            def dt_b(t, par):
                for k in range(K):
                    if k >= 2:
                        pe.wait_ge(s_dx, K * t + k - 1)
                    pe.matmul(p_dt[k % 2][:], w_dt[:, k, :], xss[:, par, :], start=True, stop=True).then_inc(s_dtm, 1)

            def gains_b(t):
                pe.wait_ge(s_bcp, t + 1)
                for k in range(K):
                    if k >= 2:
                        pe.wait_ge(s_gain, K * t + k - 1)
                    pe.matmul(p_bc[k % 2][:], pick[:, k, :], bcp[:], start=True, stop=True).then_inc(s_bc, 1)

            def ln_b(t):
                pe.wait_ge(s_y, t + 1)
                pe.matmul(p_yc[:], center[:], y[:], start=True, stop=True).then_inc(s_yc, 1)
                pe.wait_ge(s_ysq, t + 1)
                pe.matmul(p_yvar[:], mean_w[:], ysq[:], start=True, stop=True).then_inc(s_yvar, 1)

            def out_b(t):
                pe.wait_ge(s_yn, 3 * t + 3)
                pe.matmul(p_s[:], w_so[:], yn[:], start=True, stop=True).then_inc(s_s, 1)
                pe.wait_ge(s_sgated, t + 1)
                pe.matmul(p_o[:], w_o[:], sgated[:], start=True, stop=True).then_inc(s_o, 1)

            def step(t, par):
                bc_b(t, par)
                dt_b(t, par)
                ln_a(t + 1)
                var_a(t + 1)
                gains_b(t)
                ln_b(t)
                proj_a(t + 1)
                out_b(t)

            pe.wait_ge(s_x, 16 * B)
            ln_a(0)
            var_a(0)
            proj_a(0)
            with pe.Fori(0, TILES // 2 - 1) as i:
                step(2 * i, 0)
                step(2 * i + 1, 1)
            step(TILES - 2, 0)
            bc_b(TILES - 1, 1)
            dt_b(TILES - 1, 1)
            gains_b(TILES - 1)
            ln_b(TILES - 1)
            out_b(TILES - 1)

        @block.scalar
        def _(act):
            act.wait_ge(s_const, 1)

            def lnexp_table():
                act.preload_act_table_set(LN_EXP)

            def square_a(t):
                act.wait_ge(s_xc, t + 1)
                act.activation(xsq[:], p_xc[:], ACT.Square).then_inc(s_xsq, 1)

            def rstd_a(t):
                act.wait_ge(s_var, t + 1)
                act.activation(rstd[:], p_var[:], ACT.Ln, bias=eps[:, 0:1], scale=VAR_SCALE).then_inc(s_lnv, 1)
                act.wait_ge(s_lnv, t + 1)
                act.activation(rstd[:], rstd[:], ACT.Exp, bias=eps[:, 1:2], scale=-0.5).then_inc(s_rstd, 1)

            def silu_a(t, par):
                act.wait_ge(s_zg, t + 1)
                act.activation(xss[:, par, :], p_u[:], ACT.Silu).then_inc(s_silu, 1)
                act.activation(z[:, par, :], p_z[:], ACT.Silu).then_inc(s_silu, 1)
                act.activation(sg[:, par, :], p_g[:], ACT.Silu).then_inc(s_silu, 1)

            def b_copy_b(t):
                act.wait_ge(s_bcm, t + 1)
                act.activation(bs[:], p_b[0:K * S, :], ACT.Copy).then_inc(s_bs, 1)

            def softplus_b(t):
                act.wait_ge(s_dx, K * t + K)
                act.activation(sp[:], dx[:], ACT.Abs).then_inc(s_abs, 1)
                act.wait_ge(s_abs, t + 1)
                act.activation(sp[:], sp[:], ACT.Exp, scale=-1.0).then_inc(s_exp, 1)
                act.wait_ge(s_exp, t + 1)
                act.activation(sp[:], sp[:], ACT.Ln, bias=1.0).then_inc(s_sp, 1)

            def rstd_b(t):
                act.wait_ge(s_yc, t + 1)
                act.activation(ysq[:], p_yc[:], ACT.Square).then_inc(s_ysq, 1)
                act.wait_ge(s_yvar, t + 1)
                act.activation(yrstd[:], p_yvar[:], ACT.Ln, bias=eps[:, 0:1], scale=VAR_SCALE).then_inc(s_ylnv, 1)
                act.wait_ge(s_ylnv, t + 1)
                act.activation(yrstd[:], yrstd[:], ACT.Exp, bias=eps[:, 1:2], scale=-0.5).then_inc(s_yrstd, 1)

            def step(t, par):
                lnexp_table()
                b_copy_b(t)
                square_a(t + 1)
                softplus_b(t)
                rstd_a(t + 1)
                rstd_b(t)
                silu_a(t + 1, 1 - par)

            lnexp_table()
            square_a(0)
            rstd_a(0)
            silu_a(0, 0)
            with act.Fori(0, TILES // 2 - 1) as i:
                step(2 * i, 0)
                step(2 * i + 1, 1)
            step(TILES - 2, 0)
            lnexp_table()
            b_copy_b(TILES - 1)
            softplus_b(TILES - 1)
            rstd_b(TILES - 1)

        @block.vector
        def _(dve):
            dve.memset(eps[:, 1:2], 0.5 * float(np.log(VAR_SCALE)))
            dve.memset(eps[:, 0:1], EPS * VAR_SCALE).then_inc(s_const, 1)
            dve.wait_ge(s_setup, 1)
            dve.tensor_copy(w_u[:], p_xc[:, 0:2 * C]).then_inc(s_setup_cp, 1)
            dve.wait_ge(s_setup, 1 + K)
            dve.tensor_copy(w_dt[:].rearrange("p k c -> p (k c)"), p_var[:, 0:K * C]).then_inc(s_setup_cp, 1)
            dve.wait_ge(s_w, 16 * len(weights))
            dve.tensor_reduce(d_sum[:], cols[:, 8:12], AX_X, ALU.add).then_inc(s_setup_cp, 1)
            dve.wait_ge(s_setup_cp, 3)

            def xn_a(t):
                dve.wait_ge(s_rstd, t + 1)
                if not (isinstance(t, int) and t == 0):
                    dve.wait_ge(s_zg, t)
                dve.tensor_tensor(xn[:], p_xc[:], rstd[:], ALU.mult).then_inc(s_xn0, 1)
                dve.wait_ge(s_xn0, t + 1)
                dve.tensor_scalar(xn[:], xn[:], cols[:, 0:1], cols[:, 1:2], ALU.mult, ALU.add).then_inc(s_xn, 1)

            def bc_product_b(t):
                dve.wait_ge(s_bs, t + 1)
                dve.tensor_tensor(bcp[:], bs[:], p_c[0:K * S, :], ALU.mult).then_inc(s_bcp, 1)

            def dx_b(t):
                for k in range(K):
                    dve.wait_ge(s_dtm, K * t + k + 1)
                    dve.tensor_scalar(dx[:, k, :], p_dt[k % 2][:], cols[:, 4 + k:5 + k], None, ALU.add).then_inc(s_dx, 1)

            def gain_b(t, par):
                dve.wait_ge(s_sp, t + 1)
                dve.scalar_tensor_tensor(dt[:], dx[:], 0.0, sp[:], ALU.max, ALU.add).then_inc(s_dt, 1)
                dve.wait_ge(s_dt, t + 1)
                for k in range(K):
                    dve.wait_ge(s_bc, K * t + k + 1)
                    dve.tensor_tensor(gain[:, k, :], dt[:, k, :], p_bc[k % 2][:], ALU.mult).then_inc(s_gain, 1)
                dve.wait_ge(s_gain, K * t + 4)
                dve.tensor_tensor(dt[:, 0:2, :], gain[:, 0:2, :], gain[:, 2:4, :], ALU.add).then_inc(s_dsum, 1)
                dve.wait_ge(s_dsum, 2 * t + 1)
                dve.tensor_tensor(gain[:, 0, :], dt[:, 0, :], dt[:, 1, :], ALU.add).then_inc(s_dsum, 1)
                dve.wait_ge(s_dsum, 2 * t + 2)
                dve.scalar_tensor_tensor(y[:], gain[:, 0, :], d_sum[:], xss[:, par, :], ALU.add, ALU.mult).then_inc(s_y, 1)

            def gate_b(t, par):
                dve.wait_ge(s_yrstd, t + 1)
                dve.tensor_tensor(yn[:], p_yc[:], yrstd[:], ALU.mult).then_inc(s_yn, 1)
                dve.wait_ge(s_yn, 3 * t + 1)
                dve.tensor_scalar(yn[:], yn[:], cols[:, 2:3], cols[:, 3:4], ALU.mult, ALU.add).then_inc(s_yn, 1)
                dve.wait_ge(s_yn, 3 * t + 2)
                dve.tensor_tensor(yn[:], yn[:], z[:, par, :], ALU.mult).then_inc(s_yn, 1)

            def out_b(t, par):
                dve.wait_ge(s_s, t + 1)
                dve.tensor_tensor(sgated[:], p_s[:], sg[:, par, :], ALU.mult).then_inc(s_sgated, 1)
                dve.wait_ge(s_o, t + 1)
                dve.tensor_tensor(X[:, bass.ds(t * N, N)], p_o[:], X[:, bass.ds(t * N, N)], ALU.add).then_inc(s_out, 1)

            def step(t, par):
                dx_b(t)
                bc_product_b(t)
                xn_a(t + 1)
                gain_b(t, par)
                gate_b(t, par)
                out_b(t, par)

            xn_a(0)
            with dve.Fori(0, TILES // 2 - 1) as i:
                step(2 * i, 0)
                step(2 * i + 1, 1)
            step(TILES - 2, 0)
            dx_b(TILES - 1)
            bc_product_b(TILES - 1)
            gain_b(TILES - 1, 1)
            gate_b(TILES - 1, 1)
            out_b(TILES - 1, 1)


def gated_ssm_layout(w):
    K, S, R = 4, 8, 8
    xp = w["L0_conv_x_proj_w"]
    per_direction = lambda a: np.reshape(a, (K, C)).T
    return {
        "center": np.eye(C, dtype=np.float32) - np.float32(1 / C),
        "mean_w": np.full((C, C), 1 / C, np.float32),
        "w_in1": w["L0_conv_w_in"][:C],
        "ssm_in_T": w["L0_conv_ssm_in_w"].T,
        "w_g_T": w["L0_conv_w_in"][C:].T,
        "w_bc_T": np.stack([xp[:, R + j * S:R + (j + 1) * S].reshape(K * S, C).T for j in range(2)], 1),
        "xp_dt": xp[:, :R].transpose(1, 0, 2),
        "dt_w_T": w["L0_conv_dt_w"].transpose(2, 0, 1),
        "pick": np.repeat(np.repeat(np.eye(K, dtype=np.float32), S, 0)[:, :, None], C, 2),
        "ssm_out_T": w["L0_conv_ssm_out_w"].T,
        "w_out_T": w["L0_conv_w_out"].T,
        "cols": np.concatenate([w["L0_conv_norm_w"][:, None], w["L0_conv_norm_b"][:, None],
                                w["L0_conv_out_norm_w"][:, None], w["L0_conv_out_norm_b"][:, None],
                                per_direction(w["L0_conv_dt_b"]), per_direction(w["L0_conv_Ds"])], 1),
    }


def sedenion_signs():
    def conj(a):
        if len(a) == 1:
            return a
        h = len(a) // 2
        return np.concatenate([conj(a[:h]), -a[h:]])

    def mult(a, b):
        if len(a) == 1:
            return a * b
        h = len(a) // 2
        a1, a2, b1, b2 = a[:h], a[h:], b[:h], b[h:]
        return np.concatenate([mult(a1, b1) - mult(conj(b2), a2), mult(b2, a1) + mult(a2, conj(b1))])

    eye = np.eye(16, dtype=np.float32)
    return [[int(mult(eye[i], eye[i ^ k])[k]) for k in range(16)] for i in range(16)]


def sedenion_block(nc, w, X):
    P = 16
    WINDOWS = T // P
    HALVES = WINDOWS // N
    LT = 2 * N
    LTILES = T // LT
    F = 4 * C
    FB = F // 128
    SIGNS = sedenion_signs()
    with ExitStack() as ctx:
        sb = lambda name, shape, dt=F32: ctx.enter_context(nc.sbuf_tensor(name, shape, dt))
        sem = lambda name: ctx.enter_context(nc.semaphore(name))

        xn = sb("l1_xn", [C, P, WINDOWS])
        w_pos = sb("l1_w_pos", [C, P, C])
        w_neg = sb("l1_w_neg", [C, P, C])
        center = sb("l1_center", [C, C])
        mean_w = sb("l1_mean_w", [C, C])
        w_proj = sb("l1_w_proj", [C, C])
        w_fc1 = sb("l1_w_fc1", [C, F])
        w_fc2 = sb("l1_w_fc2", [128, FB, C])
        cols = sb("l1_cols", [C, 6])
        fc1_b = sb("l1_fc1_b", [128, FB])
        eps = sb("l1_eps", [C, 2])
        s_w, s_const = sem("l1_weights"), sem("l1_constants")
        weights = [(center[:], w["center"]), (mean_w[:], w["mean_w"]), (cols[:], w["cols"]),
                   (w_pos[:], w["w_sed"]), (w_proj[:], w["proj_w"]), (w_fc1[:], w["fc1_w"]),
                   (w_fc2[:], w["fc2_w"]), (fc1_b[:], w["fc1_b"])]

        with ExitStack() as part:
            sb = lambda name, shape, dt=F32: part.enter_context(nc.sbuf_tensor(name, shape, dt))
            ps = lambda name, shape: part.enter_context(nc.psum_tensor(name, shape, F32))
            sem = lambda name: part.enter_context(nc.semaphore(name))
            xsq = sb("l1a_xsq", [C, 2, LT])
            rstd = sb("l1a_rstd", [C, 2, LT])
            xhat = sb("l1a_xhat", [C, 2, LT])
            p_xc = [ps(f"l1a_xc{i}", [C, LT]) for i in range(2)]
            p_var = [ps(f"l1a_var{i}", [C, LT]) for i in range(2)]
            s_xc, s_xsq, s_var, s_lnv, s_rstd, s_xhat, s_xn = (sem("l1a_" + n) for n in (
                "xc", "xsq", "var", "lnvar", "rstd", "xhat", "xn"))
            block = part.enter_context(nc.Block())

            @block.sync
            def _(sp):
                for dst, src in weights:
                    sp.dma_start(dst, src).then_inc(s_w, 16)
                sp.wait_ge(s_w, 16 * len(weights))

            @block.tensor
            def _(pe):
                def center_tile(t, par, first=False):
                    if not first:
                        pe.wait_ge(s_xhat, t - 1)
                        pe.nop(nofuse=True)
                    for j in range(2):
                        mm = pe.matmul(p_xc[par][:, j * N:(j + 1) * N], center[:],
                                       X[:, bass.ds(t * LT + j * N, N)], start=True, stop=True)
                    mm.then_inc(s_xc, 1)

                def var_tile(t, par):
                    pe.wait_ge(s_xsq, t + 1)
                    for j in range(2):
                        mm = pe.matmul(p_var[par][:, j * N:(j + 1) * N], mean_w[:],
                                       xsq[:, par, j * N:(j + 1) * N], start=True, stop=True)
                    mm.then_inc(s_var, 1)

                pe.wait_ge(s_w, 16 * len(weights))
                center_tile(0, 0, first=True)
                center_tile(1, 1, first=True)
                var_tile(0, 0)
                with pe.Fori(0, LTILES // 2 - 1) as i:
                    center_tile(2 * i + 2, 0)
                    var_tile(2 * i + 1, 1)
                    center_tile(2 * i + 3, 1)
                    var_tile(2 * i + 2, 0)
                var_tile(LTILES - 1, 1)

            @block.scalar
            def _(act):
                def square_tile(t, par):
                    act.wait_ge(s_xc, t + 1)
                    act.activation(xsq[:, par, :], p_xc[par][:], ACT.Square).then_inc(s_xsq, 1)

                def rstd_tile(t, par, first=False):
                    act.wait_ge(s_var, t + 1)
                    if not first:
                        act.wait_ge(s_xhat, t - 1)
                    act.activation(rstd[:, par, :], p_var[par][:], ACT.Ln, bias=eps[:, 0:1], scale=VAR_SCALE).then_inc(s_lnv, 1)
                    act.wait_ge(s_lnv, t + 1)
                    act.activation(rstd[:, par, :], rstd[:, par, :], ACT.Exp, bias=eps[:, 1:2], scale=-0.5).then_inc(s_rstd, 1)

                act.preload_act_table_set(LN_EXP)
                act.wait_ge(s_const, 1)
                square_tile(0, 0)
                square_tile(1, 1)
                rstd_tile(0, 0, first=True)
                square_tile(2, 0)
                rstd_tile(1, 1, first=True)
                with act.Fori(0, LTILES // 2 - 2) as i:
                    square_tile(2 * i + 3, 1)
                    rstd_tile(2 * i + 2, 0)
                    square_tile(2 * i + 4, 0)
                    rstd_tile(2 * i + 3, 1)
                square_tile(LTILES - 1, 1)
                rstd_tile(LTILES - 2, 0)
                rstd_tile(LTILES - 1, 1)

            @block.vector
            def _(dve):
                rows = LT // W // 4
                by_place = xn[:].rearrange("c (dy dx) (v wx) -> c v dy wx dx", dy=4, dx=4, wx=W // 4)

                def xn_tile(t, par):
                    dve.wait_ge(s_rstd, t + 1)
                    dve.tensor_tensor(xhat[:, par, :], p_xc[par][:], rstd[:, par, :], ALU.mult).then_inc(s_xhat, 1)
                    dve.wait_ge(s_xhat, t + 1)
                    tokens = xhat[:, par, :].rearrange("c (v dy wx dx) -> c v dy wx dx", dy=4, wx=W // 4, dx=4)
                    for v in range(rows):
                        dve.tensor_scalar(by_place[:, bass.ds(rows * t + v, 1)].rearrange("c v dy wx dx -> c (v dy) wx dx"),
                                          tokens[:, v], cols[:, 0:1], cols[:, 1:2],
                                          ALU.mult, ALU.add).then_inc(s_xn, 1)

                dve.memset(eps[:, 1:2], 0.5 * float(np.log(VAR_SCALE)))
                dve.memset(eps[:, 0:1], EPS * VAR_SCALE).then_inc(s_const, 1)
                dve.wait_ge(s_w, 16 * len(weights))
                dve.tensor_scalar(w_neg[:], w_pos[:], -1.0, None, ALU.mult).then_inc(s_const, 1)
                with dve.Fori(0, LTILES // 2) as i:
                    xn_tile(2 * i, 0)
                    xn_tile(2 * i + 1, 1)

        with ExitStack() as part:
            sb = lambda name, shape, dt=F32: part.enter_context(nc.sbuf_tensor(name, shape, dt))
            ps = lambda name, shape: part.enter_context(nc.psum_tensor(name, shape, F32))
            sem = lambda name: part.enter_context(nc.semaphore(name))
            act_y = sb("l1b_act_y", [C, N])
            x1 = sb("l1b_x1", [C, 2, N])
            xsq = sb("l1b_xsq", [C, N])
            rstd = sb("l1b_rstd", [C, N])
            h_in = sb("l1b_h_in", [C, N])
            h = sb("l1b_h", [128, FB, N])
            p_y = [ps(f"l1b_y{i}", [C, N]) for i in range(2)]
            p_x1, p_xc, p_var = (ps("l1b_p_" + n, [C, N]) for n in ("x1", "xc", "var"))
            p_h = [ps(f"l1b_h{i}", [128, N]) for i in range(FB)]
            p_out = p_x1
            s_y, s_gy, s_pr, s_x1, s_xc, s_xsq, s_var, s_lnv, s_rstd, s_xhat, s_hin, s_fc1, s_h, s_fc2, s_out = (
                sem("l1b_" + n) for n in ("y", "gelu_y", "projected", "x1_written", "xc", "xsq", "var", "lnvar",
                                          "rstd", "xhat", "h_in", "fc1", "gelu_h", "fc2", "x_written"))
            block = part.enter_context(nc.Block())

            @block.tensor
            def _(pe):
                def product(half, k, i):
                    weight = (w_pos if SIGNS[i][k] > 0 else w_neg)[:, i ^ k, :]
                    mm = pe.matmul(p_y[k % 2][:], weight, xn[:, i, bass.ds(half * N, N)],
                                   start=(i == 0), stop=(i == P - 1))
                    if i == P - 1:
                        mm.then_inc(s_y, 1)

                def project(tile):
                    pe.wait_ge(s_gy, tile + 1)
                    pe.wait_ge(s_out, tile + 1)
                    pe.matmul(p_x1[:], w_proj[:], act_y[:], start=True, stop=True).then_inc(s_pr, 1)

                def centered(tile, par):
                    pe.wait_ge(s_x1, tile + 1)
                    pe.matmul(p_xc[:], center[:], x1[:, par, :], start=True, stop=True).then_inc(s_xc, 1)

                def variance(tile):
                    pe.wait_ge(s_xsq, tile + 1)
                    pe.matmul(p_var[:], mean_w[:], xsq[:], start=True, stop=True).then_inc(s_var, 1)

                def fc1(tile):
                    pe.wait_ge(s_hin, tile + 1)
                    for f in range(FB):
                        pe.matmul(p_h[f][:], w_fc1[:, f * 128:(f + 1) * 128], h_in[:],
                                  start=True, stop=True).then_inc(s_fc1, 1)

                def fc2(tile):
                    for f in range(FB):
                        pe.wait_ge(s_h, FB * tile + f + 1)
                        mm = pe.matmul(p_out[:], w_fc2[:, f, :], h[:, f, :], start=(f == 0), stop=(f == FB - 1))
                    mm.then_inc(s_fc2, 1)

                with pe.Fori(0, HALVES) as half:
                    for k in range(P):
                        tile = half * P + (k - 1)
                        for i in range(P):
                            product(half, k, i)
                            if k > 0:
                                if i == 3:
                                    project(tile)
                                if i == 6:
                                    centered(tile, (k - 1) % 2)
                                if i == 8:
                                    variance(tile)
                                if i == 11:
                                    fc1(tile)
                                if i == 14:
                                    fc2(tile)
                    tile = half * P + (P - 1)
                    project(tile)
                    centered(tile, (P - 1) % 2)
                    variance(tile)
                    fc1(tile)
                    fc2(tile)

            @block.scalar
            def _(act):
                with act.Fori(0, HALVES) as half:
                    for k in range(P):
                        tile = half * P + k
                        act.wait_ge(s_y, tile + 1)
                        act.activation(act_y[:], p_y[k % 2][:], ACT.Gelu).then_inc(s_gy, 1)
                        act.preload_act_table_set(LN_EXP)
                        act.wait_ge(s_xc, tile + 1)
                        act.activation(xsq[:], p_xc[:], ACT.Square).then_inc(s_xsq, 1)
                        act.wait_ge(s_var, tile + 1)
                        act.activation(rstd[:], p_var[:], ACT.Ln, bias=eps[:, 0:1], scale=VAR_SCALE).then_inc(s_lnv, 1)
                        act.wait_ge(s_lnv, tile + 1)
                        act.activation(rstd[:], rstd[:], ACT.Exp, bias=eps[:, 1:2], scale=-0.5).then_inc(s_rstd, 1)
                        for f in range(FB):
                            act.wait_ge(s_fc1, FB * tile + f + 1)
                            act.activation(h[:, f, :], p_h[f][:], ACT.Gelu, bias=fc1_b[:, f:f + 1]).then_inc(s_h, 1)

            @block.vector
            def _(dve):
                places = X[:].rearrange("c (v dy wx dx) -> c dy dx v wx", dy=4, wx=W // 4, dx=4)
                VH = N // (W // 4)
                dve.sem_inc(s_out, 1)
                with dve.Fori(0, HALVES) as half:
                    for k in range(P):
                        tile = half * P + k
                        x_k = places[:, k // 4, k % 4, bass.ds(half * VH, VH), :]
                        as_x = lambda a: a.rearrange("c (v wx) -> c v wx", wx=W // 4)
                        dve.wait_ge(s_pr, tile + 1)
                        dve.scalar_tensor_tensor(as_x(x1[:, k % 2, :]), as_x(p_x1[:]), cols[:, 2:3], x_k,
                                                 ALU.add, ALU.add).then_inc(s_x1, 1)
                        dve.wait_ge(s_rstd, tile + 1)
                        dve.tensor_tensor(h_in[:], p_xc[:], rstd[:], ALU.mult).then_inc(s_xhat, 1)
                        dve.wait_ge(s_xhat, tile + 1)
                        dve.tensor_scalar(h_in[:], h_in[:], cols[:, 3:4], cols[:, 4:5],
                                          ALU.mult, ALU.add).then_inc(s_hin, 1)
                        dve.wait_ge(s_fc2, tile + 1)
                        dve.scalar_tensor_tensor(x_k, as_x(p_out[:]), cols[:, 5:6], as_x(x1[:, k % 2, :]),
                                                 ALU.add, ALU.add).then_inc(s_out, 1)


def sedenion_layout(w):
    return {
        "center": np.eye(C, dtype=np.float32) - np.float32(1 / C),
        "mean_w": np.full((C, C), 1 / C, np.float32),
        "cols": np.stack([w["L1_conv_" + n] for n in ("norm1_g", "norm1_b", "proj_b", "norm2_g", "norm2_b", "fc2_b")], 1),
        "w_sed": w["L1_conv_w_sed"].transpose(1, 0, 2),
        "proj_w": w["L1_conv_proj_w"],
        "fc1_w": w["L1_conv_fc1_w"],
        "fc2_w": w["L1_conv_fc2_w"].reshape(-1, 128, C).transpose(1, 0, 2),
        "fc1_b": w["L1_conv_fc1_b"].reshape(-1, 128).T,
    }


HEADS, HD, WIN = 6, 16, 7
TAPS = WIN * WIN
PAD = WIN // 2
HP, WP = H + 2 * PAD, W + 2 * PAD
PAIRS = H // 2
ROWS = 2 * PAD + 2
STRIP = N // W


def attention_qkv(nc, w, X, qkv_d, x_d):
    with ExitStack() as ctx:
        sb = lambda name, shape, dt=F32: ctx.enter_context(nc.sbuf_tensor(name, shape, dt))
        ps = lambda name, shape: ctx.enter_context(nc.psum_tensor(name, shape, F32))
        sem = lambda name: ctx.enter_context(nc.semaphore(name))
        w_qkv = sb("l2a_w_qkv", [C, 3, C])
        cols = sb("l2a_cols", [C, 8])
        stats = sb("l2a_stats", [C, TILES, 6])
        moments = sb("l2a_moments", [C, 2])
        bias = sb("l2a_bias", [C, 3])
        norm = sb("l2a_norm", [C, 4])
        eps = sb("l2a_eps", [C, 2])
        zeros = sb("l2a_zeros", [C, 3, PAD * WP])
        xn = sb("l2a_xn", [C, 2, N])
        strip = sb("l2a_strip", [C, 2, 3, STRIP, WP])
        p_qkv = [[ps(f"l2a_p{par}{g}", [C, N]) for g in range(3)] for par in range(2)]
        s_w, s_zero, s_pads, s_x, s_stats, s_norm, s_lnv = (sem("l2a_" + n) for n in (
            "weights", "zeroed", "pads_stored", "x_stored", "stats", "norm", "lnvar"))
        s_xn, s_mm, s_qk, s_v = (sem("l2a_" + n) for n in ("xn", "qkv_mm", "qk_in_strip", "v_in_strip"))
        s_strip = [sem(f"l2a_strip{i}_stored") for i in range(2)]
        by_group = qkv_d.rearrange("(g c) b p -> c g b p", c=C)
        block = ctx.enter_context(nc.Block())

        @block.sync
        def _(sp):
            sp.dma_start(w_qkv[:], w["qkv_w"]).then_inc(s_w, 16)
            sp.dma_start(cols[:], w["cols"]).then_inc(s_w, 16)
            for b in range(B):
                sp.dma_start(x_d[:, b * HW:(b + 1) * HW], X[:, b * HW:(b + 1) * HW]).then_inc(s_x, 16)
            sp.wait_ge(s_zero, 1)
            for b in range(B):
                for row in (0, HP - PAD):
                    sp.dma_start(by_group[:, :, b, row * WP:(row + PAD) * WP], zeros[:]).then_inc(s_pads, 16)
            with sp.Fori(0, B) as b:
                with sp.Fori(0, H // STRIP // 2) as s2:
                    for par in range(2):
                        tile = b * (H // STRIP) + 2 * s2 + par
                        sp.wait_ge(s_qk, 2 * tile + 2)
                        sp.nop(nofuse=True)
                        sp.wait_ge(s_v, tile + 1)
                        sp.nop(nofuse=True)
                        sp.dma_start(by_group[:, :, bass.ds(b, 1), bass.ds((PAD + par * STRIP) * WP + s2 * (2 * STRIP * WP), STRIP * WP)],
                                     strip[:, par].rearrange("c g r x -> c g (r x)")).then_inc(s_strip[par], 16)
            for par in range(2):
                sp.wait_ge(s_strip[par], 16 * (TILES // 2))
            sp.wait_ge(s_pads, 16 * 2 * B)
            sp.wait_ge(s_x, 16 * B)

        @block.tensor
        def _(pe):
            def qkv(t, par, first=False):
                pe.wait_ge(s_xn, t + 1)
                if not first:
                    pe.wait_ge(s_qk, 2 * t - 2)
                    pe.wait_ge(s_v, t - 1)
                for g in range(3):
                    mm = pe.matmul(p_qkv[par][g][:], w_qkv[:, g, :], xn[:, par, :], start=True, stop=True)
                mm.then_inc(s_mm, 1)

            pe.wait_ge(s_w, 32)
            qkv(0, 0, first=True)
            qkv(1, 1, first=True)
            with pe.Fori(1, TILES // 2) as i:
                qkv(2 * i, 0)
                qkv(2 * i + 1, 1)

        @block.scalar
        def _(act):
            def qk_to_strip(t, par, first=False):
                act.wait_ge(s_mm, t + 1)
                if not first:
                    act.wait_ge(s_strip[par], 8 * (t - par))
                for g in range(2):
                    act.activation(strip[:, par, g, :, PAD:PAD + W], p_qkv[par][g][:].rearrange("c (r x) -> c r x", x=W),
                                   ACT.Identity, bias=bias[:, g:g + 1], scale=cols[:, 5 + g:6 + g]).then_inc(s_qk, 1)

            act.preload_act_table_set(LN_EXP)
            act.wait_ge(s_stats, TILES + 1)
            act.activation(norm[:, 0:1], moments[:, 1:2], ACT.Ln, bias=eps[:, 0:1], scale=VAR_SCALE).then_inc(s_lnv, 1)
            act.wait_ge(s_lnv, 1)
            act.activation(norm[:, 1:2], norm[:, 0:1], ACT.Exp, bias=eps[:, 1:2], scale=-0.5).then_inc(s_lnv, 1)
            act.wait_ge(s_norm, 5)
            qk_to_strip(0, 0, first=True)
            qk_to_strip(1, 1, first=True)
            with act.Fori(1, TILES // 2) as i:
                qk_to_strip(2 * i, 0)
                qk_to_strip(2 * i + 1, 1)

        @block.vector
        def _(dve):
            def xn_tile(t, par, first=False):
                if not first:
                    dve.wait_ge(s_mm, t - 1)
                    dve.nop(nofuse=True)
                dve.tensor_scalar(xn[:, par, :], X[:, bass.ds(t * N, N)], norm[:, 2:3], norm[:, 3:4],
                                  ALU.mult, ALU.add).then_inc(s_xn, 1)

            def v_to_strip(t, par, first=False):
                dve.wait_ge(s_mm, t + 1)
                if not first:
                    dve.wait_ge(s_strip[par], 8 * (t - par))
                dve.tensor_scalar(strip[:, par, 2, :, PAD:PAD + W], p_qkv[par][2][:].rearrange("c (r x) -> c r x", x=W),
                                  bias[:, 2:3], None, ALU.add).then_inc(s_v, 1)

            dve.memset(zeros[:], 0.0).then_inc(s_zero, 1)
            dve.memset(strip[:], 0.0).then_inc(s_norm, 1)
            dve.memset(eps[:, 1:2], 0.5 * float(np.log(VAR_SCALE)))
            dve.memset(eps[:, 0:1], EPS * VAR_SCALE).then_inc(s_norm, 1)
            with dve.Fori(0, TILES) as t:
                dve.bn_stats(stats[:, bass.ds(t, 1), :].rearrange("c t s -> c (t s)"),
                             X[:, bass.ds(t * N, N)]).then_inc(s_stats, 1)
            dve.wait_ge(s_stats, TILES)
            dve.bn_aggr(moments[:], stats[:].rearrange("c t s -> c (t s)")).then_inc(s_stats, 1)
            dve.wait_ge(s_w, 32)
            dve.tensor_tensor(bias[:], cols[:, 2:5], cols[:, 5:8], ALU.mult).then_inc(s_norm, 1)
            dve.wait_ge(s_lnv, 2)
            dve.tensor_tensor(norm[:, 2:3], cols[:, 0:1], norm[:, 1:2], ALU.mult).then_inc(s_norm, 1)
            dve.wait_ge(s_norm, 4)
            dve.tensor_tensor(norm[:, 0:1], moments[:, 0:1], norm[:, 2:3], ALU.mult).then_inc(s_zero, 1)
            dve.wait_ge(s_zero, 2)
            dve.tensor_tensor(norm[:, 3:4], cols[:, 1:2], norm[:, 0:1], ALU.subtract).then_inc(s_norm, 1)
            dve.wait_ge(s_norm, 5)
            xn_tile(0, 0, first=True)
            xn_tile(1, 1, first=True)
            v_to_strip(0, 0, first=True)
            v_to_strip(1, 1, first=True)
            with dve.Fori(1, TILES // 2) as i:
                xn_tile(2 * i, 0)
                xn_tile(2 * i + 1, 1)
                v_to_strip(2 * i, 0)
                v_to_strip(2 * i + 1, 1)


def attention_heads(nc, w, qkv_d, o_d):
    SHIFTS, GROUPS = 4, 2
    CH = 2 * HD
    GROWS = HP - SHIFTS + 1
    CP = 8
    CHUNKS = PAIRS // CP
    M = 2 * TAPS
    XT = 4
    TURNS = W // XT
    VC = HD // 2
    CG = 2
    UNITS = 2 * HD // CG
    EXPS = 4
    with ExitStack() as ctx:
        sb = lambda name, shape, dt=F32: ctx.enter_context(nc.sbuf_tensor(name, shape, dt))
        ps = lambda name, shape: ctx.enter_context(nc.psum_tensor(name, shape, F32))
        sem = lambda name: ctx.enter_context(nc.semaphore(name))
        w_conv = sb("l2b_w_conv", [128, GROUPS, WIN, M])
        ident = sb("l2b_ident", [M, M])
        dm_b = sb("l2b_dm_b", [M, 1])
        rel_b = sb("l2b_rel_b", [M, HEADS])
        head_b = sb("l2b_head_b", [M, HEADS])
        this_b = sb("l2b_this_b", [M, 1])
        img = sb("l2b_img", [128, 2, GROWS, WP])
        logits = sb("l2b_logits", [M, B, PAIRS, W])
        attn = sb("l2b_attn", [128, W, 2, TAPS])
        peak = sb("l2b_peak", [128, W, 2])
        total = sb("l2b_total", [128, W, 2])
        v = [sb(f"l2b_v{i}", [128, VC, ROWS, WP]) for i in range(2)]
        prod = [sb(f"l2b_prod{i}", [128, CG, W, TAPS]) for i in range(2)]
        osum = sb("l2b_osum", [128, HD, 2, W])
        p_conv = [ps(f"l2b_conv{i}", [M, N]) for i in range(2)]
        p_turn = [ps(f"l2b_turn{i}", [128, XT, 2, TAPS]) for i in range(3)]
        s_w, s_v, s_o = (sem("l2b_" + n) for n in ("weights", "v_loaded", "o_stored"))
        s_img = [sem(f"l2b_img{i}_loaded") for i in range(2)]
        s_bias, s_this, s_conv, s_log, s_turn, s_peak, s_sub, s_exp = (sem("l2b_" + n) for n in (
            "bias", "this_bias", "conv", "logits", "turned", "peak", "shifted", "exp"))
        s_tot, s_rcp, s_pp, s_pv, s_sum, s_osum = (sem("l2b_" + n) for n in (
            "total", "reciprocal", "pool_products", "vector_products", "summed", "scaled"))
        block = ctx.enter_context(nc.Block())

        @block.sync
        def _(sp):
            def load_image(head, b, first=False):
                if not first:
                    sp.wait_ge(s_conv, head * (B * CHUNKS) + (b - 1) * CHUNKS)
                    sp.nop(nofuse=True)
                for s in range(SHIFTS):
                    sp.dma_start(img[s * CH:(s + 1) * CH, b % 2].rearrange("c r x -> c (r x)"),
                                 qkv_d[bass.ds(head * CH, CH), b, s * WP:(s + GROWS) * WP]).then_inc(s_img[b % 2], 16)

            def load_v(head, first=False):
                for half in range(2):
                    if not first:
                        done = (half + 1) * (UNITS // 4)
                        sp.wait_ge(s_pv, head * (UNITS // 2) + (done - UNITS // 2))
                        sp.nop(nofuse=True)
                        sp.wait_ge(s_pp, head * (UNITS // 2) + (done - UNITS // 2))
                        sp.nop(nofuse=True)
                    for b in range(B):
                        src = qkv_d[bass.ds(head * HD + (2 * C + half * VC), VC), b]
                        src = bass.AP(src.tensor, src.offset,
                                      [[2 * WP, PAIRS], [B * HP * WP, VC], [1, ROWS * WP]])
                        sp.dma_start(v[half][b * PAIRS:(b + 1) * PAIRS].rearrange("p c r x -> p c (r x)"),
                                     src).then_inc(s_v, 16)

            def store_o(head):
                sp.wait_ge(s_osum, head + 1)
                sp.nop(nofuse=True)
                sp.dma_start(o_d[bass.ds(head * HD, HD)].rearrange("c (q z) -> q c z", z=2 * W),
                             osum[:].rearrange("q c r x -> q c (r x)")).then_inc(s_o, 16)

            for dst, src in ((w_conv, "w_conv"), (ident, "ident"), (dm_b, "dm_b"), (rel_b, "rel_b")):
                sp.dma_start(dst[:], w[src]).then_inc(s_w, 16)
            load_image(0, 0, first=True)
            load_image(0, 1, first=True)
            load_v(0, first=True)
            load_image(0, 2)
            load_image(0, 3)
            load_image(1, 0)
            with sp.Fori(1, HEADS - 1) as head:
                load_image(head, 1)
                load_image(head, 2)
                load_image(head, 3)
                load_image(head + 1, 0)
                load_v(head)
                store_o(head - 1)
            load_image(HEADS - 1, 1)
            load_image(HEADS - 1, 2)
            load_image(HEADS - 1, 3)
            load_v(HEADS - 1)
            store_o(HEADS - 2)
            store_o(HEADS - 1)
            sp.wait_ge(s_o, 16 * HEADS)

        @block.tensor
        def _(pe):
            def conv(head, b, ch, first=False):
                n = b * CHUNKS + ch
                if ch == 0:
                    pe.wait_ge(s_img[b % 2], 16 * SHIFTS * B // 2 * head + 16 * SHIFTS * (b // 2 + 1))
                if not first:
                    pe.wait_ge(s_log, head * (B * CHUNKS) + (n - 1))
                for g in range(GROUPS):
                    for dx in range(WIN):
                        row = 2 * CP * ch + SHIFTS * g
                        mm = pe.matmul(p_conv[n % 2][:], w_conv[:, g, dx, :],
                                       img[:, b % 2, row:row + 2 * CP - 1:2, dx:dx + W],
                                       start=(g == 0 and dx == 0), stop=(g == GROUPS - 1 and dx == WIN - 1))
                mm.then_inc(s_conv, 1)

            def turn(head, g, first=False):
                if not first:
                    pe.wait_ge(s_sub, head * TURNS + max(g - 2, 0))
                for j in range(XT):
                    mm = pe.transpose(p_turn[g % 3][:, j].rearrange("q r t -> q (r t)"),
                                      logits[:, :, :, XT * g + j].rearrange("m b p -> m (b p)"), ident[:])
                mm.then_inc(s_turn, 1)

            def head_step(head, first=False):
                for b in range(B):
                    for ch in range(CHUNKS):
                        conv(head, b, ch, first=first and b == 0 and ch < 2)
                pe.wait_ge(s_log, head * (B * CHUNKS) + B * CHUNKS)
                for g in range(TURNS):
                    turn(head, g, first=first and g < 3)

            pe.wait_ge(s_w, 64)
            head_step(0, first=True)
            with pe.Fori(1, HEADS) as head:
                head_step(head)

        @block.scalar
        def _(act):
            act.preload_act_table_set(LN_EXP)
            act.wait_ge(s_bias, 1)
            with act.Fori(0, HEADS) as head:
                act.activation(this_b[:], head_b[:, bass.ds(head, 1)], ACT.Copy).then_inc(s_this, 1)
                act.wait_ge(s_this, head + 1)
                for b in range(B):
                    for ch in range(CHUNKS):
                        n = b * CHUNKS + ch
                        act.wait_ge(s_conv, head * (B * CHUNKS) + n + 1)
                        act.activation(logits[:, b, CP * ch:CP * (ch + 1), :].rearrange("m p x -> m (p x)"),
                                       p_conv[n % 2][:], ACT.Identity, bias=this_b[:]).then_inc(s_log, 1)
                for e in range(EXPS):
                    act.wait_ge(s_sub, head * TURNS + (e + 1) * (TURNS // EXPS))
                    piece = attn[:, e * (W // EXPS):(e + 1) * (W // EXPS)].rearrange("q x r t -> q (x r t)")
                    act.activation(piece, piece, ACT.Exp).then_inc(s_exp, 1)

        def products(eng, unit, dst):
            c0, r = unit // 2 * CG, unit % 2
            for c in range(CG):
                src = v[(c0 + c) // VC][:, (c0 + c) % VC, r:r + WIN, 0:W]
                step = list(src.ap)
                window = bass.AP(src.tensor, src.offset, [step[0], [1, W], [WP, WIN], [1, WIN]])
                mm = eng.tensor_tensor(dst[:, c].rearrange("q x (dy dx) -> q x dy dx", dx=WIN), window,
                                       attn[:, :, r].rearrange("q x (dy dx) -> q x dy dx", dx=WIN), ALU.mult)
            return mm

        @block.vector
        def _(dve):
            def softmax(head):
                for g in range(TURNS):
                    dve.wait_ge(s_turn, head * TURNS + g + 1)
                    dve.tensor_reduce(peak[:, XT * g:XT * (g + 1)], p_turn[g % 3][:], AX_X, ALU.max).then_inc(s_peak, 1)
                    dve.wait_ge(s_peak, head * TURNS + g + 1)
                    top = peak[:, XT * g:XT * (g + 1)]
                    dve.tensor_tensor(attn[:, XT * g:XT * (g + 1)].rearrange("q x r t -> q (x r) t"),
                                      p_turn[g % 3][:].rearrange("q x r t -> q (x r) t"),
                                      top.rearrange("q x r -> q (x r)").unsqueeze(2).to_broadcast([128, XT * 2, TAPS]),
                                      ALU.subtract).then_inc(s_sub, 1)
                for e in range(EXPS):
                    dve.wait_ge(s_exp, head * EXPS + e + 1)
                    part = slice(e * (W // EXPS), (e + 1) * (W // EXPS))
                    dve.tensor_reduce(total[:, part], attn[:, part], AX_X, ALU.add).then_inc(s_tot, 1)
                dve.wait_ge(s_tot, head * EXPS + EXPS)
                dve.reciprocal(total[:], total[:]).then_inc(s_rcp, 1)

            def sums(head, unit, first=False):
                c0, r = unit // 2 * CG, unit % 2
                if unit % 2:
                    dve.wait_ge(s_pp, head * (UNITS // 2) + unit // 2 + 1)
                else:
                    dve.wait_ge(s_pv, head * (UNITS // 2) + unit // 2 + 1)
                dve.tensor_reduce(osum[:, c0:c0 + CG, r, :], prod[unit % 2][:], AX_X, ALU.add).then_inc(s_sum, 1)

            def head_step(head, first=False):
                softmax(head)
                dve.wait_ge(s_v, 16 * 2 * B * head + 16 * 2 * B)
                if not first:
                    dve.wait_ge(s_o, 16 * head)
                for unit in range(0, UNITS, 2):
                    if unit:
                        dve.wait_ge(s_sum, head * UNITS + unit - 1)
                    products(dve, unit, prod[0]).then_inc(s_pv, 1)
                    sums(head, unit)
                    sums(head, unit + 1)
                dve.wait_ge(s_sum, head * UNITS + UNITS)
                dve.wait_ge(s_rcp, head + 1)
                inverse = bass.AP(total[:].tensor, total[:].offset, [list(total[:].ap)[0], [0, HD], [1, 2], [2, W]])
                dve.tensor_tensor(osum[:], osum[:], inverse, ALU.mult).then_inc(s_osum, 1)

            dve.wait_ge(s_w, 64)
            dve.tensor_scalar(head_b[:], rel_b[:], dm_b[:], None, ALU.add).then_inc(s_bias, 1)
            head_step(0, first=True)
            with dve.Fori(1, HEADS) as head:
                head_step(head)

        @block.gpsimd
        def _(pool):
            def head_step(head, first=False):
                pool.wait_ge(s_exp, head * EXPS + EXPS)
                pool.wait_ge(s_v, 16 * 2 * B * head + 16 * 2 * B)
                for unit in range(1, UNITS, 2):
                    if not (first and unit == 1):
                        pool.wait_ge(s_sum, head * UNITS + (unit - 1))
                    products(pool, unit, prod[1]).then_inc(s_pp, 1)

            head_step(0, first=True)
            with pool.Fori(1, HEADS) as head:
                head_step(head)


def attention_out(nc, w, X, o_d, x_d):
    F = 4 * C
    FB = F // 128
    with ExitStack() as ctx:
        sb = lambda name, shape, dt=F32: ctx.enter_context(nc.sbuf_tensor(name, shape, dt))
        ps = lambda name, shape: ctx.enter_context(nc.psum_tensor(name, shape, F32))
        sem = lambda name: ctx.enter_context(nc.semaphore(name))
        w_proj = sb("l2c_w_proj", [C, C])
        w_c1 = sb("l2c_w_c1", [C, F])
        w_c2 = sb("l2c_w_c2", [128, FB, C])
        c1_b = sb("l2c_c1_b", [128, FB])
        cols = sb("l2c_cols", [C, 2])
        o = sb("l2c_o", [C, T])
        x1 = sb("l2c_x1", [C, 2, N])
        h = sb("l2c_h", [128, FB, N])
        p_x1 = [ps(f"l2c_p_x1{i}", [C, N]) for i in range(2)]
        p_out = [ps(f"l2c_p_out{i}", [C, N]) for i in range(2)]
        p_h = [ps(f"l2c_p_h{i}", [128, N]) for i in range(FB)]
        s_w, s_o, s_x = (sem("l2c_" + n) for n in ("weights", "o_loaded", "x_loaded"))
        s_pr, s_x1, s_c1, s_h, s_c2, s_out = (sem("l2c_" + n) for n in (
            "projected", "x1_written", "c1", "gelu_h", "c2", "x_written"))
        block = ctx.enter_context(nc.Block())

        @block.sync
        def _(sp):
            for dst, src in ((w_proj, "proj_w"), (w_c1, "c1_w"), (w_c2, "c2_w"), (c1_b, "c1_b"), (cols, "cols_out")):
                sp.dma_start(dst[:], w[src]).then_inc(s_w, 16)
            for b in range(B):
                image = slice(b * HW, (b + 1) * HW)
                sp.dma_start(o[:, image], o_d[:, image]).then_inc(s_o, 16)
                sp.dma_start(X[:, image], x_d[:, image]).then_inc(s_x, 16)

        @block.tensor
        def _(pe):
            def project(t, par, first=False):
                if not first:
                    pe.wait_ge(s_x1, t - 1)
                    pe.nop(nofuse=True)
                pe.matmul(p_x1[par][:], w_proj[:], o[:, bass.ds(t * N, N)], start=True, stop=True).then_inc(s_pr, 1)

            def mlp(t, par, first=False):
                pe.wait_ge(s_x1, t + 1)
                for f in range(FB):
                    if not first:
                        pe.wait_ge(s_h, FB * t + f - FB + 1)
                    pe.matmul(p_h[f][:], w_c1[:, f * 128:(f + 1) * 128], x1[:, par, :],
                              start=True, stop=True).then_inc(s_c1, 1)

            def mlp_out(t, par, first=False):
                if not first:
                    pe.wait_ge(s_out, t - 1)
                for f in range(FB):
                    pe.wait_ge(s_h, FB * t + f + 1)
                    mm = pe.matmul(p_out[par][:], w_c2[:, f, :], h[:, f, :], start=(f == 0), stop=(f == FB - 1))
                mm.then_inc(s_c2, 1)

            pe.wait_ge(s_w, 16 * 5)
            pe.wait_ge(s_o, 16 * B)
            project(0, 0, first=True)
            mlp(0, 0, first=True)
            project(1, 1, first=True)
            mlp_out(0, 0, first=True)
            mlp(1, 1)
            project(2, 0)
            mlp_out(1, 1, first=True)
            with pe.Fori(1, TILES // 2 - 1) as i:
                mlp(2 * i, 0)
                project(2 * i + 1, 1)
                mlp_out(2 * i, 0)
                mlp(2 * i + 1, 1)
                project(2 * i + 2, 0)
                mlp_out(2 * i + 1, 1)
            mlp(TILES - 2, 0)
            project(TILES - 1, 1)
            mlp_out(TILES - 2, 0)
            mlp(TILES - 1, 1)
            mlp_out(TILES - 1, 1)

        @block.scalar
        def _(act):
            def gelus(t, first=False):
                for f in range(FB):
                    act.wait_ge(s_c1, FB * t + f + 1)
                    if not first:
                        act.wait_ge(s_c2, t)
                    act.activation(h[:, f, :], p_h[f][:], ACT.Gelu, bias=c1_b[:, f:f + 1]).then_inc(s_h, 1)

            act.wait_ge(s_w, 16 * 5)
            gelus(0, first=True)
            with act.Fori(1, TILES) as t:
                gelus(t)

        @block.vector
        def _(dve):
            def x1_tile(t, par, first=False):
                if not first:
                    dve.wait_ge(s_out, t - 1)
                dve.wait_ge(s_pr, t + 1)
                dve.scalar_tensor_tensor(x1[:, par, :], p_x1[par][:], cols[:, 0:1], X[:, bass.ds(t * N, N)],
                                         ALU.add, ALU.add).then_inc(s_x1, 1)

            def out_tile(t, par):
                dve.wait_ge(s_c2, t + 1)
                dve.scalar_tensor_tensor(X[:, bass.ds(t * N, N)], p_out[par][:], cols[:, 1:2], x1[:, par, :],
                                         ALU.add, ALU.add).then_inc(s_out, 1)

            dve.wait_ge(s_w, 16 * 5)
            dve.wait_ge(s_x, 16 * B)
            x1_tile(0, 0, first=True)
            x1_tile(1, 1, first=True)
            with dve.Fori(0, TILES // 2 - 1) as i:
                out_tile(2 * i, 0)
                x1_tile(2 * i + 2, 0)
                out_tile(2 * i + 1, 1)
                x1_tile(2 * i + 3, 1)
            out_tile(TILES - 2, 0)
            out_tile(TILES - 1, 1)


def local_attention_layout(w):
    g = {n[len("L2_conv_"):]: a for n, a in w.items() if n.startswith("L2_conv_")}
    q, k, v = (np.arange(i * C, (i + 1) * C).reshape(HEADS, HD) for i in range(3))
    rows = np.concatenate([np.concatenate([q, k], 1).ravel(), v.ravel()]).reshape(3, C)
    is_q = rows < C
    scale = np.where(is_q, np.float32(HD ** -0.5), np.float32(1)).astype(np.float32)
    conv = np.zeros((4, 2 * HD, 2, WIN, 2, TAPS), np.float32)
    for s in range(4):
        for grp in range(2):
            for r in range(2):
                dy = 4 * grp + s - r
                if 0 <= dy < WIN:
                    conv[s, :, grp, :, r, :] = g["dm_w"][:, :, dy, :].transpose(1, 2, 0)
    return {
        "qkv_w": g["qkv_w"][rows].transpose(2, 0, 1),
        "cols": np.concatenate([g["bn_gamma"][:, None], g["bn_beta"][:, None], g["qkv_b"][rows].T, scale.T], 1),
        "w_conv": conv.reshape(8 * HD, 2, WIN, 2 * TAPS),
        "ident": np.eye(2 * TAPS, dtype=np.float32),
        "dm_b": np.tile(g["dm_b"], 2)[:, None],
        "rel_b": np.tile(g["rel_bias"], (2, 1)),
        "proj_w": g["proj_w"].T,
        "c1_w": g["c1_w"].T,
        "c2_w": g["c2_w"].T.reshape(-1, 128, C).transpose(1, 0, 2),
        "c1_b": g["c1_b"].reshape(-1, 128).T,
        "cols_out": np.stack([g["proj_b"], g["c2_b"]], 1),
    }


def selective_scan(nc, w, X):
    K, S, R, DL = 4, 16, 6, 8
    G = C // DL
    Q = 32
    PARTS = C // Q
    CHUNKS = HW // N
    STEPS = K * CHUNKS
    LAG = 3
    HCS = 4
    DAS = 3
    SMALL_E = 2.0 ** -8
    COLS = N // H
    with ExitStack() as ctx:
        sb = lambda name, shape, dt=F32: ctx.enter_context(nc.sbuf_tensor(name, shape, dt))
        ps = lambda name, shape: ctx.enter_context(nc.psum_tensor(name, shape, F32))
        sem = lambda name: ctx.enter_context(nc.semaphore(name))
        xp_dt = sb("l3_xp_dt", [R, K, C])
        dt_w = sb("l3_dt_w", [R, K, C])
        w_dt = sb("l3_w_dt", [C, K, C])
        w_rep = sb("l3_w_rep", [C, K, 2, 128])
        pick_f = sb("l3_pick_f", [C, Q // DL, 128])
        pick = sb("l3_pick", [C, Q // DL, 128], BF16)
        y_pick = sb("l3_y_pick", [128, G, C])
        a_neg = sb("l3_a_neg", [128, K * G])
        cols = sb("l3_cols", [C, 2 * K])
        d_sum = sb("l3_d_sum", [C, 1])

        xt = sb("l3_xt", [C, HW])
        y_sum = sb("l3_y_sum", [C, HW])
        dx_pos = sb("l3_dx_pos", [C, N])
        e_x = sb("l3_e_x", [C, N])
        log_e = sb("l3_log_e", [C, N])
        series = sb("l3_series", [C, N])
        small = sb("l3_small", [C, N], mybir.dt.uint8)
        dd = sb("l3_dd", [C, 2, 2, N])
        parts = sb("l3_parts", [C, 2, PARTS, 2, N], BF16)
        stacked = sb("l3_stacked", [C, 2, PARTS, 2, N], BF16)
        b_rep = sb("l3_b_rep", [128, 2, N])
        c_rep = sb("l3_c_rep", [128, 2, N])
        da = sb("l3_da", [128, DAS, N])
        bu = sb("l3_bu", [128, DAS, N])
        h = sb("l3_h", [128, G, N])
        hc = sb("l3_hc", [128, HCS, N])
        p_da = [ps(f"l3_p_da{i}", [128, N]) for i in range(2)]
        p_du = [ps(f"l3_p_du{i}", [128, N]) for i in range(2)]
        p_y = [ps(f"l3_p_y{i}", [C, N]) for i in range(2)]
        p_dt, p_bc = ps("l3_p_dt", [C, N]), ps("l3_p_bc", [128, N])

        s_w, s_setup, s_setup_cp, s_a, s_xt = (sem("l3_" + n) for n in (
            "weights", "setup_mm", "setup_copied", "a", "xt_written"))
        s_dt, s_dx, s_abs, s_exp, s_sp, s_delta, s_du, s_hi, s_rest, s_mid, s_lo = (sem("l3_" + n) for n in (
            "dt_mm", "dx", "dt_abs", "dt_exp", "softplus_log", "delta", "du", "part_hi", "rest", "part_mid", "part_lo"))
        s_factor, s_series, s_logp = sem("l3_series_factor"), sem("l3_series_and_mask"), sem("l3_log1p")
        s_stack = [sem(f"l3_stacked{i}") for i in range(2)]
        s_bc, s_bccp = sem("l3_bc_mm"), sem("l3_bc_copied")
        s_rep, s_da, s_bu, s_h, s_hc, s_ymm, s_y = (sem("l3_" + n) for n in (
            "replicated", "da", "bu", "h", "hc", "y_mm", "y_added"))
        REP0, DA0, BU0, H0, HC0, YMM0, Y0 = 2 * G, 2, 2, DAS, 2 * G, HCS, 2
        DX0, DELTA0, LO0, BCCP0 = 1, 1, 2, 1
        weights = [(xp_dt, "xp_dt"), (dt_w, "dt_w_T"), (w_rep, "w_rep"), (pick_f, "pick"),
                   (y_pick, "y_pick"), (a_neg, "a_logs"), (cols, "cols")]
        block = ctx.enter_context(nc.Block())

        def chunk_of(k, c):
            return c if k < 2 else CHUNKS - 1 - c

        def u_of(k, b, c):
            at = chunk_of(k, c) * N
            return X[:, bass.ds(b * HW + at, N)] if k % 2 == 0 else xt[:, bass.ds(at, N)]

        def ahead(k, c, by):
            if not isinstance(c, int):
                return k, c + by
            at = k * CHUNKS + c + by
            return (at // CHUNKS, at % CHUNKS) if 0 <= at < STEPS else None

        def all_steps(eng, image_start, step, image_end):
            def at(b, k, c, par):
                step(b, b * STEPS + (k * CHUNKS) + c, k, c, par, ahead(k, c, 1), ahead(k, c, 2))

            with eng.Fori(0, B) as b:
                image_start(b)
                for k in range(K):
                    at(b, k, 0, 0)
                    at(b, k, 1, 1)
                    with eng.Fori(1, CHUNKS // 2 - 1) as i:
                        at(b, k, 2 * i, 0)
                        at(b, k, 2 * i + 1, 1)
                    at(b, k, CHUNKS - 2, 0)
                    at(b, k, CHUNKS - 1, 1)
                image_end(b)

        @block.sync
        def _(sp_):
            for dst, src in weights:
                sp_.dma_start(dst[:], w[src]).then_inc(s_w, 16)

            def restack(m, par):
                for part, (ready, credit) in enumerate(((s_hi, 0), (s_mid, 0), (s_lo, LO0))):
                    sp_.wait_ge(ready, m + 1 + credit)
                    sp_.nop(nofuse=True)
                    if part == 0:
                        sp_.wait_ge(s_rep, G * (m - 1) + REP0)
                        sp_.nop(nofuse=True)
                    for q in range(PARTS):
                        sp_.dma_start(stacked[part * Q:(part + 1) * Q, par, q],
                                      parts[q * Q:(q + 1) * Q, par, part]).then_inc(s_stack[par], 16)

            with sp_.Fori(0, B * STEPS // 2) as i:
                restack(2 * i, 0)
                restack(2 * i + 1, 1)

        @block.tensor
        def _(pe):
            pe.wait_ge(s_w, 16 * len(weights))
            for k in range(K):
                pe.matmul(p_dt[:, k * C:(k + 1) * C], xp_dt[:, k, :], dt_w[:, k, :],
                          start=True, stop=True).then_inc(s_setup, 1)
            pe.wait_ge(s_setup_cp, 2)
            pe.sem_inc(s_rep, REP0)
            pe.sem_inc(s_ymm, YMM0)

            def delta_mm(m, b, k, c):
                pe.wait_ge(s_dx, m + DX0)
                pe.nop(nofuse=True)
                pe.matmul(p_dt[:], w_dt[:, k, :], u_of(k, b, c), start=True, stop=True).then_inc(s_dt, 1)

            def bc_mm(m, b, k, c, j):
                pe.wait_ge(s_bccp, 2 * m + j + BCCP0)
                pe.nop(nofuse=True)
                pe.matmul(p_bc[:], w_rep[:, k, j, :], u_of(k, b, c), start=True, stop=True).then_inc(s_bc, 1)

            def replicate(n, g, par):
                pe.wait_ge(s_da, G * n + g - 1 + DA0)
                pe.matmul(p_da[g % 2][:], pick[:, g % (Q // DL), :], stacked[:, par, g * DL // Q, 0, :],
                          start=True, stop=True)
                pe.wait_ge(s_bu, G * n + g - 1 + BU0)
                pe.matmul(p_du[g % 2][:], pick[:, g % (Q // DL), :], stacked[:, par, g * DL // Q, 1, :],
                          start=True, stop=True).then_inc(s_rep, 1)

            def y_mm(n, g, par):
                pe.wait_ge(s_hc, G * n + g + 1 + HC0)
                if g == 0:
                    pe.wait_ge(s_y, n - 1 + Y0)
                pe.matmul(p_y[par][:], y_pick[:, g, :], hc[:, g % HCS, :],
                          start=(g == 0), stop=(g == G - 1)).then_inc(s_ymm, 1)

            def image_start(b):
                m = b * STEPS
                delta_mm(m, b, 0, 0)
                delta_mm(m + 1, b, 0, 1)
                bc_mm(m, b, 0, 0, 0)
                bc_mm(m, b, 0, 0, 1)
                pe.wait_ge(s_xt, b + 1)

            def step(b, n, k, c, par, n1, n2):
                pe.wait_ge(s_stack[par], stack_count(b, k, c, par))
                for g in range(G):
                    replicate(n, g, par)
                    if g >= LAG:
                        y_mm(n, g - LAG, par)
                    elif ahead(k, c, -1):
                        y_mm(n - 1, G + g - LAG, 1 - par)
                    if n2 and g == 0:
                        delta_mm(n + 2, b, *n2)
                    if n1 and g == 3:
                        bc_mm(n + 1, b, *n1, 0)
                    if n1 and g == 7:
                        bc_mm(n + 1, b, *n1, 1)

            def image_end(b):
                for g in range(G - LAG, G):
                    y_mm(b * STEPS + (STEPS - 1), g, 1)

            def stack_count(b, k, c, par):
                per = 16 * PARTS * PARTS
                return b * (per * STEPS // 2) + per * (k * CHUNKS // 2 + 1) + (c - par) * (per // 2)

            all_steps(pe, image_start, step, image_end)

        @block.scalar
        def _(act):
            act.preload_act_table_set(LN_EXP)
            act.wait_ge(s_w, 16 * len(weights))
            act.activation(a_neg[:], a_neg[:], ACT.Exp).then_inc(s_a, 1)
            act.wait_ge(s_a, 2)
            act.sem_inc(s_da, DA0)
            act.sem_inc(s_dx, DX0)
            act.sem_inc(s_bccp, BCCP0)

            def abs_dx(m, k):
                act.wait_ge(s_dt, m + 1)
                act.nop(nofuse=True)
                act.wait_ge(s_delta, m + DELTA0)
                act.activation(e_x[:], p_dt[:], ACT.Abs, bias=cols[:, k:k + 1]).then_inc(s_abs, 1)
                act.activation(dx_pos[:], p_dt[:], ACT.Relu, bias=cols[:, k:k + 1]).then_inc(s_dx, 1)

            def exp_dx(m):
                act.wait_ge(s_abs, m + 1)
                act.activation(e_x[:], e_x[:], ACT.Exp, scale=-1.0).then_inc(s_exp, 1)

            def factor(m):
                act.wait_ge(s_exp, m + 1)
                act.activation(series[:], e_x[:], ACT.Copy, scale=-0.5, bias=1.0).then_inc(s_factor, 1)

            def log_1e(m):
                act.activation(log_e[:], e_x[:], ACT.Ln, bias=1.0).then_inc(s_sp, 1)

            def bc_copy(m, par, j):
                act.wait_ge(s_bc, 2 * m + j + 1)
                if j == 1:
                    act.wait_ge(s_hc, G * (m - 1) + HC0)
                act.activation((b_rep, c_rep)[j][:, par, :], p_bc[:], ACT.Copy).then_inc(s_bccp, 1)

            def part_hi(m, par):
                act.wait_ge(s_du, m + 1)
                act.activation(parts[:, par, 0], dd[:, par], ACT.Copy).then_inc(s_hi, 1)

            def part_mid(m, par):
                act.wait_ge(s_rest, m + 1)
                act.activation(parts[:, par, 1], dd[:, par], ACT.Copy).then_inc(s_mid, 1)

            def decay(n, k, g):
                act.wait_ge(s_rep, G * n + g + 1 + REP0)
                act.wait_ge(s_h, G * n + g + 1 - DAS + H0)
                act.activation(da[:, g % DAS, :], p_da[g % 2][:], ACT.Exp,
                               scale=a_neg[:, k * G + g:k * G + g + 1]).then_inc(s_da, 1)

            def image_start(b):
                act.activation(xt[:].rearrange("c (x y) -> c x y", y=H),
                               X[:, bass.ds(b * HW, HW)].rearrange("c (y x) -> c x y", x=W), ACT.Copy).then_inc(s_xt, 1)
                m = b * STEPS
                abs_dx(m, 0)
                for front in (exp_dx, factor, log_1e):
                    front(m)
                bc_copy(m, 0, 0)
                bc_copy(m, 0, 1)
                part_hi(m, 0)
                part_mid(m, 0)
                abs_dx(m + 1, 0)
                for front in (exp_dx, factor, log_1e):
                    front(m + 1)

            def step(b, n, k, c, par, n1, n2):
                for g in range(G):
                    decay(n, k, g)
                    if n2 and g == 1:
                        abs_dx(n + 2, n2[0])
                    if n1 and g == 1:
                        part_hi(n + 1, 1 - par)
                    if n2 and g == 2:
                        exp_dx(n + 2)
                    if n2 and g == 3:
                        factor(n + 2)
                        log_1e(n + 2)
                    if n1 and g == 4:
                        part_mid(n + 1, 1 - par)
                    if n1 and g == 5:
                        bc_copy(n + 1, 1 - par, 0)
                    if n1 and g == 9:
                        bc_copy(n + 1, 1 - par, 1)

            all_steps(act, image_start, step, lambda b: None)

        @block.gpsimd
        def _(pool):
            pool.sem_inc(s_hc, HC0)
            pool.sem_inc(s_lo, LO0)

            def delta_u(m, b, k, c, par):
                pool.wait_ge(s_delta, m + 1 + DELTA0)
                pool.nop(nofuse=True)
                pool.tensor_tensor(dd[:, par, 1, :], dd[:, par, 0, :], u_of(k, b, c), ALU.mult).then_inc(s_du, 1)

            def part_lo(m, par):
                pool.wait_ge(s_mid, m + 1)
                pool.tensor_tensor(parts[:, par, 2], dd[:, par], parts[:, par, 1], ALU.subtract).then_inc(s_lo, 1)

            def times_c(n, g, par):
                if g == 0:
                    pool.wait_ge(s_bccp, 2 * n + 2 + BCCP0)
                pool.wait_ge(s_h, G * n + g + 1 + H0)
                pool.wait_ge(s_ymm, G * n + g + 1 - HCS + YMM0)
                pool.tensor_tensor(hc[:, g % HCS, :], h[:, g, :], c_rep[:, par, :], ALU.mult).then_inc(s_hc, 1)

            def image_start(b):
                m = b * STEPS
                pool.wait_ge(s_xt, b + 1)
                delta_u(m, b, 0, 0, 0)
                part_lo(m, 0)

            def step(b, n, k, c, par, n1, n2):
                for g in range(G):
                    if n1 and g == 0:
                        delta_u(n + 1, b, *n1, 1 - par)
                    times_c(n, g, par)
                    if n1 and g == 5:
                        part_lo(n + 1, 1 - par)

            all_steps(pool, image_start, step, lambda b: None)

        @block.vector
        def _(dve):
            dve.wait_ge(s_setup, K)
            dve.tensor_copy(w_dt[:].rearrange("c k d -> c (k d)"), p_dt[:, 0:K * C]).then_inc(s_setup_cp, 1)
            dve.wait_ge(s_w, 16 * len(weights))
            dve.tensor_copy(pick[:], pick_f[:]).then_inc(s_setup_cp, 1)
            dve.tensor_reduce(d_sum[:], cols[:, K:2 * K], AX_X, ALU.add).then_inc(s_setup_cp, 1)
            dve.wait_ge(s_a, 1)
            dve.tensor_scalar(a_neg[:], a_neg[:], -1.0, None, ALU.mult).then_inc(s_a, 1)
            dve.wait_ge(s_setup_cp, 3)
            for s, credit in ((s_delta, DELTA0), (s_bu, BU0), (s_h, H0), (s_y, Y0)):
                dve.sem_inc(s, credit)

            def series_and_mask(m):
                dve.wait_ge(s_factor, m + 1)
                dve.tensor_tensor(series[:], series[:], e_x[:], ALU.mult).then_inc(s_series, 1)
                dve.tensor_scalar(small[:], e_x[:], SMALL_E, None, ALU.is_lt).then_inc(s_series, 1)

            def take_small(m):
                dve.wait_ge(s_sp, m + 1)
                dve.nop(nofuse=True)
                dve.wait_ge(s_series, 2 * m + 2)
                dve.nop(nofuse=True)
                dve.copy_predicated(log_e[:], small[:], series[:]).then_inc(s_logp, 1)

            def delta(m, par):
                dve.wait_ge(s_logp, m + 1)
                dve.wait_ge(s_lo, m - 1 + LO0)
                dve.tensor_tensor(dd[:, par, 0, :], dx_pos[:], log_e[:], ALU.add).then_inc(s_delta, 1)

            def rest(m, par):
                dve.wait_ge(s_hi, m + 1)
                dve.tensor_tensor(dd[:, par], dd[:, par], parts[:, par, 0], ALU.subtract).then_inc(s_rest, 1)

            def times_b(n, g, par):
                if g == 0:
                    dve.wait_ge(s_bccp, 2 * n + 1 + BCCP0)
                dve.wait_ge(s_rep, G * n + g + 1 + REP0)
                dve.wait_ge(s_h, G * n + g + 1 - DAS + H0)
                dve.tensor_tensor(bu[:, g % DAS, :], p_du[g % 2][:], b_rep[:, par, :], ALU.mult).then_inc(s_bu, 1)

            def scan(n, k, c, g, par):
                backward = k >= 2
                way = slice(None, None, -1) if backward else slice(None)
                first = 0 if backward else N - 1
                dve.wait_ge(s_da, G * n + g + 1 + DA0)
                dve.wait_ge(s_hc, G * (n - 1) + g + 1 + HC0)
                dve.wait_ge(s_bu, G * n + g + 1 + BU0)
                state = 0.0 if isinstance(c, int) and c == 0 else h[:, g, first:first + 1]
                dve.tensor_tensor_scan(h[:, g, way], da[:, g % DAS, way], bu[:, g % DAS, way],
                                       state, ALU.mult, ALU.add).then_inc(s_h, 1)

            def add_y(n, k, c, par):
                at = chunk_of(k, c)
                dve.wait_ge(s_ymm, G * n + G + YMM0)
                dve.nop(nofuse=True)
                if k == 0:
                    dve.tensor_copy(y_sum[:, bass.ds(at * N, N)], p_y[par][:]).then_inc(s_y, 1)
                elif k == 2:
                    piece = y_sum[:, bass.ds(at * N, N)]
                    dve.tensor_tensor(piece, piece, p_y[par][:], ALU.add).then_inc(s_y, 1)
                else:
                    piece = y_sum[:].rearrange("c (y x) -> c x y", x=W)[:, bass.ds(at * COLS, COLS), :]
                    dve.tensor_tensor(piece, piece, p_y[par][:].rearrange("c (x y) -> c x y", y=H), ALU.add).then_inc(s_y, 1)

            def image_start(b):
                m = b * STEPS
                series_and_mask(m)
                take_small(m)
                delta(m, 0)
                rest(m, 0)
                series_and_mask(m + 1)
                take_small(m + 1)
                delta(m + 1, 1)
                times_b(m, 0, 0)

            def step(b, n, k, c, par, n1, n2):
                for g in range(G):
                    if g < G - 1:
                        times_b(n, g + 1, par)
                    elif n1:
                        times_b(n + 1, 0, 1 - par)
                    scan(n, k, c, g, par)
                    if n1 and g == 2:
                        rest(n + 1, 1 - par)
                    if n2 and g == 5:
                        series_and_mask(n + 2)
                    if g == 9 and ahead(k, c, -1):
                        add_y(n - 1, *ahead(k, c, -1), 1 - par)
                    if n2 and g == 7:
                        take_small(n + 2)
                    if n2 and g == 8:
                        delta(n + 2, par)

            def image_end(b):
                add_y(b * STEPS + (STEPS - 1), K - 1, CHUNKS - 1, 1)
                dve.wait_ge(s_y, b * STEPS + STEPS + Y0)
                dve.nop(nofuse=True)
                image = X[:, bass.ds(b * HW, HW)]
                dve.scalar_tensor_tensor(image, image, d_sum[:], y_sum[:], ALU.mult, ALU.add)

            all_steps(dve, image_start, step, image_end)


def channel_norm_out(nc, w, X, out):
    LT = 2 * N
    LTILES = T // LT
    with ExitStack() as ctx:
        sb = lambda name, shape, dt=F32: ctx.enter_context(nc.sbuf_tensor(name, shape, dt))
        ps = lambda name, shape: ctx.enter_context(nc.psum_tensor(name, shape, F32))
        sem = lambda name: ctx.enter_context(nc.semaphore(name))
        center = sb("l3n_center", [C, C])
        mean_w = sb("l3n_mean_w", [C, C])
        cols = sb("l3n_cols", [C, 2])
        eps = sb("l3n_eps", [C, 2])
        xsq = sb("l3n_xsq", [C, 2, LT])
        rstd = sb("l3n_rstd", [C, 2, LT])
        xhat = sb("l3n_xhat", [C, 2, LT])
        result = sb("l3n_result", [C, 2, LT])
        p_xc = [ps(f"l3n_xc{i}", [C, LT]) for i in range(2)]
        p_var = [ps(f"l3n_var{i}", [C, LT]) for i in range(2)]
        s_w, s_const, s_xc, s_xsq, s_var, s_lnv, s_rstd, s_xhat, s_res = (sem("l3n_" + n) for n in (
            "weights", "constants", "xc", "xsq", "var", "lnvar", "rstd", "xhat", "result"))
        s_store = [sem(f"l3n_stored{i}") for i in range(2)]
        block = ctx.enter_context(nc.Block())

        @block.sync
        def _(sp):
            for dst, src in ((center, "center"), (mean_w, "mean_w"), (cols, "cols_out")):
                sp.dma_start(dst[:], w[src]).then_inc(s_w, 16)
            with sp.Fori(0, B) as b:
                with sp.Fori(0, HW // LT // 2) as i:
                    for par in range(2):
                        t = b * (HW // LT) + 2 * i + par
                        sp.wait_ge(s_res, t + 1)
                        sp.nop(nofuse=True)
                        sp.dma_start(out[bass.ds(b, 1), :, bass.ds(i * (2 * LT) + par * LT, LT)].rearrange("b c t -> (b c) t"),
                                     result[:, par, :]).then_inc(s_store[par], 16)
            for par in range(2):
                sp.wait_ge(s_store[par], 16 * (LTILES // 2))

        @block.tensor
        def _(pe):
            def center_tile(t, par, first=False):
                if not first:
                    pe.wait_ge(s_xhat, t - 1)
                    pe.nop(nofuse=True)
                for j in range(2):
                    mm = pe.matmul(p_xc[par][:, j * N:(j + 1) * N], center[:],
                                   X[:, bass.ds(t * LT + j * N, N)], start=True, stop=True)
                mm.then_inc(s_xc, 1)

            def var_tile(t, par):
                pe.wait_ge(s_xsq, t + 1)
                for j in range(2):
                    mm = pe.matmul(p_var[par][:, j * N:(j + 1) * N], mean_w[:],
                                   xsq[:, par, j * N:(j + 1) * N], start=True, stop=True)
                mm.then_inc(s_var, 1)

            pe.wait_ge(s_w, 16 * 3)
            center_tile(0, 0, first=True)
            center_tile(1, 1, first=True)
            var_tile(0, 0)
            with pe.Fori(0, LTILES // 2 - 1) as i:
                center_tile(2 * i + 2, 0)
                var_tile(2 * i + 1, 1)
                center_tile(2 * i + 3, 1)
                var_tile(2 * i + 2, 0)
            var_tile(LTILES - 1, 1)

        @block.scalar
        def _(act):
            def square_tile(t, par):
                act.wait_ge(s_xc, t + 1)
                act.activation(xsq[:, par, :], p_xc[par][:], ACT.Square).then_inc(s_xsq, 1)

            def rstd_tile(t, par, first=False):
                act.wait_ge(s_var, t + 1)
                if not first:
                    act.wait_ge(s_xhat, t - 1)
                act.activation(rstd[:, par, :], p_var[par][:], ACT.Ln, bias=eps[:, 0:1], scale=WIDE_VAR_SCALE).then_inc(s_lnv, 1)
                act.wait_ge(s_lnv, t + 1)
                act.activation(rstd[:, par, :], rstd[:, par, :], ACT.Exp, bias=eps[:, 1:2], scale=-0.5).then_inc(s_rstd, 1)

            act.preload_act_table_set(LN_EXP)
            act.wait_ge(s_const, 1)
            square_tile(0, 0)
            square_tile(1, 1)
            rstd_tile(0, 0, first=True)
            square_tile(2, 0)
            rstd_tile(1, 1, first=True)
            with act.Fori(0, LTILES // 2 - 2) as i:
                square_tile(2 * i + 3, 1)
                rstd_tile(2 * i + 2, 0)
                square_tile(2 * i + 4, 0)
                rstd_tile(2 * i + 3, 1)
            square_tile(LTILES - 1, 1)
            rstd_tile(LTILES - 2, 0)
            rstd_tile(LTILES - 1, 1)

        @block.vector
        def _(dve):
            def out_tile(t, par, first=False):
                dve.wait_ge(s_rstd, t + 1)
                dve.tensor_tensor(xhat[:, par, :], p_xc[par][:], rstd[:, par, :], ALU.mult).then_inc(s_xhat, 1)
                dve.wait_ge(s_xhat, t + 1)
                if not first:
                    dve.wait_ge(s_store[par], 8 * (t - par))
                dve.tensor_scalar(result[:, par, :], xhat[:, par, :], cols[:, 0:1], cols[:, 1:2],
                                  ALU.mult, ALU.add).then_inc(s_res, 1)

            dve.memset(eps[:, 1:2], 0.5 * float(np.log(WIDE_VAR_SCALE)))
            dve.memset(eps[:, 0:1], EPS * WIDE_VAR_SCALE).then_inc(s_const, 1)
            dve.wait_ge(s_w, 16 * 3)
            out_tile(0, 0, first=True)
            out_tile(1, 1, first=True)
            with dve.Fori(1, LTILES // 2) as i:
                out_tile(2 * i, 0)
                out_tile(2 * i + 1, 1)


def selective_scan_layout(w):
    g = {n[len("L3_conv_"):]: a for n, a in w.items() if n.startswith("L3_conv_")}
    K, S, R, DL, Q = 4, 16, 6, 8, 32
    G = C // DL
    xp = g["x_proj_weight"]
    bc = xp[:, R:].reshape(K, 2, S, 1, C)
    pick = np.zeros((C // Q, Q, Q // DL, S, DL), np.float32)
    for j in range(Q // DL):
        for dl in range(DL):
            pick[:, j * DL + dl, j, :, dl] = 1
    y_pick = np.zeros((S, DL, G, C), np.float32)
    for grp in range(G):
        for dl in range(DL):
            y_pick[:, dl, grp, grp * DL + dl] = 1
    return {
        "xp_dt": xp[:, :R].transpose(1, 0, 2),
        "dt_w_T": g["dt_projs_weight"].transpose(2, 0, 1),
        "w_rep": np.broadcast_to(bc, (K, 2, S, DL, C)).reshape(K, 2, S * DL, C).transpose(3, 0, 1, 2),
        "pick": pick.reshape(C, Q // DL, S * DL),
        "y_pick": y_pick.reshape(S * DL, G, C),
        "a_logs": g["A_logs"].reshape(K, G, DL, S).transpose(3, 2, 0, 1).reshape(S * DL, K * G),
        "cols": np.concatenate([g["dt_projs_bias"].T, g["Ds"].reshape(K, C).T], 1),
        "center": np.eye(C, dtype=np.float32) - np.float32(1 / C),
        "mean_w": np.full((C, C), 1 / C, np.float32),
        "cols_out": np.stack([g["ln_g"].reshape(C), g["ln_b"].reshape(C)], 1),
    }


LAYOUTS = {"L0": gated_ssm_layout, "L1": sedenion_layout, "L2": local_attention_layout, "L3": selective_scan_layout}


def build(nc, x, w, out):
    qkv_d = nc.dram_tensor("qkv_scratch", (3 * C, B, HP * WP), F32, kind="Internal").ap()
    o_d = nc.dram_tensor("o_scratch", (C, T), F32, kind="Internal").ap()
    x_d = nc.dram_tensor("x_scratch", (C, T), F32, kind="Internal").ap()
    with ExitStack() as ctx:
        X = ctx.enter_context(nc.sbuf_tensor("x_front", [C, T], F32))
        gated_ssm_block(nc, x, w["L0"], X)
        sedenion_block(nc, w["L1"], X)
        attention_qkv(nc, w["L2"], X, qkv_d, x_d)
    attention_heads(nc, w["L2"], qkv_d, o_d)
    with ExitStack() as ctx:
        X = ctx.enter_context(nc.sbuf_tensor("x_back", [C, T], F32))
        attention_out(nc, w["L2"], X, o_d, x_d)
        selective_scan(nc, w["L3"], X)
        channel_norm_out(nc, w["L3"], X, out)


def kernel(**inputs):
    import concourse.bacc as _bacc
    from concourse.bass_utils import run_bass_kernel_spmd as _run

    inputs = {name: np.asarray(a) for name, a in inputs.items()}
    nc = _bacc.Bacc("TRN2", target_bir_lowering=False, num_devices=1)
    arrays = {}

    def given(name, a):
        arrays[name] = np.ascontiguousarray(a)
        return nc.dram_tensor(name, a.shape, mybir.dt.from_np(a.dtype), kind="ExternalInput").ap()

    x = given("x", inputs["x"].reshape(B, C, HW))
    weights = {block: {n: given(f"{block}_{n}", a) for n, a in layout(inputs).items()}
               for block, layout in LAYOUTS.items()}
    out = nc.dram_tensor("out", (B, C, HW), F32, kind="ExternalOutput").ap()
    build(nc, x, weights, out)
    r = _run(nc, [arrays], core_ids=[0])
    return r.results[0]["out"].reshape(B, C, H, W)
```

```python
from contextlib import ExitStack

import numpy as np

import concourse.bass as bass
from concourse import mybir

ALU = mybir.AluOpType
ACT = mybir.ActivationFunctionType
AX_X = mybir.AxisListType.X
F32 = mybir.dt.float32
F32R = mybir.dt.float32r
HL = ("high", "low")
LN_EXP = "natural_log_exp_and_others"

B, C, H, W = 4, 96, 64, 64
HW = H * W
T = B * HW
N = 512
TILES = T // N
EPS = 1e-5
VAR_SCALE = 2.0 ** -12
WIDE_VAR_SCALE = 2.0 ** -46


def gated_ssm_block(nc, x, w, X):
    K, S, R = 4, 8, 8
    with ExitStack() as ctx:
        sb = lambda name, shape, dt=F32: ctx.enter_context(nc.sbuf_tensor(name, shape, dt))
        ps = lambda name, shape: ctx.enter_context(nc.psum_tensor(name, shape, F32))
        sem = lambda name: ctx.enter_context(nc.semaphore(name))

        center = sb("l0_center", [C, C])
        mean_w = sb("l0_mean_w", [C, C])
        w_in1 = sb("l0_w_in1", [C, C])
        ssm_in = sb("l0_ssm_in", [C, 2 * C])
        w_u = sb("l0_w_u", [C, 2 * C])
        w_g = sb("l0_w_g", [C, C])
        w_bc = sb("l0_w_bc", [C, 2, K * S])
        xp_dt = sb("l0_xp_dt", [R, K, C])
        dt_w = sb("l0_dt_w", [R, K, C])
        w_dt = sb("l0_w_dt", [C, K, C])
        pick = sb("l0_pick", [K * S, K, C])
        w_so = sb("l0_w_so", [C, C])
        w_o = sb("l0_w_o", [C, C])
        cols = sb("l0_cols", [C, 12])
        d_sum = sb("l0_d_sum", [C, 1])
        eps = sb("l0_eps", [C, 2])

        KEEP = 4
        xsq = sb("l0_xsq", [C, N])
        rstd = sb("l0_rstd", [C, N])
        xn = sb("l0_xn", [C, N])
        xss = sb("l0_xss", [C, KEEP, N])
        z = sb("l0_z", [C, KEEP, N])
        sg = sb("l0_sg", [C, KEEP, N])
        bs = sb("l0_bs", [2 * K * S, N])
        bcp = sb("l0_bcp", [K * S, 2, N])
        dx = sb("l0_dx", [C, K, N])
        sp = sb("l0_sp", [C, K, N])
        dt = sb("l0_dt", [C, 2, K, N])
        gain = sb("l0_gain", [C, K, N])
        y = sb("l0_y", [C, N])
        ysq = sb("l0_ysq", [C, N])
        yrstd = sb("l0_yrstd", [C, N])
        yn = sb("l0_yn", [C, N])
        sgated = sb("l0_sgated", [C, N])

        p_xc, p_var, p_u = ps("l0_p0", [C, N]), ps("l0_p1", [C, N]), ps("l0_p2", [C, N])
        p_z, p_g = p_xc, p_var
        p_b_c = ps("l0_p3", [2 * K * S, N])
        p_dt = [ps("l0_p4", [C, N]), ps("l0_p5", [C, N])]
        p_bc = [ps("l0_p6", [C, N]), ps("l0_p7", [C, N])]
        p_yc, p_yvar, p_s, p_o = p_bc[0], p_bc[1], p_bc[0], p_bc[1]

        s_w, s_x = sem("l0_weights"), sem("l0_x_loaded")
        s_setup, s_setup_cp, s_const = sem("l0_setup_mm"), sem("l0_setup_copied"), sem("l0_constants")
        s_xc, s_xsq, s_var, s_lnv, s_rstd, s_xn0, s_xn = (sem("l0_" + n) for n in (
            "xc", "xsq", "var", "lnvar", "rstd", "xn_plain", "xn"))
        s_zg, s_silu = sem("l0_projections"), sem("l0_silu")
        s_bcm, s_bs, s_bcp, s_dtm, s_dx, s_abs, s_exp, s_sp, s_dt, s_bc, s_gain = (sem("l0_" + n) for n in (
            "b_and_c", "b_copied", "bc_product", "dt_mm", "dx", "dt_abs", "dt_exp", "softplus_log", "dt",
            "bc_mm", "gain"))
        s_dsum = sem("l0_gain_sums")
        s_y, s_yc, s_ysq, s_yvar, s_ylnv, s_yrstd, s_yn, s_s, s_sgated, s_o, s_out = (sem("l0_" + n) for n in (
            "y", "yc", "ysq", "yvar", "ylnvar", "yrstd", "yn", "s", "s_gated", "o", "x_written"))
        SILU0, BCP0, DX0, DT0, Y0, OUT0 = 1, 1, 2, 2, 1, KEEP
        block = ctx.enter_context(nc.Block())

        def all_tiles(eng, step):
            step(-2, 2, 0, True, False, False)
            step(-1, 3, 1, True, True, False)
            with eng.Fori(0, TILES // KEEP - 1) as i:
                for q in range(KEEP):
                    step(KEEP * i + q, q, q % 2, True, True, True)
            for q in range(KEEP):
                step(TILES - KEEP + q, q, q % 2, q < KEEP - 2, q < KEEP - 1, True)

        weights = [(center[:], w["center"]), (mean_w[:], w["mean_w"]), (w_in1[:], w["w_in1"]),
                   (ssm_in[:], w["ssm_in_T"]), (w_g[:], w["w_g_T"]), (w_bc[:], w["w_bc_T"]),
                   (xp_dt[:], w["xp_dt"]), (dt_w[:], w["dt_w_T"]), (pick[:], w["pick"]),
                   (w_so[:], w["ssm_out_T"]), (w_o[:], w["w_out_T"]), (cols[:], w["cols"])]

        @block.sync
        def _(sp_):
            for dst, src in weights:
                sp_.dma_start(dst, src).then_inc(s_w, 16)
            for b in range(B):
                sp_.dma_start(X[:, b * HW:(b + 1) * HW], x[b]).then_inc(s_x, 16)

        @block.tensor
        def _(pe):
            pe.wait_ge(s_w, 16 * len(weights))
            pe.matmul(p_xc[:, 0:2 * C], w_in1[:], ssm_in[:], start=True, stop=True).then_inc(s_setup, 1)
            for k in range(K):
                pe.matmul(p_var[:, k * C:(k + 1) * C], xp_dt[:, k, :], dt_w[:, k, :],
                          start=True, stop=True).then_inc(s_setup, 1)
            pe.wait_ge(s_setup_cp, 2)

            def ln_a(m):
                pe.wait_ge(s_silu, 3 * m + SILU0)
                pe.nop(nofuse=True)
                pe.matmul(p_xc[:], center[:], X[:, bass.ds(m * N, N)], start=True, stop=True).then_inc(s_xc, 1)

            def var_a(m):
                pe.wait_ge(s_xsq, m + 1)
                pe.matmul(p_var[:], mean_w[:], xsq[:], start=True, stop=True).then_inc(s_var, 1)

            def proj_a(m):
                pe.wait_ge(s_xn, m + 1)
                pe.matmul(p_u[:], w_u[:, 0:C], xn[:], start=True, stop=True)
                pe.matmul(p_z[:], w_u[:, C:2 * C], xn[:], start=True, stop=True)
                pe.matmul(p_g[:], w_g[:], xn[:], start=True, stop=True).then_inc(s_zg, 1)

            def bc_d(m, q):
                pe.wait_ge(s_silu, 3 * m + 1 + SILU0)
                pe.wait_ge(s_bcp, m + BCP0)
                pe.matmul(p_b_c[:], w_bc[:].rearrange("c j r -> c (j r)"), xss[:, q, :],
                          start=True, stop=True).then_inc(s_bcm, 1)

            def dt_d(m, q, k):
                pe.wait_ge(s_dx, K * m + k - 1 + DX0)
                pe.matmul(p_dt[k % 2][:], w_dt[:, k, :], xss[:, q, :], start=True, stop=True).then_inc(s_dtm, 1)

            def gains_g(t, par, k):
                if k == 0:
                    pe.wait_ge(s_bcp, t + 1 + BCP0)
                    pe.wait_ge(s_out, t + OUT0)
                if k >= 2:
                    pe.wait_ge(s_gain, K * t + k - 1)
                pe.matmul(p_bc[k % 2][:], pick[:, k, :], bcp[:, par, :], start=True, stop=True).then_inc(s_bc, 1)

            def step(t, q, par, a, d, g):
                q1 = (q + 1) % KEEP
                if g:
                    gains_g(t, par, 0)
                    gains_g(t, par, 1)
                if a:
                    ln_a(t + 2)
                if d:
                    bc_d(t + 1, q1)
                    dt_d(t + 1, q1, 0)
                    dt_d(t + 1, q1, 1)
                if g:
                    gains_g(t, par, 2)
                    gains_g(t, par, 3)
                if a:
                    var_a(t + 2)
                if d:
                    dt_d(t + 1, q1, 2)
                    dt_d(t + 1, q1, 3)
                if g:
                    pe.wait_ge(s_y, t + 1 + Y0)
                    pe.matmul(p_yc[:], center[:], y[:], start=True, stop=True).then_inc(s_yc, 1)
                if a:
                    proj_a(t + 2)
                if g:
                    pe.wait_ge(s_ysq, t + 1)
                    pe.matmul(p_yvar[:], mean_w[:], ysq[:], start=True, stop=True).then_inc(s_yvar, 1)
                    pe.wait_ge(s_yn, 3 * t + 3)
                    pe.matmul(p_s[:], w_so[:], yn[:], start=True, stop=True).then_inc(s_s, 1)
                    pe.wait_ge(s_sgated, t + 1)
                    pe.matmul(p_o[:], w_o[:], sgated[:], start=True, stop=True).then_inc(s_o, 1)

            pe.wait_ge(s_x, 16 * B)
            all_tiles(pe, step)

        @block.scalar
        def _(act):
            act.wait_ge(s_const, 1)
            act.sem_inc(s_silu, SILU0)

            def square_a(m):
                act.wait_ge(s_xc, m + 1)
                act.activation(xsq[:], p_xc[:], ACT.Square).then_inc(s_xsq, 1)

            def rstd_a(m):
                act.wait_ge(s_var, m + 1)
                act.activation(rstd[:], p_var[:], ACT.Ln, bias=eps[:, 0:1], scale=VAR_SCALE).then_inc(s_lnv, 1)
                act.wait_ge(s_lnv, m + 1)
                act.activation(rstd[:], rstd[:], ACT.Exp, bias=eps[:, 1:2], scale=-0.5).then_inc(s_rstd, 1)

            def silu_a(m, q):
                act.wait_ge(s_zg, m + 1)
                act.wait_ge(s_out, m + 1 - KEEP + OUT0)
                act.activation(xss[:, q, :], p_u[:], ACT.Silu).then_inc(s_silu, 1)
                act.activation(z[:, q, :], p_z[:], ACT.Silu).then_inc(s_silu, 1)
                act.activation(sg[:, q, :], p_g[:], ACT.Silu).then_inc(s_silu, 1)

            def b_copy_d(m):
                act.wait_ge(s_bcm, m + 1)
                act.activation(bs[K * S:2 * K * S, :], p_b_c[0:K * S, :], ACT.Copy).then_inc(s_bs, 1)

            def half_of(a, half):
                return a[:, 2 * half:2 * half + 2, :]

            def abs_d(m, half):
                act.wait_ge(s_dx, K * m + 2 * half + 2 + DX0)
                act.wait_ge(s_dt, 2 * m + half - 1 + DT0)
                act.activation(half_of(sp, half), half_of(dx, half), ACT.Abs).then_inc(s_abs, 1)

            def exp_d(m, half):
                act.wait_ge(s_abs, 2 * m + half + 1)
                act.activation(half_of(sp, half), half_of(sp, half), ACT.Exp, scale=-1.0).then_inc(s_exp, 1)

            def ln_d(m, half):
                act.wait_ge(s_exp, 2 * m + half + 1)
                act.activation(half_of(sp, half), half_of(sp, half), ACT.Ln, bias=1.0).then_inc(s_sp, 1)

            def step(t, q, par, a, d, g):
                act.preload_act_table_set(LN_EXP)
                if a:
                    square_a(t + 2)
                if d:
                    b_copy_d(t + 1)
                    abs_d(t + 1, 0)
                    exp_d(t + 1, 0)
                if a:
                    rstd_a(t + 2)
                if d:
                    ln_d(t + 1, 0)
                if g:
                    act.wait_ge(s_yc, t + 1)
                    act.activation(ysq[:], p_yc[:], ACT.Square).then_inc(s_ysq, 1)
                if d:
                    abs_d(t + 1, 1)
                    exp_d(t + 1, 1)
                if g:
                    act.wait_ge(s_yvar, t + 1)
                    act.activation(yrstd[:], p_yvar[:], ACT.Ln, bias=eps[:, 0:1], scale=VAR_SCALE).then_inc(s_ylnv, 1)
                    act.wait_ge(s_ylnv, t + 1)
                    act.activation(yrstd[:], yrstd[:], ACT.Exp, bias=eps[:, 1:2], scale=-0.5).then_inc(s_yrstd, 1)
                if d:
                    ln_d(t + 1, 1)
                if a:
                    silu_a(t + 2, (q + 2) % KEEP)

            all_tiles(act, step)

        @block.vector
        def _(dve):
            for s, credit in ((s_bcp, BCP0), (s_dx, DX0), (s_dt, DT0), (s_y, Y0), (s_out, OUT0)):
                dve.sem_inc(s, credit)
            dve.memset(eps[:, 1:2], 0.5 * float(np.log(VAR_SCALE)))
            dve.memset(eps[:, 0:1], EPS * VAR_SCALE).then_inc(s_const, 1)
            dve.wait_ge(s_setup, 1)
            dve.tensor_copy(w_u[:], p_xc[:, 0:2 * C]).then_inc(s_setup_cp, 1)
            dve.wait_ge(s_setup, 1 + K)
            dve.tensor_copy(w_dt[:].rearrange("p k c -> p (k c)"), p_var[:, 0:K * C]).then_inc(s_setup_cp, 1)
            dve.wait_ge(s_w, 16 * len(weights))
            dve.tensor_reduce(d_sum[:], cols[:, 8:12], AX_X, ALU.add).then_inc(s_setup_cp, 1)
            dve.wait_ge(s_setup_cp, 3)

            def xn_a(m):
                dve.wait_ge(s_rstd, m + 1)
                dve.tensor_tensor(xn[:], p_xc[:], rstd[:], ALU.mult).then_inc(s_xn0, 1)
                dve.wait_ge(s_xn0, m + 1)
                dve.tensor_scalar(xn[:], xn[:], cols[:, 0:1], cols[:, 1:2], ALU.mult, ALU.add).then_inc(s_xn, 1)

            def bc_product_d(m, par):
                dve.wait_ge(s_bs, m + 1)
                dve.tensor_tensor(bcp[:, par, :], bs[K * S:2 * K * S, :], p_b_c[K * S:2 * K * S, :], ALU.mult).then_inc(s_bcp, 1)

            def dx_d(m, k):
                if k == 0:
                    dve.wait_ge(s_dt, 2 * m + DT0)
                dve.wait_ge(s_dtm, K * m + k + 1)
                dve.tensor_scalar(dx[:, k, :], p_dt[k % 2][:], cols[:, 4 + k:5 + k], None, ALU.add).then_inc(s_dx, 1)

            def dt_d(m, par, half):
                dve.wait_ge(s_sp, 2 * m + half + 1)
                ks = slice(2 * half, 2 * half + 2)
                dve.scalar_tensor_tensor(dt[:, par, ks, :], dx[:, ks, :], 0.0, sp[:, ks, :], ALU.max, ALU.add).then_inc(s_dt, 1)

            def gain_g(t, par, k):
                if k == 0:
                    dve.wait_ge(s_dt, 2 * t + 2 + DT0)
                    dve.wait_ge(s_y, t + Y0)
                dve.wait_ge(s_bc, K * t + k + 1)
                dve.tensor_tensor(gain[:, k, :], dt[:, par, k, :], p_bc[k % 2][:], ALU.mult).then_inc(s_gain, 1)

            def y_g(t, q, par):
                dve.wait_ge(s_gain, K * t + 4)
                dve.tensor_tensor(dt[:, par, 0:2, :], gain[:, 0:2, :], gain[:, 2:4, :], ALU.add).then_inc(s_dsum, 1)
                dve.wait_ge(s_dsum, 2 * t + 1)
                dve.tensor_tensor(gain[:, 0, :], dt[:, par, 0, :], dt[:, par, 1, :], ALU.add).then_inc(s_dsum, 1)
                dve.wait_ge(s_dsum, 2 * t + 2)
                dve.scalar_tensor_tensor(y[:], gain[:, 0, :], d_sum[:], xss[:, q, :], ALU.add, ALU.mult).then_inc(s_y, 1)

            def gate_g(t, q):
                dve.wait_ge(s_yrstd, t + 1)
                dve.tensor_tensor(yn[:], p_yc[:], yrstd[:], ALU.mult).then_inc(s_yn, 1)
                dve.wait_ge(s_yn, 3 * t + 1)
                dve.tensor_scalar(yn[:], yn[:], cols[:, 2:3], cols[:, 3:4], ALU.mult, ALU.add).then_inc(s_yn, 1)
                dve.wait_ge(s_yn, 3 * t + 2)
                dve.wait_ge(s_silu, 3 * t + 3 + SILU0)
                dve.tensor_tensor(yn[:], yn[:], z[:, q, :], ALU.mult).then_inc(s_yn, 1)

            def out_g(t, q):
                dve.wait_ge(s_s, t + 1)
                dve.tensor_tensor(sgated[:], p_s[:], sg[:, q, :], ALU.mult).then_inc(s_sgated, 1)
                dve.wait_ge(s_o, t + 1)
                dve.tensor_tensor(X[:, bass.ds(t * N, N)], p_o[:], X[:, bass.ds(t * N, N)], ALU.add).then_inc(s_out, 1)

            def step(t, q, par, a, d, g):
                if g:
                    gain_g(t, par, 0)
                    gain_g(t, par, 1)
                if d:
                    dx_d(t + 1, 0)
                    dx_d(t + 1, 1)
                if g:
                    gain_g(t, par, 2)
                    gain_g(t, par, 3)
                    y_g(t, q, par)
                if d:
                    dx_d(t + 1, 2)
                    dx_d(t + 1, 3)
                if a:
                    xn_a(t + 2)
                if d:
                    bc_product_d(t + 1, 1 - par)
                    dt_d(t + 1, 1 - par, 0)
                if g:
                    gate_g(t, q)
                if d:
                    dt_d(t + 1, 1 - par, 1)
                if g:
                    out_g(t, q)

            all_tiles(dve, step)


def gated_ssm_layout(w):
    K, S, R = 4, 8, 8
    xp = w["L0_conv_x_proj_w"]
    per_direction = lambda a: np.reshape(a, (K, C)).T
    return {
        "center": np.eye(C, dtype=np.float32) - np.float32(1 / C),
        "mean_w": np.full((C, C), 1 / C, np.float32),
        "w_in1": w["L0_conv_w_in"][:C],
        "ssm_in_T": w["L0_conv_ssm_in_w"].T,
        "w_g_T": w["L0_conv_w_in"][C:].T,
        "w_bc_T": np.stack([xp[:, R + j * S:R + (j + 1) * S].reshape(K * S, C).T for j in range(2)], 1),
        "xp_dt": xp[:, :R].transpose(1, 0, 2),
        "dt_w_T": w["L0_conv_dt_w"].transpose(2, 0, 1),
        "pick": np.repeat(np.repeat(np.eye(K, dtype=np.float32), S, 0)[:, :, None], C, 2),
        "ssm_out_T": w["L0_conv_ssm_out_w"].T,
        "w_out_T": w["L0_conv_w_out"].T,
        "cols": np.concatenate([w["L0_conv_norm_w"][:, None], w["L0_conv_norm_b"][:, None],
                                w["L0_conv_out_norm_w"][:, None], w["L0_conv_out_norm_b"][:, None],
                                per_direction(w["L0_conv_dt_b"]), per_direction(w["L0_conv_Ds"])], 1),
    }


def sedenion_signs():
    def conj(a):
        if len(a) == 1:
            return a
        h = len(a) // 2
        return np.concatenate([conj(a[:h]), -a[h:]])

    def mult(a, b):
        if len(a) == 1:
            return a * b
        h = len(a) // 2
        a1, a2, b1, b2 = a[:h], a[h:], b[:h], b[h:]
        return np.concatenate([mult(a1, b1) - mult(conj(b2), a2), mult(b2, a1) + mult(a2, conj(b1))])

    eye = np.eye(16, dtype=np.float32)
    return [[int(mult(eye[i], eye[i ^ k])[k]) for k in range(16)] for i in range(16)]


def sedenion_block(nc, w, X):
    P = 16
    HALVES = T // P // N
    HT = TILES // HALVES
    DEPTH = 4
    F = 4 * C
    FB = F // 128
    SIGNS = sedenion_signs()
    with ExitStack() as ctx:
        sb = lambda name, shape, dt=F32: ctx.enter_context(nc.sbuf_tensor(name, shape, dt))
        sem = lambda name: ctx.enter_context(nc.semaphore(name))

        xn = [sb(f"l1_xn_{part}", [C, P, N], F32R) for part in HL]
        w_pos = [sb(f"l1_w_pos_{part}", [C, P, C], F32R) for part in HL]
        w_neg = [sb(f"l1_w_neg_{part}", [C, P, C], F32R) for part in HL]
        w_fc1 = [sb(f"l1_w_fc1_{part}", [C, F], F32R) for part in HL]
        w_fc2 = [sb(f"l1_w_fc2_{part}", [128, FB, C], F32R) for part in HL]
        center = sb("l1_center", [C, C])
        mean_w = sb("l1_mean_w", [C, C])
        w_proj = sb("l1_w_proj", [C, C])
        cols = sb("l1_cols", [C, 6])
        fc1_b = sb("l1_fc1_b", [128, FB])
        eps = sb("l1_eps", [C, 2])
        s_w, s_const = sem("l1_weights"), sem("l1_constants")

        a_sems = [sem("l1a_" + n) for n in ("xc", "xsq", "var", "lnvar", "rstd", "xhat", "normed", "xn_high", "xn_low",
                                            "weights_high")]
        b_sems = [sem("l1b_" + n) for n in ("y", "gelu_y", "projected", "x1_written", "xc", "xsq", "var", "lnvar",
                                            "rstd", "xhat", "h_in", "fc1", "gelu_h", "fc2", "x_written",
                                            "h_in_high", "h_in_low", "h_high", "h_low")]

        for half in range(HALVES):
            with ExitStack() as part:
                sb = lambda name, shape, dt=F32: part.enter_context(nc.sbuf_tensor(name, shape, dt))
                ps = lambda name, shape: part.enter_context(nc.psum_tensor(name, shape, F32))
                if half == 0:
                    w_sed = sb("l1a_w_sed", [C, P, C])
                    fc1 = sb("l1a_fc1", [C, F])
                    fc2 = sb("l1a_fc2", [128, FB, C])
                    weights = [(center[:], w["center"]), (mean_w[:], w["mean_w"]), (cols[:], w["cols"]),
                               (w_sed[:], w["w_sed"]), (w_proj[:], w["proj_w"]), (fc1[:], w["fc1_w"]),
                               (fc2[:], w["fc2_w"]), (fc1_b[:], w["fc1_b"])]
                normed = sb(f"l1a_h{half}_normed", [C, 2, N])
                xsq = sb(f"l1a_h{half}_xsq", [C, DEPTH, N])
                rstd = sb(f"l1a_h{half}_rstd", [C, DEPTH, N])
                xhat = sb(f"l1a_h{half}_xhat", [C, 2, N])
                p_xc = [ps(f"l1a_h{half}_xc{i}", [C, N]) for i in range(DEPTH)]
                p_var = [ps(f"l1a_h{half}_var{i}", [C, N]) for i in range(DEPTH)]
                s_xc, s_xsq, s_var, s_lnv, s_rstd, s_xhat, s_normed, s_hi, s_lo, s_whi = a_sems
                rows = N // W // 4
                XHAT0, LO0 = DEPTH, 2 * rows
                block = part.enter_context(nc.Block())

                def all_tiles(eng, step):
                    with eng.Fori(half * HT // DEPTH, (half + 1) * HT // DEPTH - 1) as i:
                        for q in range(DEPTH):
                            step(DEPTH * i + q, q, DEPTH)
                    for q in range(DEPTH):
                        step((half + 1) * HT - DEPTH + q, q, DEPTH - 1 - q)

                if half == 0:
                    @block.sync
                    def _(sp):
                        for dst, src in weights:
                            sp.dma_start(dst, src).then_inc(s_w, 16)

                @block.tensor
                def _(pe):
                    def center_tile(m, q):
                        pe.wait_ge(s_xhat, m + 1 - DEPTH + XHAT0)
                        pe.nop(nofuse=True)
                        pe.matmul(p_xc[q][:], center[:], X[:, bass.ds(m * N, N)], start=True, stop=True).then_inc(s_xc, 1)

                    def var_tile(m, q):
                        pe.wait_ge(s_xsq, m + 1)
                        pe.matmul(p_var[q][:], mean_w[:], xsq[:, q, :], start=True, stop=True).then_inc(s_var, 1)

                    def step(t, q, ahead):
                        if ahead >= 3:
                            center_tile(t + 3, (q + 3) % DEPTH)
                        if ahead >= 1:
                            var_tile(t + 1, (q + 1) % DEPTH)

                    if half == 0:
                        pe.wait_ge(s_w, 16 * len(weights))
                    for q in range(3):
                        center_tile(half * HT + q, q)
                    var_tile(half * HT, 0)
                    all_tiles(pe, step)

                @block.scalar
                def _(act):
                    def square_tile(m, q):
                        act.wait_ge(s_xc, m + 1)
                        act.activation(xsq[:, q, :], p_xc[q][:], ACT.Square).then_inc(s_xsq, 1)

                    def step(t, q, ahead):
                        if ahead >= 2:
                            square_tile(t + 2, (q + 2) % DEPTH)
                        act.wait_ge(s_var, t + 1)
                        act.activation(rstd[:, q, :], p_var[q][:], ACT.Ln, bias=eps[:, 0:1], scale=VAR_SCALE).then_inc(s_lnv, 1)
                        act.wait_ge(s_lnv, t + 1)
                        act.activation(rstd[:, q, :], rstd[:, q, :], ACT.Exp, bias=eps[:, 1:2], scale=-0.5).then_inc(s_rstd, 1)

                    act.preload_act_table_set(LN_EXP)
                    act.wait_ge(s_const, 1)
                    square_tile(half * HT, 0)
                    square_tile(half * HT + 1, 1)
                    all_tiles(act, step)

                def by_place(a, row):
                    view = a[:].rearrange("c (dy dx) (v wx) -> c v dy wx dx", dy=4, dx=4, wx=W // 4)
                    return view[:, bass.ds(row, 1)].rearrange("c v dy wx dx -> c (v dy) wx dx")

                def tokens(q, v):
                    return normed[:, q % 2, :].rearrange("c (v dy wx dx) -> c v dy wx dx", dy=4, wx=W // 4, dx=4)[:, v]

                @block.vector
                def _(dve):
                    def step(t, q, ahead):
                        dve.wait_ge(s_rstd, t + 1)
                        dve.tensor_tensor(xhat[:, q % 2, :], p_xc[q][:], rstd[:, q, :], ALU.mult).then_inc(s_xhat, 1)
                        dve.wait_ge(s_xhat, t + 1 + XHAT0)
                        dve.wait_ge(s_lo, rows * (t - 1) + LO0)
                        dve.tensor_scalar(normed[:, q % 2, :], xhat[:, q % 2, :], cols[:, 0:1], cols[:, 1:2],
                                          ALU.mult, ALU.add).then_inc(s_normed, 1)
                        dve.wait_ge(s_normed, t + 1)
                        for v in range(rows):
                            dve.tensor_copy(by_place(xn[0], rows * (t - half * HT) + v), tokens(q, v)).then_inc(s_hi, 1)

                    if half == 0:
                        dve.sem_inc(s_xhat, XHAT0)
                        dve.memset(eps[:, 1:2], 0.5 * float(np.log(VAR_SCALE)))
                        dve.memset(eps[:, 0:1], EPS * VAR_SCALE).then_inc(s_const, 1)
                        dve.wait_ge(s_w, 16 * len(weights))
                        for high, full in ((w_pos[0], w_sed), (w_fc1[0], fc1), (w_fc2[0], fc2)):
                            dve.tensor_copy(high[:], full[:]).then_inc(s_whi, 1)
                        dve.wait_ge(s_whi, 3)
                        dve.tensor_scalar(w_neg[0][:], w_pos[0][:], -1.0, None, ALU.mult).then_inc(s_const, 1)
                    all_tiles(dve, step)

                @block.gpsimd
                def _(pool):
                    def step(t, q, ahead):
                        for v in range(rows):
                            pool.wait_ge(s_hi, rows * t + v + 1)
                            pool.nop(nofuse=True)
                            pool.tensor_tensor(by_place(xn[1], rows * (t - half * HT) + v), tokens(q, v),
                                               by_place(xn[0], rows * (t - half * HT) + v), ALU.subtract).then_inc(s_lo, 1)

                    if half == 0:
                        pool.sem_inc(s_lo, LO0)
                        pool.wait_ge(s_w, 16 * len(weights))
                        pool.wait_ge(s_whi, 3)
                        for low, full, high in ((w_pos[1], w_sed, w_pos[0]), (w_neg[1], w_pos[0], w_sed),
                                                (w_fc1[1], fc1, w_fc1[0]), (w_fc2[1], fc2, w_fc2[0])):
                            pool.tensor_tensor(low[:], full[:], high[:], ALU.subtract)
                    all_tiles(pool, step)

            with ExitStack() as part:
                sb = lambda name, shape, dt=F32: part.enter_context(nc.sbuf_tensor(name, shape, dt))
                ps = lambda name, shape: part.enter_context(nc.psum_tensor(name, shape, F32))
                act_y = sb(f"l1b_h{half}_act_y", [C, N])
                x1 = sb(f"l1b_h{half}_x1", [C, 2, N])
                xsq = sb(f"l1b_h{half}_xsq", [C, N])
                rstd = sb(f"l1b_h{half}_rstd", [C, N])
                h_in = sb(f"l1b_h{half}_h_in", [C, N])
                h_in_hl = [sb(f"l1b_h{half}_h_in_{part}", [C, N], F32R) for part in HL]
                h = sb(f"l1b_h{half}_h", [128, FB, N])
                h_hl = [sb(f"l1b_h{half}_h_{part}", [128, FB, N], F32R) for part in HL]
                p_y = [ps(f"l1b_h{half}_y{i}", [C, N]) for i in range(2)]
                p_x1, p_xc, p_var = (ps(f"l1b_h{half}_p_" + n, [C, N]) for n in ("x1", "xc", "var"))
                p_h = [ps(f"l1b_h{half}_h{i}", [128, N]) for i in range(FB)]
                p_out = p_x1
                OUT0 = 2
                (s_y, s_gy, s_pr, s_x1, s_xc, s_xsq, s_var, s_lnv, s_rstd, s_xhat, s_hin, s_fc1, s_h, s_fc2, s_out,
                 s_in_hi, s_in_lo, s_h_hi, s_h_lo) = b_sems
                block = part.enter_context(nc.Block())

                @block.tensor
                def _(pe):
                    def three_passes(out, weight, x, start, stop):
                        pe.matmul(out, weight[0], x[0], start=start, stop=False)
                        pe.matmul(out, weight[1], x[0], start=False, stop=False)
                        return pe.matmul(out, weight[0], x[1], start=False, stop=stop)

                    def product(k, i):
                        weight = w_pos if SIGNS[i][k] > 0 else w_neg
                        mm = three_passes(p_y[k % 2][:], [part[:, i ^ k, :] for part in weight],
                                          [part[:, i, :] for part in xn], i == 0, i == P - 1)
                        if i == P - 1:
                            mm.then_inc(s_y, 1)

                    def project(tile):
                        pe.wait_ge(s_gy, tile + 1)
                        pe.wait_ge(s_out, tile - 1 + OUT0)
                        pe.matmul(p_x1[:], w_proj[:], act_y[:], start=True, stop=True).then_inc(s_pr, 1)

                    def centered(tile, par):
                        pe.wait_ge(s_x1, tile + 1)
                        pe.matmul(p_xc[:], center[:], x1[:, par, :], start=True, stop=True).then_inc(s_xc, 1)

                    def variance(tile):
                        pe.wait_ge(s_xsq, tile + 1)
                        pe.matmul(p_var[:], mean_w[:], xsq[:], start=True, stop=True).then_inc(s_var, 1)

                    def mlp_in(tile):
                        pe.wait_ge(s_in_lo, tile + 1)
                        for f in range(FB):
                            three_passes(p_h[f][:], [part[:, f * 128:(f + 1) * 128] for part in w_fc1],
                                         [part[:] for part in h_in_hl], True, True).then_inc(s_fc1, 1)

                    def mlp_out(tile):
                        for f in range(FB):
                            pe.wait_ge(s_h_lo, FB * tile + f + 1)
                            mm = three_passes(p_out[:], [part[:, f, :] for part in w_fc2],
                                              [part[:, f, :] for part in h_hl], f == 0, f == FB - 1)
                        mm.then_inc(s_fc2, 1)

                    for k in range(P + 2):
                        before, before2 = half * P + k - 1, half * P + k - 2
                        for i in range(P):
                            if k < P:
                                product(k, i)
                            if 0 < k <= P:
                                if i == 1:
                                    project(before)
                                if i == 6:
                                    centered(before, (k - 1) % 2)
                                if i == 9:
                                    variance(before)
                            if k > 1:
                                if i == 3:
                                    mlp_in(before2)
                                if i == 13:
                                    mlp_out(before2)

                @block.scalar
                def _(act):
                    for k in range(1, P + 2):
                        before, before2 = half * P + k - 1, half * P + k - 2
                        if k <= P:
                            act.wait_ge(s_y, before + 1)
                            act.activation(act_y[:], p_y[(k - 1) % 2][:], ACT.Gelu).then_inc(s_gy, 1)
                        if k > 1:
                            for f in range(FB):
                                act.wait_ge(s_fc1, FB * before2 + f + 1)
                                act.activation(h[:, f, :], p_h[f][:], ACT.Gelu, bias=fc1_b[:, f:f + 1]).then_inc(s_h, 1)
                        if k <= P:
                            act.preload_act_table_set(LN_EXP)
                            act.wait_ge(s_xc, before + 1)
                            act.activation(xsq[:], p_xc[:], ACT.Square).then_inc(s_xsq, 1)
                            act.wait_ge(s_var, before + 1)
                            act.activation(rstd[:], p_var[:], ACT.Ln, bias=eps[:, 0:1], scale=VAR_SCALE).then_inc(s_lnv, 1)
                            act.wait_ge(s_lnv, before + 1)
                            act.activation(rstd[:], rstd[:], ACT.Exp, bias=eps[:, 1:2], scale=-0.5).then_inc(s_rstd, 1)

                @block.vector
                def _(dve):
                    places = X[:].rearrange("c (v dy wx dx) -> c dy dx v wx", dy=4, wx=W // 4, dx=4)
                    VH = N // (W // 4)
                    as_x = lambda a: a.rearrange("c (v wx) -> c v wx", wx=W // 4)
                    x_place = lambda k: places[:, k // 4, k % 4, half * VH:(half + 1) * VH, :]

                    def residual(k, tile):
                        dve.wait_ge(s_pr, tile + 1)
                        dve.scalar_tensor_tensor(as_x(x1[:, k % 2, :]), as_x(p_x1[:]), cols[:, 2:3], x_place(k),
                                                 ALU.add, ALU.add).then_inc(s_x1, 1)

                    def high_of_h(tile):
                        for f in range(FB):
                            dve.wait_ge(s_h, FB * tile + f + 1)
                            dve.tensor_copy(h_hl[0][:, f, :], h[:, f, :]).then_inc(s_h_hi, 1)

                    def normalise(tile):
                        dve.wait_ge(s_rstd, tile + 1)
                        dve.tensor_tensor(h_in[:], p_xc[:], rstd[:], ALU.mult).then_inc(s_xhat, 1)
                        dve.wait_ge(s_xhat, tile + 1)
                        dve.tensor_scalar(h_in[:], h_in[:], cols[:, 3:4], cols[:, 4:5],
                                          ALU.mult, ALU.add).then_inc(s_hin, 1)
                        dve.wait_ge(s_hin, tile + 1)
                        dve.tensor_copy(h_in_hl[0][:], h_in[:]).then_inc(s_in_hi, 1)

                    def write_x(k, tile):
                        dve.wait_ge(s_fc2, tile + 1)
                        dve.scalar_tensor_tensor(x_place(k), as_x(p_out[:]), cols[:, 5:6], as_x(x1[:, k % 2, :]),
                                                 ALU.add, ALU.add).then_inc(s_out, 1)

                    if half == 0:
                        dve.sem_inc(s_out, OUT0)
                    for k in range(1, P + 2):
                        before, before2 = half * P + k - 1, half * P + k - 2
                        if k <= P:
                            residual(k - 1, before)
                        if k > 1:
                            high_of_h(before2)
                        if k <= P:
                            normalise(before)
                        if k > 1:
                            write_x(k - 2, before2)

                @block.gpsimd
                def _(pool):
                    for k in range(1, P + 2):
                        before, before2 = half * P + k - 1, half * P + k - 2
                        if k > 1:
                            for f in range(FB):
                                pool.wait_ge(s_h_hi, FB * before2 + f + 1)
                                pool.tensor_tensor(h_hl[1][:, f, :], h[:, f, :], h_hl[0][:, f, :], ALU.subtract).then_inc(s_h_lo, 1)
                        if k <= P:
                            pool.wait_ge(s_in_hi, before + 1)
                            pool.tensor_tensor(h_in_hl[1][:], h_in[:], h_in_hl[0][:], ALU.subtract).then_inc(s_in_lo, 1)


def sedenion_layout(w):
    return {
        "center": np.eye(C, dtype=np.float32) - np.float32(1 / C),
        "mean_w": np.full((C, C), 1 / C, np.float32),
        "cols": np.stack([w["L1_conv_" + n] for n in ("norm1_g", "norm1_b", "proj_b", "norm2_g", "norm2_b", "fc2_b")], 1),
        "w_sed": w["L1_conv_w_sed"].transpose(1, 0, 2),
        "proj_w": w["L1_conv_proj_w"],
        "fc1_w": w["L1_conv_fc1_w"],
        "fc2_w": w["L1_conv_fc2_w"].reshape(-1, 128, C).transpose(1, 0, 2),
        "fc1_b": w["L1_conv_fc1_b"].reshape(-1, 128).T,
    }


HEADS, HD, WIN = 6, 16, 7
TAPS = WIN * WIN
PAD = WIN // 2
HP, WP = H + 2 * PAD, W + 2 * PAD
PAIRS = H // 2
ROWS = 2 * PAD + 2
STRIP = N // W


def attention_qkv(nc, w, X, qkv_d, x_d):
    QK = 2
    with ExitStack() as ctx:
        sb = lambda name, shape, dt=F32: ctx.enter_context(nc.sbuf_tensor(name, shape, dt))
        ps = lambda name, shape: ctx.enter_context(nc.psum_tensor(name, shape, F32))
        sem = lambda name: ctx.enter_context(nc.semaphore(name))
        w_qkv = sb("l2a_w_qkv", [C, 3, C])
        cols = sb("l2a_cols", [C, 8])
        stats = sb("l2a_stats", [C, TILES, 6])
        moments = sb("l2a_moments", [C, 2])
        bias = sb("l2a_bias", [C, 3])
        norm = sb("l2a_norm", [C, 4])
        eps = sb("l2a_eps", [C, 2])
        zeros = sb("l2a_zeros", [C, 2 * QK + 1, PAD * WP])
        xn = sb("l2a_xn", [C, 2, N])
        qk = sb("l2a_qk", [C, 2, QK, N])
        strip = sb("l2a_strip", [C, 2, 2, QK, STRIP, WP], F32R)
        v_strip = sb("l2a_v_strip", [C, 2, STRIP, WP])
        p_qkv = [[ps(f"l2a_p{par}{g}", [C, N]) for g in range(3)] for par in range(2)]
        s_w, s_zero, s_pads, s_x, s_stats, s_norm, s_lnv = (sem("l2a_" + n) for n in (
            "weights", "zeroed", "pads_stored", "x_stored", "stats", "norm", "lnvar"))
        s_xn, s_mm, s_qk, s_hi, s_lo, s_v = (sem("l2a_" + n) for n in (
            "xn", "qkv_mm", "qk", "high_in_strip", "low_in_strip", "v_in_strip"))
        s_strip = [sem(f"l2a_strip{i}_stored") for i in range(2)]
        by_group = qkv_d.rearrange("(g c) b p -> c g b p", c=C)
        block = ctx.enter_context(nc.Block())

        @block.sync
        def _(sp):
            sp.dma_start(w_qkv[:], w["qkv_w"]).then_inc(s_w, 16)
            sp.dma_start(cols[:], w["cols"]).then_inc(s_w, 16)
            for b in range(B):
                sp.dma_start(x_d[:, b * HW:(b + 1) * HW], X[:, b * HW:(b + 1) * HW]).then_inc(s_x, 16)
            sp.wait_ge(s_zero, 1)
            for b in range(B):
                for row in (0, HP - PAD):
                    sp.dma_start(by_group[:, :, b, row * WP:(row + PAD) * WP], zeros[:]).then_inc(s_pads, 16)
            with sp.Fori(0, B) as b:
                with sp.Fori(0, H // STRIP // 2) as s2:
                    for par in range(2):
                        tile = b * (H // STRIP) + 2 * s2 + par
                        place = bass.ds((PAD + par * STRIP) * WP + s2 * (2 * STRIP * WP), STRIP * WP)
                        sp.wait_ge(s_v, tile + 1)
                        sp.nop(nofuse=True)
                        sp.dma_start(by_group[:, 2 * QK:, bass.ds(b, 1), place],
                                     v_strip[:, par].rearrange("c r x -> c (r x)")).then_inc(s_strip[par], 16)
                        sp.wait_ge(s_lo, tile + 1)
                        sp.nop(nofuse=True)
                        sp.dma_start(by_group[:, 0:2 * QK, bass.ds(b, 1), place],
                                     strip[:, par].bitcast(F32).rearrange("c p g r x -> c (p g) (r x)")).then_inc(s_strip[par], 16)
            for par in range(2):
                sp.wait_ge(s_strip[par], 32 * (TILES // 2))
            sp.wait_ge(s_pads, 16 * 2 * B)
            sp.wait_ge(s_x, 16 * B)

        @block.tensor
        def _(pe):
            def qkv(t, par, first=False):
                pe.wait_ge(s_xn, t + 1)
                if not first:
                    pe.wait_ge(s_qk, QK * (t - 1))
                    pe.wait_ge(s_v, t - 1)
                for g in range(3):
                    mm = pe.matmul(p_qkv[par][g][:], w_qkv[:, g, :], xn[:, par, :], start=True, stop=True)
                mm.then_inc(s_mm, 1)

            pe.wait_ge(s_w, 32)
            qkv(0, 0, first=True)
            qkv(1, 1, first=True)
            with pe.Fori(1, TILES // 2) as i:
                qkv(2 * i, 0)
                qkv(2 * i + 1, 1)

        @block.scalar
        def _(act):
            def qk_tile(t, par, first=False):
                act.wait_ge(s_mm, t + 1)
                if not first:
                    act.wait_ge(s_lo, t - 1)
                for g in range(QK):
                    act.activation(qk[:, par, g, :], p_qkv[par][g][:],
                                   ACT.Identity, bias=bias[:, g:g + 1], scale=cols[:, 5 + g:6 + g]).then_inc(s_qk, 1)

            act.preload_act_table_set(LN_EXP)
            act.wait_ge(s_stats, TILES + 1)
            act.activation(norm[:, 0:1], moments[:, 1:2], ACT.Ln, bias=eps[:, 0:1], scale=VAR_SCALE).then_inc(s_lnv, 1)
            act.wait_ge(s_lnv, 1)
            act.activation(norm[:, 1:2], norm[:, 0:1], ACT.Exp, bias=eps[:, 1:2], scale=-0.5).then_inc(s_lnv, 1)
            act.wait_ge(s_norm, 5)
            qk_tile(0, 0, first=True)
            qk_tile(1, 1, first=True)
            with act.Fori(1, TILES // 2) as i:
                qk_tile(2 * i, 0)
                qk_tile(2 * i + 1, 1)

        @block.vector
        def _(dve):
            def xn_tile(t, par, first=False):
                if not first:
                    dve.wait_ge(s_mm, t - 1)
                    dve.nop(nofuse=True)
                dve.tensor_scalar(xn[:, par, :], X[:, bass.ds(t * N, N)], norm[:, 2:3], norm[:, 3:4],
                                  ALU.mult, ALU.add).then_inc(s_xn, 1)

            def to_strips(t, par, first=False):
                dve.wait_ge(s_mm, t + 1)
                if not first:
                    dve.wait_ge(s_strip[par], 16 * (t - par))
                dve.tensor_scalar(v_strip[:, par, :, PAD:PAD + W], p_qkv[par][2][:].rearrange("c (r x) -> c r x", x=W),
                                  bias[:, 2:3], None, ALU.add).then_inc(s_v, 1)
                dve.wait_ge(s_qk, QK * (t + 1))
                dve.tensor_copy(strip[:, par, 0, :, :, PAD:PAD + W],
                                qk[:, par].rearrange("c g (r x) -> c g r x", x=W)).then_inc(s_hi, 1)

            dve.memset(zeros[:], 0.0).then_inc(s_zero, 1)
            dve.memset(strip[:].bitcast(F32), 0.0)
            dve.memset(v_strip[:], 0.0).then_inc(s_norm, 1)
            dve.memset(eps[:, 1:2], 0.5 * float(np.log(VAR_SCALE)))
            dve.memset(eps[:, 0:1], EPS * VAR_SCALE).then_inc(s_norm, 1)
            with dve.Fori(0, TILES) as t:
                dve.bn_stats(stats[:, bass.ds(t, 1), :].rearrange("c t s -> c (t s)"),
                             X[:, bass.ds(t * N, N)]).then_inc(s_stats, 1)
            dve.wait_ge(s_stats, TILES)
            dve.bn_aggr(moments[:], stats[:].rearrange("c t s -> c (t s)")).then_inc(s_stats, 1)
            dve.wait_ge(s_w, 32)
            dve.tensor_tensor(bias[:], cols[:, 2:5], cols[:, 5:8], ALU.mult).then_inc(s_norm, 1)
            dve.wait_ge(s_lnv, 2)
            dve.tensor_tensor(norm[:, 2:3], cols[:, 0:1], norm[:, 1:2], ALU.mult).then_inc(s_norm, 1)
            dve.wait_ge(s_norm, 4)
            dve.tensor_tensor(norm[:, 0:1], moments[:, 0:1], norm[:, 2:3], ALU.mult).then_inc(s_zero, 1)
            dve.wait_ge(s_zero, 2)
            dve.tensor_tensor(norm[:, 3:4], cols[:, 1:2], norm[:, 0:1], ALU.subtract).then_inc(s_norm, 1)
            dve.wait_ge(s_norm, 5)
            xn_tile(0, 0, first=True)
            xn_tile(1, 1, first=True)
            to_strips(0, 0, first=True)
            to_strips(1, 1, first=True)
            with dve.Fori(1, TILES // 2) as i:
                xn_tile(2 * i, 0)
                xn_tile(2 * i + 1, 1)
                to_strips(2 * i, 0)
                to_strips(2 * i + 1, 1)

        @block.gpsimd
        def _(pool):
            def low_tile(t, par):
                pool.wait_ge(s_hi, t + 1)
                pool.nop(nofuse=True)
                pool.tensor_tensor(strip[:, par, 1, :, :, PAD:PAD + W], qk[:, par].rearrange("c g (r x) -> c g r x", x=W),
                                   strip[:, par, 0, :, :, PAD:PAD + W], ALU.subtract).then_inc(s_lo, 1)

            with pool.Fori(0, TILES // 2) as i:
                low_tile(2 * i, 0)
                low_tile(2 * i + 1, 1)


def attention_heads(nc, w, qkv_d, o_d):
    SHIFTS, GROUPS = 4, 2
    CH = 2 * HD
    CP = 8
    CHUNKS = PAIRS // CP
    HB = 2 * B
    HCHUNKS = CHUNKS // 2
    GROWS = 2 * CP * HCHUNKS + SHIFTS - 1
    M = 2 * TAPS
    XT = 4
    TURNS = W // XT
    VC = HD // 2
    UNITS = 2 * HD
    ON_DVE = [u % 5 in (0, 2) for u in range(UNITS)]
    DVE_UNITS = sum(ON_DVE)
    POOL_UNITS = UNITS - DVE_UNITS
    POOL_PRODS = 2
    EXPS = 4
    with ExitStack() as ctx:
        sb = lambda name, shape, dt=F32: ctx.enter_context(nc.sbuf_tensor(name, shape, dt))
        ps = lambda name, shape: ctx.enter_context(nc.psum_tensor(name, shape, F32))
        sem = lambda name: ctx.enter_context(nc.semaphore(name))
        w_conv = [sb(f"l2b_w_conv_{part}", [128, GROUPS, WIN, M], F32R) for part in HL]
        ident = sb("l2b_ident", [M, M])
        dm_b = sb("l2b_dm_b", [M, 1])
        rel_b = sb("l2b_rel_b", [M, HEADS])
        head_b = sb("l2b_head_b", [M, HEADS])
        this_b = sb("l2b_this_b", [M, 1])
        img = [sb(f"l2b_img_{part}", [128, 2, GROWS, WP], F32R) for part in HL]
        logits = sb("l2b_logits", [M, B, PAIRS, W])
        attn = sb("l2b_attn", [128, W, 2, TAPS])
        peak = sb("l2b_peak", [128, W, 2])
        total = sb("l2b_total", [128, W, 2])
        v = [sb(f"l2b_v{i}", [128, VC, ROWS, WP]) for i in range(2)]
        prod = [sb(f"l2b_prod{i}", [128, W, TAPS]) for i in range(1 + POOL_PRODS)]
        w_full = prod[0][:].rearrange("q x t -> q (x t)")[:, 0:GROUPS * WIN * M]
        osum = sb("l2b_osum", [128, HD, 2, W])
        p_conv = [ps(f"l2b_conv{i}", [M, N]) for i in range(2)]
        p_turn = [ps(f"l2b_turn{i}", [128, XT, 2, TAPS]) for i in range(3)]
        s_w, s_v, s_o = (sem("l2b_" + n) for n in ("weights", "v_loaded", "o_stored"))
        s_img = [sem(f"l2b_img{i}_loaded") for i in range(2)]
        s_bias, s_this, s_conv, s_log, s_turn, s_peak, s_sub, s_exp = (sem("l2b_" + n) for n in (
            "bias", "this_bias", "conv", "logits", "turned", "peak", "shifted", "exp"))
        s_tot, s_rcp, s_pp, s_pv, s_sum, s_osum = (sem("l2b_" + n) for n in (
            "total", "reciprocal", "pool_products", "vector_products", "summed", "scaled"))
        block = ctx.enter_context(nc.Block())

        @block.sync
        def _(sp):
            def load_image(head, hb, first=False):
                if not first:
                    sp.wait_ge(s_conv, head * (B * CHUNKS) + (hb - 1) * HCHUNKS)
                    sp.nop(nofuse=True)
                row = hb % 2 * 2 * CP * HCHUNKS
                for part in range(2):
                    for s in range(SHIFTS):
                        sp.dma_start(img[part][s * CH:(s + 1) * CH, hb % 2].bitcast(F32).rearrange("c r x -> c (r x)"),
                                     qkv_d[bass.ds(head * CH + part * (2 * C), CH), hb // 2,
                                           (row + s) * WP:(row + s + GROWS) * WP]).then_inc(s_img[hb % 2], 16)

            def load_v(head, first=False):
                for half in range(2):
                    if not first:
                        dve_done = sum(ON_DVE[:(half + 1) * (UNITS // 2)])
                        pool_done = (half + 1) * (UNITS // 2) - dve_done
                        sp.wait_ge(s_pv, head * DVE_UNITS + (dve_done - DVE_UNITS))
                        sp.nop(nofuse=True)
                        sp.wait_ge(s_pp, head * POOL_UNITS + (pool_done - POOL_UNITS))
                        sp.nop(nofuse=True)
                    for b in range(B):
                        src = qkv_d[bass.ds(head * HD + (4 * C + half * VC), VC), b]
                        src = bass.AP(src.tensor, src.offset,
                                      [[2 * WP, PAIRS], [B * HP * WP, VC], [1, ROWS * WP]])
                        sp.dma_start(v[half][b * PAIRS:(b + 1) * PAIRS].rearrange("p c r x -> p c (r x)"),
                                     src).then_inc(s_v, 16)

            def store_o(head):
                sp.wait_ge(s_osum, head + 1)
                sp.nop(nofuse=True)
                sp.dma_start(o_d[bass.ds(head * HD, HD)].rearrange("c (q z) -> q c z", z=2 * W),
                             osum[:].rearrange("q c r x -> q c (r x)")).then_inc(s_o, 16)

            for dst, src in ((w_full, "w_conv"), (ident[:], "ident"), (dm_b[:], "dm_b"), (rel_b[:], "rel_b")):
                sp.dma_start(dst, w[src].rearrange("c g x m -> c (g x m)") if dst is w_full else w[src]).then_inc(s_w, 16)
            load_image(0, 0, first=True)
            load_image(0, 1, first=True)
            load_v(0, first=True)
            for hb in range(2, HB):
                load_image(0, hb)
            load_image(1, 0)
            load_image(1, 1)
            with sp.Fori(1, HEADS - 1) as head:
                for hb in range(2, HB):
                    load_image(head, hb)
                load_image(head + 1, 0)
                load_image(head + 1, 1)
                load_v(head)
                store_o(head - 1)
            for hb in range(2, HB):
                load_image(HEADS - 1, hb)
            load_v(HEADS - 1)
            store_o(HEADS - 2)
            store_o(HEADS - 1)
            sp.wait_ge(s_o, 16 * HEADS)

        @block.tensor
        def _(pe):
            def conv(head, n, first=False):
                hb, ch = n // HCHUNKS, n % HCHUNKS
                if ch == 0:
                    pe.wait_ge(s_img[hb % 2], 16 * 2 * SHIFTS * (HB // 2) * head + 16 * 2 * SHIFTS * (hb // 2 + 1))
                if not first:
                    pe.wait_ge(s_log, head * (B * CHUNKS) + (n - 1))
                passes = [(w_part, x_part, g, dx) for w_part, x_part in ((0, 0), (1, 0), (0, 1))
                          for g in range(GROUPS) for dx in range(WIN)]
                for at, (w_part, x_part, g, dx) in enumerate(passes):
                    row = 2 * CP * ch + SHIFTS * g
                    mm = pe.matmul(p_conv[n % 2][:], w_conv[w_part][:, g, dx, :],
                                   img[x_part][:, hb % 2, row:row + 2 * CP - 1:2, dx:dx + W],
                                   start=(at == 0), stop=(at == len(passes) - 1))
                mm.then_inc(s_conv, 1)

            def turn(head, g, first=False):
                if not first:
                    pe.wait_ge(s_sub, head * TURNS + max(g - 2, 0))
                for j in range(XT):
                    mm = pe.transpose(p_turn[g % 3][:, j].rearrange("q r t -> q (r t)"),
                                      logits[:, :, :, XT * g + j].rearrange("m b p -> m (b p)"), ident[:])
                mm.then_inc(s_turn, 1)

            def head_step(head, first=False):
                for n in range(B * CHUNKS):
                    conv(head, n, first=first and n < 2)
                pe.wait_ge(s_log, head * (B * CHUNKS) + B * CHUNKS)
                for g in range(TURNS):
                    turn(head, g, first=first and g < 3)

            pe.wait_ge(s_w, 64)
            pe.wait_ge(s_bias, 3)
            head_step(0, first=True)
            with pe.Fori(1, HEADS) as head:
                head_step(head)

        @block.scalar
        def _(act):
            act.preload_act_table_set(LN_EXP)
            act.wait_ge(s_bias, 1)
            with act.Fori(0, HEADS) as head:
                act.activation(this_b[:], head_b[:, bass.ds(head, 1)], ACT.Copy).then_inc(s_this, 1)
                act.wait_ge(s_this, head + 1)
                for b in range(B):
                    for ch in range(CHUNKS):
                        n = b * CHUNKS + ch
                        act.wait_ge(s_conv, head * (B * CHUNKS) + n + 1)
                        act.activation(logits[:, b, CP * ch:CP * (ch + 1), :].rearrange("m p x -> m (p x)"),
                                       p_conv[n % 2][:], ACT.Identity, bias=this_b[:]).then_inc(s_log, 1)
                for e in range(EXPS):
                    act.wait_ge(s_sub, head * TURNS + (e + 1) * (TURNS // EXPS))
                    piece = attn[:, e * (W // EXPS):(e + 1) * (W // EXPS)].rearrange("q x r t -> q (x r t)")
                    act.activation(piece, piece, ACT.Exp).then_inc(s_exp, 1)

        def products(eng, unit, dst):
            c, r = unit // 2, unit % 2
            src = v[c // VC][:, c % VC, r:r + WIN, 0:W]
            step = list(src.ap)
            window = bass.AP(src.tensor, src.offset, [step[0], [1, W], [WP, WIN], [1, WIN]])
            return eng.tensor_tensor(dst.rearrange("q x (dy dx) -> q x dy dx", dx=WIN), window,
                                     attn[:, :, r].rearrange("q x (dy dx) -> q x dy dx", dx=WIN), ALU.mult)

        def pool_unit(unit):
            return unit - sum(ON_DVE[:unit])

        @block.vector
        def _(dve):
            def softmax(head):
                for g in range(TURNS):
                    dve.wait_ge(s_turn, head * TURNS + g + 1)
                    dve.tensor_reduce(peak[:, XT * g:XT * (g + 1)], p_turn[g % 3][:], AX_X, ALU.max).then_inc(s_peak, 1)
                    dve.wait_ge(s_peak, head * TURNS + g + 1)
                    top = peak[:, XT * g:XT * (g + 1)]
                    dve.tensor_tensor(attn[:, XT * g:XT * (g + 1)].rearrange("q x r t -> q (x r) t"),
                                      p_turn[g % 3][:].rearrange("q x r t -> q (x r) t"),
                                      top.rearrange("q x r -> q (x r)").unsqueeze(2).to_broadcast([128, XT * 2, TAPS]),
                                      ALU.subtract).then_inc(s_sub, 1)
                for e in range(EXPS):
                    dve.wait_ge(s_exp, head * EXPS + e + 1)
                    part = slice(e * (W // EXPS), (e + 1) * (W // EXPS))
                    dve.tensor_reduce(total[:, part], attn[:, part], AX_X, ALU.add).then_inc(s_tot, 1)
                dve.wait_ge(s_tot, head * EXPS + EXPS)
                dve.reciprocal(total[:], total[:]).then_inc(s_rcp, 1)

            def sums(head, unit):
                if ON_DVE[unit]:
                    which = 0
                    dve.wait_ge(s_pv, head * DVE_UNITS + unit - pool_unit(unit) + 1)
                else:
                    which = 1 + pool_unit(unit) % POOL_PRODS
                    dve.wait_ge(s_pp, head * POOL_UNITS + pool_unit(unit) + 1)
                dve.tensor_reduce(osum[:, unit // 2, unit % 2, :], prod[which][:], AX_X, ALU.add).then_inc(s_sum, 1)

            def head_step(head, first=False):
                softmax(head)
                dve.wait_ge(s_v, 16 * 2 * B * head + 16 * 2 * B)
                if not first:
                    dve.wait_ge(s_o, 16 * head)
                for unit in range(UNITS):
                    if ON_DVE[unit]:
                        if unit:
                            dve.wait_ge(s_sum, head * UNITS + unit)
                        products(dve, unit, prod[0][:]).then_inc(s_pv, 1)
                    sums(head, unit)
                dve.wait_ge(s_sum, head * UNITS + UNITS)
                dve.wait_ge(s_rcp, head + 1)
                inverse = bass.AP(total[:].tensor, total[:].offset, [list(total[:].ap)[0], [0, HD], [1, 2], [2, W]])
                dve.tensor_tensor(osum[:], osum[:], inverse, ALU.mult).then_inc(s_osum, 1)

            dve.wait_ge(s_w, 64)
            dve.tensor_scalar(head_b[:], rel_b[:], dm_b[:], None, ALU.add).then_inc(s_bias, 1)
            high, low = (part[:].rearrange("q g x m -> q (g x m)") for part in w_conv)
            dve.tensor_copy(high, w_full).then_inc(s_bias, 1)
            dve.wait_ge(s_bias, 2)
            dve.tensor_tensor(low, w_full, high, ALU.subtract).then_inc(s_bias, 1)
            head_step(0, first=True)
            with dve.Fori(1, HEADS) as head:
                head_step(head)

        @block.gpsimd
        def _(pool):
            def head_step(head, first=False):
                pool.wait_ge(s_exp, head * EXPS + EXPS)
                pool.wait_ge(s_v, 16 * 2 * B * head + 16 * 2 * B)
                mine = [unit for unit in range(UNITS) if not ON_DVE[unit]]
                for j, unit in enumerate(mine):
                    if j >= POOL_PRODS:
                        pool.wait_ge(s_sum, head * UNITS + (mine[j - POOL_PRODS] + 1))
                    products(pool, unit, prod[1 + j % POOL_PRODS][:]).then_inc(s_pp, 1)

            head_step(0, first=True)
            with pool.Fori(1, HEADS) as head:
                head_step(head)


def attention_out(nc, w, X, o_d, x_d):
    F = 4 * C
    FB = F // 128
    with ExitStack() as ctx:
        sb = lambda name, shape, dt=F32: ctx.enter_context(nc.sbuf_tensor(name, shape, dt))
        ps = lambda name, shape: ctx.enter_context(nc.psum_tensor(name, shape, F32))
        sem = lambda name: ctx.enter_context(nc.semaphore(name))
        w_proj = sb("l2c_w_proj", [C, C])
        w_c1 = sb("l2c_w_c1", [C, F])
        w_c2 = sb("l2c_w_c2", [128, FB, C])
        c1_b = sb("l2c_c1_b", [128, FB])
        cols = sb("l2c_cols", [C, 2])
        o = sb("l2c_o", [C, T])
        x1 = sb("l2c_x1", [C, 2, N])
        h = sb("l2c_h", [128, FB, N])
        p_x1 = [ps(f"l2c_p_x1{i}", [C, N]) for i in range(2)]
        p_out = [ps(f"l2c_p_out{i}", [C, N]) for i in range(2)]
        p_h = [ps(f"l2c_p_h{i}", [128, N]) for i in range(FB)]
        s_w, s_o, s_x = (sem("l2c_" + n) for n in ("weights", "o_loaded", "x_loaded"))
        s_pr, s_x1, s_c1, s_h, s_c2, s_out = (sem("l2c_" + n) for n in (
            "projected", "x1_written", "c1", "gelu_h", "c2", "x_written"))
        block = ctx.enter_context(nc.Block())

        @block.sync
        def _(sp):
            for dst, src in ((w_proj, "proj_w"), (w_c1, "c1_w"), (w_c2, "c2_w"), (c1_b, "c1_b"), (cols, "cols_out")):
                sp.dma_start(dst[:], w[src]).then_inc(s_w, 16)
            for b in range(B):
                image = slice(b * HW, (b + 1) * HW)
                sp.dma_start(o[:, image], o_d[:, image]).then_inc(s_o, 16)
                sp.dma_start(X[:, image], x_d[:, image]).then_inc(s_x, 16)

        @block.tensor
        def _(pe):
            def project(t, par, first=False):
                if not first:
                    pe.wait_ge(s_x1, t - 1)
                    pe.nop(nofuse=True)
                pe.matmul(p_x1[par][:], w_proj[:], o[:, bass.ds(t * N, N)], start=True, stop=True).then_inc(s_pr, 1)

            def mlp(t, par, first=False):
                pe.wait_ge(s_x1, t + 1)
                for f in range(FB):
                    if not first:
                        pe.wait_ge(s_h, FB * t + f - FB + 1)
                    pe.matmul(p_h[f][:], w_c1[:, f * 128:(f + 1) * 128], x1[:, par, :],
                              start=True, stop=True).then_inc(s_c1, 1)

            def mlp_out(t, par, first=False):
                if not first:
                    pe.wait_ge(s_out, t - 1)
                for f in range(FB):
                    pe.wait_ge(s_h, FB * t + f + 1)
                    mm = pe.matmul(p_out[par][:], w_c2[:, f, :], h[:, f, :], start=(f == 0), stop=(f == FB - 1))
                mm.then_inc(s_c2, 1)

            pe.wait_ge(s_w, 16 * 5)
            pe.wait_ge(s_o, 16 * B)
            project(0, 0, first=True)
            mlp(0, 0, first=True)
            project(1, 1, first=True)
            mlp_out(0, 0, first=True)
            mlp(1, 1)
            project(2, 0)
            mlp_out(1, 1, first=True)
            with pe.Fori(1, TILES // 2 - 1) as i:
                mlp(2 * i, 0)
                project(2 * i + 1, 1)
                mlp_out(2 * i, 0)
                mlp(2 * i + 1, 1)
                project(2 * i + 2, 0)
                mlp_out(2 * i + 1, 1)
            mlp(TILES - 2, 0)
            project(TILES - 1, 1)
            mlp_out(TILES - 2, 0)
            mlp(TILES - 1, 1)
            mlp_out(TILES - 1, 1)

        @block.scalar
        def _(act):
            def gelus(t, first=False):
                for f in range(FB):
                    act.wait_ge(s_c1, FB * t + f + 1)
                    if not first:
                        act.wait_ge(s_c2, t)
                    act.activation(h[:, f, :], p_h[f][:], ACT.Gelu, bias=c1_b[:, f:f + 1]).then_inc(s_h, 1)

            act.wait_ge(s_w, 16 * 5)
            gelus(0, first=True)
            with act.Fori(1, TILES) as t:
                gelus(t)

        @block.vector
        def _(dve):
            def x1_tile(t, par, first=False):
                if not first:
                    dve.wait_ge(s_out, t - 1)
                dve.wait_ge(s_pr, t + 1)
                dve.scalar_tensor_tensor(x1[:, par, :], p_x1[par][:], cols[:, 0:1], X[:, bass.ds(t * N, N)],
                                         ALU.add, ALU.add).then_inc(s_x1, 1)

            def out_tile(t, par):
                dve.wait_ge(s_c2, t + 1)
                dve.scalar_tensor_tensor(X[:, bass.ds(t * N, N)], p_out[par][:], cols[:, 1:2], x1[:, par, :],
                                         ALU.add, ALU.add).then_inc(s_out, 1)

            dve.wait_ge(s_w, 16 * 5)
            dve.wait_ge(s_x, 16 * B)
            x1_tile(0, 0, first=True)
            x1_tile(1, 1, first=True)
            with dve.Fori(0, TILES // 2 - 1) as i:
                out_tile(2 * i, 0)
                x1_tile(2 * i + 2, 0)
                out_tile(2 * i + 1, 1)
                x1_tile(2 * i + 3, 1)
            out_tile(TILES - 2, 0)
            out_tile(TILES - 1, 1)


def local_attention_layout(w):
    g = {n[len("L2_conv_"):]: a for n, a in w.items() if n.startswith("L2_conv_")}
    q, k, v = (np.arange(i * C, (i + 1) * C).reshape(HEADS, HD) for i in range(3))
    rows = np.concatenate([np.concatenate([q, k], 1).ravel(), v.ravel()]).reshape(3, C)
    is_q = rows < C
    scale = np.where(is_q, np.float32(HD ** -0.5), np.float32(1)).astype(np.float32)
    conv = np.zeros((4, 2 * HD, 2, WIN, 2, TAPS), np.float32)
    for s in range(4):
        for grp in range(2):
            for r in range(2):
                dy = 4 * grp + s - r
                if 0 <= dy < WIN:
                    conv[s, :, grp, :, r, :] = g["dm_w"][:, :, dy, :].transpose(1, 2, 0)
    return {
        "qkv_w": g["qkv_w"][rows].transpose(2, 0, 1),
        "cols": np.concatenate([g["bn_gamma"][:, None], g["bn_beta"][:, None], g["qkv_b"][rows].T, scale.T], 1),
        "w_conv": conv.reshape(8 * HD, 2, WIN, 2 * TAPS),
        "ident": np.eye(2 * TAPS, dtype=np.float32),
        "dm_b": np.tile(g["dm_b"], 2)[:, None],
        "rel_b": np.tile(g["rel_bias"], (2, 1)),
        "proj_w": g["proj_w"].T,
        "c1_w": g["c1_w"].T,
        "c2_w": g["c2_w"].T.reshape(-1, 128, C).transpose(1, 0, 2),
        "c1_b": g["c1_b"].reshape(-1, 128).T,
        "cols_out": np.stack([g["proj_b"], g["c2_b"]], 1),
    }


def selective_scan(nc, w, X):
    K, S, R, DL = 4, 16, 6, 8
    G = C // DL
    Q = 48
    PARTS = C // Q
    CHUNKS = HW // N
    STEPS = K * CHUNKS
    LAG = 5
    HCS = 6
    DAS = 3
    DUS = 3
    SMALL_E = 2.0 ** -8
    COLS = N // H
    with ExitStack() as ctx:
        sb = lambda name, shape, dt=F32: ctx.enter_context(nc.sbuf_tensor(name, shape, dt))
        ps = lambda name, shape: ctx.enter_context(nc.psum_tensor(name, shape, F32))
        sem = lambda name: ctx.enter_context(nc.semaphore(name))
        xp_dt = sb("l3_xp_dt", [R, K, C])
        dt_w = sb("l3_dt_w", [R, K, C])
        w_dt = sb("l3_w_dt", [C, K, C])
        w_rep = sb("l3_w_rep", [C, K, 2, 128])
        pick_f = sb("l3_pick_f", [C, Q // DL, 128])
        pick = sb("l3_pick", [C, Q // DL, 128], F32R)
        y_pick = sb("l3_y_pick", [128, G, C])
        a_neg = sb("l3_a_neg", [128, K * G])
        cols = sb("l3_cols", [C, 2 * K])
        d_sum = sb("l3_d_sum", [C, 1])

        xt = sb("l3_xt", [C, HW])
        y_sum = sb("l3_y_sum", [C, HW])
        dx_pos = sb("l3_dx_pos", [C, N])
        e_x = sb("l3_e_x", [C, N])
        log_e = sb("l3_log_e", [C, N])
        series = sb("l3_series", [C, N])
        small = sb("l3_small", [C, N], mybir.dt.uint8)
        dd = sb("l3_dd", [C, 2, N])
        parts = sb("l3_parts", [C, PARTS, 2, N], F32R)
        stacked = sb("l3_stacked", [C, 2, PARTS, 2, N], F32R)
        b_rep = sb("l3_b_rep", [128, 2, N])
        c_rep = sb("l3_c_rep", [128, 2, N])
        da = sb("l3_da", [128, DAS, N])
        bu = sb("l3_bu", [128, DAS, N])
        h = sb("l3_h", [128, G, N])
        hc = sb("l3_hc", [128, HCS, N])
        p_da = [ps(f"l3_p_da{i}", [128, N]) for i in range(2)]
        p_du = [ps(f"l3_p_du{i}", [128, N]) for i in range(DUS)]
        p_y = [ps(f"l3_p_y{i}", [C, N]) for i in range(2)]
        p_bc = ps("l3_p_bc", [128, N])

        s_w, s_setup, s_setup_cp, s_a, s_xt = (sem("l3_" + n) for n in (
            "weights", "setup_mm", "setup_copied", "a", "xt_written"))
        s_dt, s_dx, s_abs, s_exp, s_sp, s_delta, s_du, s_hi, s_lo = (sem("l3_" + n) for n in (
            "dt_mm", "dx", "dt_abs", "dt_exp", "softplus_log", "delta", "du", "part_hi", "part_lo"))
        s_factor, s_series, s_logp = sem("l3_series_factor"), sem("l3_series_and_mask"), sem("l3_log1p")
        s_stack = [sem(f"l3_stacked{i}") for i in range(2)]
        s_bc, s_bccp = sem("l3_bc_mm"), sem("l3_bc_copied")
        s_rep, s_da, s_bu, s_h, s_hc, s_ymm, s_y = (sem("l3_" + n) for n in (
            "replicated", "da", "bu", "h", "hc", "y_mm", "y_added"))
        REP0, DA0, BU0, H0, HC0, YMM0, Y0 = 2 * G, 2, DUS, DAS, 2 * G, HCS, 2
        DX0, DELTA0, LO0, BCCP0 = 1, 1, 1, 1
        weights = [(xp_dt, "xp_dt"), (dt_w, "dt_w_T"), (w_rep, "w_rep"), (pick_f, "pick"),
                   (y_pick, "y_pick"), (a_neg, "a_logs"), (cols, "cols")]
        block = ctx.enter_context(nc.Block())

        def chunk_of(k, c):
            return c if k < 2 else CHUNKS - 1 - c

        def u_of(k, b, c):
            at = chunk_of(k, c) * N
            return X[:, bass.ds(b * HW + at, N)] if k % 2 == 0 else xt[:, bass.ds(at, N)]

        def ahead(k, c, by):
            if not isinstance(c, int):
                return k, c + by
            at = k * CHUNKS + c + by
            return (at // CHUNKS, at % CHUNKS) if 0 <= at < STEPS else None

        def all_steps(eng, image_start, step, image_end):
            def at(b, k, c, par):
                step(b, b * STEPS + (k * CHUNKS) + c, k, c, par, ahead(k, c, 1), ahead(k, c, 2))

            with eng.Fori(0, B) as b:
                image_start(b)
                for k in range(K):
                    at(b, k, 0, 0)
                    at(b, k, 1, 1)
                    with eng.Fori(1, CHUNKS // 2 - 1) as i:
                        at(b, k, 2 * i, 0)
                        at(b, k, 2 * i + 1, 1)
                    at(b, k, CHUNKS - 2, 0)
                    at(b, k, CHUNKS - 1, 1)
                image_end(b)

        @block.sync
        def _(sp_):
            for dst, src in weights:
                sp_.dma_start(dst[:], w[src]).then_inc(s_w, 16)

            def restack(m, par):
                for part, (ready, credit) in enumerate(((s_hi, 0), (s_lo, LO0))):
                    sp_.wait_ge(ready, m + 1 + credit)
                    sp_.nop(nofuse=True)
                    if part == 0:
                        sp_.wait_ge(s_rep, G * (m - 1) + REP0)
                        sp_.nop(nofuse=True)
                    for q in range(PARTS):
                        sp_.dma_start(stacked[part * Q:(part + 1) * Q, par, q].bitcast(F32),
                                      parts[q * Q:(q + 1) * Q, part].bitcast(F32)).then_inc(s_stack[par], 16)

            with sp_.Fori(0, B * STEPS // 2) as i:
                restack(2 * i, 0)
                restack(2 * i + 1, 1)

        @block.tensor
        def _(pe):
            pe.wait_ge(s_w, 16 * len(weights))
            for k in range(K):
                pe.matmul(p_bc[0:C, k * C:(k + 1) * C], xp_dt[:, k, :], dt_w[:, k, :],
                          start=True, stop=True).then_inc(s_setup, 1)
            pe.wait_ge(s_setup_cp, 2)
            pe.sem_inc(s_rep, REP0)
            pe.sem_inc(s_ymm, YMM0)

            def delta_mm(m, b, k, c, copied):
                pe.wait_ge(s_dx, m + DX0)
                pe.nop(nofuse=True)
                pe.wait_ge(s_bccp, 2 * copied + BCCP0)
                pe.nop(nofuse=True)
                pe.matmul(p_bc[0:C, :], w_dt[:, k, :], u_of(k, b, c), start=True, stop=True).then_inc(s_dt, 1)

            def bc_mm(m, b, k, c, j, dts=None):
                pe.wait_ge(s_bccp, 2 * m + j + BCCP0)
                pe.nop(nofuse=True)
                if dts is not None:
                    pe.wait_ge(s_dx, dts + DX0)
                    pe.nop(nofuse=True)
                pe.matmul(p_bc[:], w_rep[:, k, j, :], u_of(k, b, c), start=True, stop=True).then_inc(s_bc, 1)

            def replicate(n, g, par):
                pe.wait_ge(s_bu, G * n + g + 1 - DUS + BU0)
                pe.matmul(p_du[g % DUS][:], pick[:, g % (Q // DL), :], stacked[:, par, g * DL // Q, 1, :],
                          start=True, stop=True)
                pe.wait_ge(s_da, G * n + g - 1 + DA0)
                pe.matmul(p_da[g % 2][:], pick[:, g % (Q // DL), :], stacked[:, par, g * DL // Q, 0, :],
                          start=True, stop=True).then_inc(s_rep, 1)

            def y_mm(n, g, par):
                pe.wait_ge(s_hc, G * n + g + 1 + HC0)
                if g == 0:
                    pe.wait_ge(s_y, n - 1 + Y0)
                pe.matmul(p_y[par][:], y_pick[:, g, :], hc[:, g % HCS, :],
                          start=(g == 0), stop=(g == G - 1)).then_inc(s_ymm, 1)

            def image_start(b):
                m = b * STEPS
                delta_mm(m, b, 0, 0, m)
                bc_mm(m, b, 0, 0, 0, m + 1)
                bc_mm(m, b, 0, 0, 1)
                delta_mm(m + 1, b, 0, 1, m + 1)
                pe.wait_ge(s_xt, b + 1)

            def step(b, n, k, c, par, n1, n2):
                pe.wait_ge(s_stack[par], stack_count(b, k, c, par))
                for g in range(G):
                    replicate(n, g, par)
                    if g >= LAG:
                        y_mm(n, g - LAG, par)
                    elif ahead(k, c, -1):
                        y_mm(n - 1, G + g - LAG, 1 - par)
                    if n2 and g == 0:
                        delta_mm(n + 2, b, *n2, n + 1)
                    if n1 and g == 3:
                        bc_mm(n + 1, b, *n1, 0, n + 3 if n2 else None)
                    if n1 and g == 7:
                        bc_mm(n + 1, b, *n1, 1)

            def image_end(b):
                for g in range(G - LAG, G):
                    y_mm(b * STEPS + (STEPS - 1), g, 1)

            def stack_count(b, k, c, par):
                per = 16 * PARTS * PARTS
                return b * (per * STEPS // 2) + per * (k * CHUNKS // 2 + 1) + (c - par) * (per // 2)

            all_steps(pe, image_start, step, image_end)

        @block.scalar
        def _(act):
            act.preload_act_table_set(LN_EXP)
            act.wait_ge(s_w, 16 * len(weights))
            act.activation(a_neg[:], a_neg[:], ACT.Exp).then_inc(s_a, 1)
            act.wait_ge(s_a, 2)
            act.sem_inc(s_da, DA0)
            act.sem_inc(s_dx, DX0)
            act.sem_inc(s_bccp, BCCP0)

            def abs_dx(m, k):
                act.wait_ge(s_dt, m + 1)
                act.nop(nofuse=True)
                act.wait_ge(s_delta, m + DELTA0)
                act.activation(e_x[:], p_bc[0:C, :], ACT.Abs, bias=cols[:, k:k + 1]).then_inc(s_abs, 1)
                act.activation(dx_pos[:], p_bc[0:C, :], ACT.Relu, bias=cols[:, k:k + 1]).then_inc(s_dx, 1)

            def exp_dx(m):
                act.wait_ge(s_abs, m + 1)
                act.activation(e_x[:], e_x[:], ACT.Exp, scale=-1.0).then_inc(s_exp, 1)

            def factor(m):
                act.wait_ge(s_exp, m + 1)
                act.activation(series[:], e_x[:], ACT.Copy, scale=-0.5, bias=1.0).then_inc(s_factor, 1)

            def log_1e(m):
                act.activation(log_e[:], e_x[:], ACT.Ln, bias=1.0).then_inc(s_sp, 1)

            def bc_copy(m, par, j):
                act.wait_ge(s_bc, 2 * m + j + 1)
                if j == 1:
                    act.wait_ge(s_hc, G * (m - 1) + HC0)
                act.activation((b_rep, c_rep)[j][:, par, :], p_bc[:], ACT.Copy).then_inc(s_bccp, 1)

            def part_hi(m):
                act.wait_ge(s_du, m + 1)
                act.activation(parts[:, 0], dd[:], ACT.Copy).then_inc(s_hi, 1)

            def decay(n, k, g):
                act.wait_ge(s_rep, G * n + g + 1 + REP0)
                act.wait_ge(s_h, G * n + g + 1 - DAS + H0)
                act.activation(da[:, g % DAS, :], p_da[g % 2][:], ACT.Exp,
                               scale=a_neg[:, k * G + g:k * G + g + 1]).then_inc(s_da, 1)

            def image_start(b):
                act.activation(xt[:].rearrange("c (x y) -> c x y", y=H),
                               X[:, bass.ds(b * HW, HW)].rearrange("c (y x) -> c x y", x=W), ACT.Copy).then_inc(s_xt, 1)
                m = b * STEPS
                abs_dx(m, 0)
                for front in (exp_dx, factor, log_1e):
                    front(m)
                bc_copy(m, 0, 0)
                bc_copy(m, 0, 1)
                part_hi(m)
                abs_dx(m + 1, 0)
                for front in (exp_dx, factor, log_1e):
                    front(m + 1)

            def step(b, n, k, c, par, n1, n2):
                for g in range(G):
                    decay(n, k, g)
                    if n2 and g == 1:
                        abs_dx(n + 2, n2[0])
                    if n1 and g == 5:
                        part_hi(n + 1)
                    if n2 and g == 2:
                        exp_dx(n + 2)
                    if n2 and g == 3:
                        factor(n + 2)
                    if n2 and g == 4:
                        log_1e(n + 2)
                    if n1 and g == 5:
                        bc_copy(n + 1, 1 - par, 0)
                    if n1 and g == 9:
                        bc_copy(n + 1, 1 - par, 1)

            all_steps(act, image_start, step, lambda b: None)

        @block.gpsimd
        def _(pool):
            pool.sem_inc(s_hc, HC0)
            pool.sem_inc(s_lo, LO0)

            def delta_u(m, b, k, c):
                pool.wait_ge(s_delta, m + 1 + DELTA0)
                pool.nop(nofuse=True)
                pool.tensor_tensor(dd[:, 1, :], dd[:, 0, :], u_of(k, b, c), ALU.mult).then_inc(s_du, 1)

            def part_lo(m, j):
                pool.wait_ge(s_hi, m + 1)
                part = pool.tensor_tensor(parts[:, 1, j], dd[:, j], parts[:, 0, j], ALU.subtract)
                if j == 1:
                    part.then_inc(s_lo, 1)

            def times_c(n, g, par):
                if g == 0:
                    pool.wait_ge(s_bccp, 2 * n + 2 + BCCP0)
                pool.wait_ge(s_h, G * n + g + 1 + H0)
                pool.wait_ge(s_ymm, G * n + g + 1 - HCS + YMM0)
                pool.tensor_tensor(hc[:, g % HCS, :], h[:, g, :], c_rep[:, par, :], ALU.mult).then_inc(s_hc, 1)

            def image_start(b):
                m = b * STEPS
                pool.wait_ge(s_xt, b + 1)
                delta_u(m, b, 0, 0)
                part_lo(m, 0)
                part_lo(m, 1)

            def step(b, n, k, c, par, n1, n2):
                for g in range(G):
                    if n1 and g == 0:
                        delta_u(n + 1, b, *n1)
                    times_c(n, g, par)
                    if n1 and g in (2, 4):
                        part_lo(n + 1, g // 2 - 1)

            all_steps(pool, image_start, step, lambda b: None)

        @block.vector
        def _(dve):
            dve.wait_ge(s_setup, K)
            dve.tensor_copy(w_dt[:].rearrange("c k d -> c (k d)"), p_bc[0:C, 0:K * C]).then_inc(s_setup_cp, 1)
            dve.wait_ge(s_w, 16 * len(weights))
            dve.tensor_copy(pick[:], pick_f[:]).then_inc(s_setup_cp, 1)
            dve.tensor_reduce(d_sum[:], cols[:, K:2 * K], AX_X, ALU.add).then_inc(s_setup_cp, 1)
            dve.wait_ge(s_a, 1)
            dve.tensor_scalar(a_neg[:], a_neg[:], -1.0, None, ALU.mult).then_inc(s_a, 1)
            dve.wait_ge(s_setup_cp, 3)
            for s, credit in ((s_delta, DELTA0), (s_bu, BU0), (s_h, H0), (s_y, Y0)):
                dve.sem_inc(s, credit)

            def series_and_mask(m):
                dve.wait_ge(s_factor, m + 1)
                dve.tensor_tensor(series[:], series[:], e_x[:], ALU.mult).then_inc(s_series, 1)
                dve.tensor_scalar(small[:], e_x[:], SMALL_E, None, ALU.is_lt).then_inc(s_series, 1)

            def take_small(m):
                dve.wait_ge(s_sp, m + 1)
                dve.nop(nofuse=True)
                dve.wait_ge(s_series, 2 * m + 2)
                dve.nop(nofuse=True)
                dve.copy_predicated(log_e[:], small[:], series[:]).then_inc(s_logp, 1)

            def delta(m):
                dve.wait_ge(s_logp, m + 1)
                dve.wait_ge(s_lo, m + LO0)
                dve.tensor_tensor(dd[:, 0, :], dx_pos[:], log_e[:], ALU.add).then_inc(s_delta, 1)

            def times_b(n, g, par):
                if g == 0:
                    dve.wait_ge(s_bccp, 2 * n + 1 + BCCP0)
                dve.wait_ge(s_rep, G * n + g + 1 + REP0)
                dve.wait_ge(s_h, G * n + g + 1 - DAS + H0)
                dve.tensor_tensor(bu[:, g % DAS, :], p_du[g % DUS][:], b_rep[:, par, :], ALU.mult).then_inc(s_bu, 1)

            def scan(n, k, c, g, par):
                backward = k >= 2
                way = slice(None, None, -1) if backward else slice(None)
                first = 0 if backward else N - 1
                dve.wait_ge(s_da, G * n + g + 1 + DA0)
                dve.wait_ge(s_hc, G * (n - 1) + g + 1 + HC0)
                dve.wait_ge(s_bu, G * n + g + 1 + BU0)
                state = 0.0 if isinstance(c, int) and c == 0 else h[:, g, first:first + 1]
                dve.tensor_tensor_scan(h[:, g, way], da[:, g % DAS, way], bu[:, g % DAS, way],
                                       state, ALU.mult, ALU.add).then_inc(s_h, 1)

            def add_y(n, k, c, par):
                at = chunk_of(k, c)
                dve.wait_ge(s_ymm, G * n + G + YMM0)
                dve.nop(nofuse=True)
                if k == 0:
                    dve.tensor_copy(y_sum[:, bass.ds(at * N, N)], p_y[par][:]).then_inc(s_y, 1)
                elif k == 2:
                    piece = y_sum[:, bass.ds(at * N, N)]
                    dve.tensor_tensor(piece, piece, p_y[par][:], ALU.add).then_inc(s_y, 1)
                else:
                    piece = y_sum[:].rearrange("c (y x) -> c x y", x=W)[:, bass.ds(at * COLS, COLS), :]
                    dve.tensor_tensor(piece, piece, p_y[par][:].rearrange("c (x y) -> c x y", y=H), ALU.add).then_inc(s_y, 1)

            def image_start(b):
                m = b * STEPS
                series_and_mask(m)
                take_small(m)
                delta(m)
                series_and_mask(m + 1)
                take_small(m + 1)
                delta(m + 1)
                times_b(m, 0, 0)

            def step(b, n, k, c, par, n1, n2):
                for g in range(G):
                    if g < G - 1:
                        times_b(n, g + 1, par)
                    elif n1:
                        times_b(n + 1, 0, 1 - par)
                    scan(n, k, c, g, par)
                    if n2 and g == 5:
                        series_and_mask(n + 2)
                    if g == 9 and ahead(k, c, -1):
                        add_y(n - 1, *ahead(k, c, -1), 1 - par)
                    if n2 and g == 7:
                        take_small(n + 2)
                    if n2 and g == 8:
                        delta(n + 2)

            def image_end(b):
                add_y(b * STEPS + (STEPS - 1), K - 1, CHUNKS - 1, 1)
                dve.wait_ge(s_y, b * STEPS + STEPS + Y0)
                dve.nop(nofuse=True)
                image = X[:, bass.ds(b * HW, HW)]
                dve.scalar_tensor_tensor(image, image, d_sum[:], y_sum[:], ALU.mult, ALU.add)

            all_steps(dve, image_start, step, image_end)


def channel_norm_out(nc, w, X, out):
    DEPTH = 4
    ST = 2 * N
    with ExitStack() as ctx:
        sb = lambda name, shape, dt=F32: ctx.enter_context(nc.sbuf_tensor(name, shape, dt))
        ps = lambda name, shape: ctx.enter_context(nc.psum_tensor(name, shape, F32))
        sem = lambda name: ctx.enter_context(nc.semaphore(name))
        center = sb("l3n_center", [C, C])
        mean_w = sb("l3n_mean_w", [C, C])
        cols = sb("l3n_cols", [C, 2])
        eps = sb("l3n_eps", [C, 2])
        xsq = sb("l3n_xsq", [C, DEPTH, N])
        rstd = sb("l3n_rstd", [C, DEPTH, N])
        xhat = sb("l3n_xhat", [C, 2, N])
        result = sb("l3n_result", [C, 2, ST])
        p_xc = [ps(f"l3n_xc{i}", [C, N]) for i in range(DEPTH)]
        p_var = [ps(f"l3n_var{i}", [C, N]) for i in range(DEPTH)]
        s_w, s_const, s_xc, s_xsq, s_var, s_lnv, s_rstd, s_xhat, s_res = (sem("l3n_" + n) for n in (
            "weights", "constants", "xc", "xsq", "var", "lnvar", "rstd", "xhat", "result"))
        s_store = [sem(f"l3n_stored{i}") for i in range(2)]
        XHAT0, STORE0 = DEPTH, 16
        block = ctx.enter_context(nc.Block())

        def all_tiles(eng, step):
            with eng.Fori(0, TILES // DEPTH - 1) as i:
                for q in range(DEPTH):
                    step(DEPTH * i + q, q, DEPTH)
            for q in range(DEPTH):
                step(TILES - DEPTH + q, q, DEPTH - 1 - q)

        @block.sync
        def _(sp):
            for dst, src in ((center, "center"), (mean_w, "mean_w"), (cols, "cols_out")):
                sp.dma_start(dst[:], w[src]).then_inc(s_w, 16)
            with sp.Fori(0, B) as b:
                with sp.Fori(0, HW // ST // 2) as i:
                    for par in range(2):
                        sp.wait_ge(s_res, b * (HW // N) + 4 * i + 2 * par + 2)
                        sp.nop(nofuse=True)
                        sp.dma_start(out[bass.ds(b, 1), :, bass.ds(i * (2 * ST) + par * ST, ST)].rearrange("b c t -> (b c) t"),
                                     result[:, par, :]).then_inc(s_store[par], 16)
            for par in range(2):
                sp.wait_ge(s_store[par], 16 * (T // ST // 2) + STORE0)

        @block.tensor
        def _(pe):
            def center_tile(m, q):
                pe.wait_ge(s_xhat, m + 1 - DEPTH + XHAT0)
                pe.nop(nofuse=True)
                pe.matmul(p_xc[q][:], center[:], X[:, bass.ds(m * N, N)], start=True, stop=True).then_inc(s_xc, 1)

            def var_tile(m, q):
                pe.wait_ge(s_xsq, m + 1)
                pe.matmul(p_var[q][:], mean_w[:], xsq[:, q, :], start=True, stop=True).then_inc(s_var, 1)

            def step(t, q, ahead):
                if ahead >= 3:
                    center_tile(t + 3, (q + 3) % DEPTH)
                if ahead >= 1:
                    var_tile(t + 1, (q + 1) % DEPTH)

            pe.wait_ge(s_w, 16 * 3)
            for m in range(3):
                center_tile(m, m)
            var_tile(0, 0)
            all_tiles(pe, step)

        @block.scalar
        def _(act):
            def square_tile(m, q):
                act.wait_ge(s_xc, m + 1)
                act.activation(xsq[:, q, :], p_xc[q][:], ACT.Square).then_inc(s_xsq, 1)

            def step(t, q, ahead):
                if ahead >= 2:
                    square_tile(t + 2, (q + 2) % DEPTH)
                act.wait_ge(s_var, t + 1)
                act.activation(rstd[:, q, :], p_var[q][:], ACT.Ln, bias=eps[:, 0:1], scale=WIDE_VAR_SCALE).then_inc(s_lnv, 1)
                act.wait_ge(s_lnv, t + 1)
                act.activation(rstd[:, q, :], rstd[:, q, :], ACT.Exp, bias=eps[:, 1:2], scale=-0.5).then_inc(s_rstd, 1)

            act.preload_act_table_set(LN_EXP)
            act.wait_ge(s_const, 1)
            square_tile(0, 0)
            square_tile(1, 1)
            all_tiles(act, step)

        @block.vector
        def _(dve):
            def step(t, q, ahead):
                dve.wait_ge(s_rstd, t + 1)
                dve.tensor_tensor(xhat[:, q % 2, :], p_xc[q][:], rstd[:, q, :], ALU.mult).then_inc(s_xhat, 1)
                dve.wait_ge(s_xhat, t + 1 + XHAT0)
                if q % 2 == 0:
                    dve.wait_ge(s_store[q // 2], 4 * (t - q) + STORE0)
                dve.tensor_scalar(result[:, q // 2, q % 2 * N:(q % 2 + 1) * N], xhat[:, q % 2, :],
                                  cols[:, 0:1], cols[:, 1:2], ALU.mult, ALU.add).then_inc(s_res, 1)

            dve.sem_inc(s_xhat, XHAT0)
            for s in s_store:
                dve.sem_inc(s, STORE0)
            dve.memset(eps[:, 1:2], 0.5 * float(np.log(WIDE_VAR_SCALE)))
            dve.memset(eps[:, 0:1], EPS * WIDE_VAR_SCALE).then_inc(s_const, 1)
            dve.wait_ge(s_w, 16 * 3)
            all_tiles(dve, step)


def selective_scan_layout(w):
    g = {n[len("L3_conv_"):]: a for n, a in w.items() if n.startswith("L3_conv_")}
    K, S, R, DL, Q = 4, 16, 6, 8, 48
    G = C // DL
    xp = g["x_proj_weight"]
    bc = xp[:, R:].reshape(K, 2, S, 1, C)
    pick = np.zeros((C // Q, Q, Q // DL, S, DL), np.float32)
    for j in range(Q // DL):
        for dl in range(DL):
            pick[:, j * DL + dl, j, :, dl] = 1
    y_pick = np.zeros((S, DL, G, C), np.float32)
    for grp in range(G):
        for dl in range(DL):
            y_pick[:, dl, grp, grp * DL + dl] = 1
    return {
        "xp_dt": xp[:, :R].transpose(1, 0, 2),
        "dt_w_T": g["dt_projs_weight"].transpose(2, 0, 1),
        "w_rep": np.broadcast_to(bc, (K, 2, S, DL, C)).reshape(K, 2, S * DL, C).transpose(3, 0, 1, 2),
        "pick": pick.reshape(C, Q // DL, S * DL),
        "y_pick": y_pick.reshape(S * DL, G, C),
        "a_logs": g["A_logs"].reshape(K, G, DL, S).transpose(3, 2, 0, 1).reshape(S * DL, K * G),
        "cols": np.concatenate([g["dt_projs_bias"].T, g["Ds"].reshape(K, C).T], 1),
        "center": np.eye(C, dtype=np.float32) - np.float32(1 / C),
        "mean_w": np.full((C, C), 1 / C, np.float32),
        "cols_out": np.stack([g["ln_g"].reshape(C), g["ln_b"].reshape(C)], 1),
    }


LAYOUTS = {"L0": gated_ssm_layout, "L1": sedenion_layout, "L2": local_attention_layout, "L3": selective_scan_layout}


def build(nc, x, w, out):
    qkv_d = nc.dram_tensor("qkv_scratch", (5 * C, B, HP * WP), F32, kind="Internal").ap()
    o_d = nc.dram_tensor("o_scratch", (C, T), F32, kind="Internal").ap()
    x_d = nc.dram_tensor("x_scratch", (C, T), F32, kind="Internal").ap()
    with ExitStack() as ctx:
        X = ctx.enter_context(nc.sbuf_tensor("x_front", [C, T], F32))
        gated_ssm_block(nc, x, w["L0"], X)
        sedenion_block(nc, w["L1"], X)
        attention_qkv(nc, w["L2"], X, qkv_d, x_d)
    attention_heads(nc, w["L2"], qkv_d, o_d)
    with ExitStack() as ctx:
        X = ctx.enter_context(nc.sbuf_tensor("x_back", [C, T], F32))
        attention_out(nc, w["L2"], X, o_d, x_d)
        selective_scan(nc, w["L3"], X)
        channel_norm_out(nc, w["L3"], X, out)


def kernel(**inputs):
    import concourse.bacc as _bacc
    from concourse.bass_utils import run_bass_kernel_spmd as _run

    inputs = {name: np.asarray(a) for name, a in inputs.items()}
    nc = _bacc.Bacc("TRN2", target_bir_lowering=False, num_devices=1)
    arrays = {}

    def given(name, a):
        arrays[name] = np.ascontiguousarray(a)
        return nc.dram_tensor(name, a.shape, mybir.dt.from_np(a.dtype), kind="ExternalInput").ap()

    x = given("x", inputs["x"].reshape(B, C, HW))
    weights = {block: {n: given(f"{block}_{n}", a) for n, a in layout(inputs).items()}
               for block, layout in LAYOUTS.items()}
    out = nc.dram_tensor("out", (B, C, HW), F32, kind="ExternalOutput").ap()
    build(nc, x, weights, out)
    r = _run(nc, [arrays], core_ids=[0])
    return r.results[0]["out"].reshape(B, C, H, W)
```
